# Optimizing a Trainium2 kernel written in Bass

```python
import numpy as np
import jax
import jax.numpy as jnp

def _softmax(x, axis=-1):
    return jax.nn.softmax(x, axis=axis)

def _gelu(x):
    return jax.nn.gelu(x, approximate=True)

def _silu(x):
    return jax.nn.silu(x)

def _sigmoid(x):
    return jax.nn.sigmoid(x)

def _layernorm(x, axis=-1, eps=1e-05):
    m = jnp.mean(x, axis=axis, keepdims=True)
    v = jnp.var(x, axis=axis, keepdims=True)
    return (x - m) / jnp.sqrt(v + eps)

def _scatter_add(tgt, idx, src, axis=0):
    return tgt.at[idx].add(src)

def _segment_sum(src, seg, n):
    return jax.ops.segment_sum(src, seg, n)
kernel_name = 'mk_xattn_ffn_d1_seqx_r4_7ac368'

def setup_inputs(seed: int=0):
    np.random.seed(seed)
    _w = jnp.asarray

    def _rec_inputs():
        import jax
        import jax.numpy as jnp
        _rk = jax.random.key(seed)
        x = -0.0002928 + 1 * jax.random.normal(jax.random.fold_in(_rk, 1), (16, 256, 256), jnp.float32)
        _lenS = 256 - jax.random.randint(jax.random.fold_in(_rk, 7), (16,), 0, max(1, 256 // 4) + 1, jnp.int32)
        _lenS2 = 256 - jax.random.randint(jax.random.fold_in(_rk, 8), (16,), 0, max(1, 256 // 4) + 1, jnp.int32)
        _ctx_1024P = jax.random.normal(jax.random.fold_in(_rk, 11), (16, 16, 256), jnp.float32)
        _ctx_1024c = jax.random.dirichlet(jax.random.fold_in(_rk, 511), 0.3 * jnp.ones((16,), jnp.float32), (16, 256))
        _ctx_1024t = jnp.einsum('bsk,bkd->bsd', _ctx_1024c, _ctx_1024P)
        _ctx_1024t = _ctx_1024t * jax.lax.rsqrt(jnp.mean(jnp.square(_ctx_1024t)) + 1e-12) * 0.953939
        ctx_1024 = -1.39393e-06 + 0.999914 * (_ctx_1024t + 0.3 * jax.random.normal(jax.random.fold_in(_rk, 611), (16, 256, 256), jnp.float32))
        _validS = jnp.arange(256)[None, :] < _lenS[:, None]
        _validS2 = jnp.arange(256)[None, :] < _lenS2[:, None]
        _causal = jnp.tril(jnp.ones((256, 256), dtype=bool))
        mask_1x1xSxS2_ik0 = jnp.where(jnp.broadcast_to(_validS2[0:1, None, None, :], (1, 1, 256, 256)), 0, 1).astype(jnp.int32)
        return (x, ctx_1024, mask_1x1xSxS2_ik0)
    x, ctx_1024, mask_1x1xSxS2_ik0 = _rec_inputs()

    def _L0_xattn_setup():
        import jax, jax.numpy as jnp
        import numpy as np
        B, T, D, H = (2, 512, 256, 16)
        DK = D // H
        key = jax.random.key(seed)
        ks = jax.random.split(key, 12)
        s = 1.0 / np.sqrt(D)
        inp = {'Q': jax.random.normal(ks[0], (B, T, D), jnp.float32), 'K': jax.random.normal(ks[1], (B, T, D), jnp.float32), 'V': jax.random.normal(ks[2], (B, T, D), jnp.float32), 'mask': jnp.tril(jnp.ones((T, T), jnp.int32))[None, None], 'Wq_w': jax.random.normal(ks[3], (D, D), jnp.float32) * s, 'Wq_b': jax.random.normal(ks[4], (D,), jnp.float32) * s, 'Wk_w': jax.random.normal(ks[5], (D, D), jnp.float32) * s, 'Wk_b': jax.random.normal(ks[6], (D,), jnp.float32) * s, 'Wv_w': jax.random.normal(ks[7], (D, D), jnp.float32) * s, 'Wv_b': jax.random.normal(ks[8], (D,), jnp.float32) * s, 'Wo_w': jax.random.normal(ks[9], (D, D), jnp.float32) * s, 'Wo_b': jax.random.normal(ks[10], (D,), jnp.float32) * s}
        return inp
    _L0_xattn_all = _L0_xattn_setup()
    _L0_xattn_in = {k: v for k, v in _L0_xattn_all.items() if k in ('Wq_w', 'Wq_b', 'Wk_w', 'Wk_b', 'Wv_w', 'Wv_b', 'Wo_w', 'Wo_b')}
    del _L0_xattn_all

    def _L0_ffn_setup():
        import jax, jax.numpy as jnp
        import numpy as np
        HIDDEN_SIZE = 256
        NUM_EXPERTS = 8
        MOE_INTERMEDIATE_SIZE = 352
        NUM_EXPERTS_PER_TOK = 2
        SHARED_EXPERT_INTERMEDIATE_SIZE = 704
        B, T = (2, 256)
        W_SCALE = 0.02
        key = jax.random.key(seed)
        ks = jax.random.split(key, 8)
        H, E, I, SI = (HIDDEN_SIZE, NUM_EXPERTS, MOE_INTERMEDIATE_SIZE, SHARED_EXPERT_INTERMEDIATE_SIZE)
        return {'x': jax.random.normal(ks[0], (B, T, H), jnp.float32), 'gate_w': jax.random.normal(ks[1], (E, H), jnp.float32) * W_SCALE, 'experts_gate_up': jax.random.normal(ks[2], (E, 2 * I, H), jnp.float32) * W_SCALE, 'experts_down': jax.random.normal(ks[3], (E, H, I), jnp.float32) * W_SCALE, 'shared_gate_w': jax.random.normal(ks[4], (SI, H), jnp.float32) * W_SCALE, 'shared_up_w': jax.random.normal(ks[5], (SI, H), jnp.float32) * W_SCALE, 'shared_down_w': jax.random.normal(ks[6], (H, SI), jnp.float32) * W_SCALE, 'shared_expert_gate_w': jax.random.normal(ks[7], (1, H), jnp.float32) * W_SCALE}
    _L0_ffn_all = _L0_ffn_setup()
    _L0_ffn_in = {k: v for k, v in _L0_ffn_all.items() if k in ('gate_w', 'experts_gate_up', 'experts_down', 'shared_gate_w', 'shared_up_w', 'shared_down_w', 'shared_expert_gate_w')}
    del _L0_ffn_all
    return {'x': x, 'ctx_1024': ctx_1024, 'mask_1x1xSxS2_ik0': mask_1x1xSxS2_ik0, 'L0_xattn_Wq_w': _L0_xattn_in['Wq_w'], 'L0_xattn_Wq_b': _L0_xattn_in['Wq_b'], 'L0_xattn_Wk_w': _L0_xattn_in['Wk_w'], 'L0_xattn_Wk_b': _L0_xattn_in['Wk_b'], 'L0_xattn_Wv_w': _L0_xattn_in['Wv_w'], 'L0_xattn_Wv_b': _L0_xattn_in['Wv_b'], 'L0_xattn_Wo_w': _L0_xattn_in['Wo_w'], 'L0_xattn_Wo_b': _L0_xattn_in['Wo_b'], 'L0_ffn_gate_w': _L0_ffn_in['gate_w'], 'L0_ffn_experts_gate_up': _L0_ffn_in['experts_gate_up'], 'L0_ffn_experts_down': _L0_ffn_in['experts_down'], 'L0_ffn_shared_gate_w': _L0_ffn_in['shared_gate_w'], 'L0_ffn_shared_up_w': _L0_ffn_in['shared_up_w'], 'L0_ffn_shared_down_w': _L0_ffn_in['shared_down_w'], 'L0_ffn_shared_expert_gate_w': _L0_ffn_in['shared_expert_gate_w']}

def reference(x, ctx_1024, mask_1x1xSxS2_ik0, L0_xattn_Wq_w, L0_xattn_Wq_b, L0_xattn_Wk_w, L0_xattn_Wk_b, L0_xattn_Wv_w, L0_xattn_Wv_b, L0_xattn_Wo_w, L0_xattn_Wo_b, L0_ffn_gate_w, L0_ffn_experts_gate_up, L0_ffn_experts_down, L0_ffn_shared_gate_w, L0_ffn_shared_up_w, L0_ffn_shared_down_w, L0_ffn_shared_expert_gate_w):
    import jax
    import jax.numpy as jnp

    def _L0_xattn_ref(Q, K, V, mask, Wq_w, Wq_b, Wk_w, Wk_b, Wv_w, Wv_b, Wo_w, Wo_b):
        import jax, jax.numpy as jnp
        import numpy as np
        B, T, D, H = (2, 512, 256, 16)
        DK = D // H
        b, tq, c = Q.shape
        tk = K.shape[1]
        q = (Q @ Wq_w + Wq_b).reshape(b, tq, H, DK).transpose(0, 2, 1, 3)
        k = (K @ Wk_w + Wk_b).reshape(b, tk, H, DK).transpose(0, 2, 1, 3)
        v = (V @ Wv_w + Wv_b).reshape(b, tk, H, DK).transpose(0, 2, 1, 3)
        scores = jnp.einsum('bhqd,bhkd->bhqk', q, k) / jnp.sqrt(jnp.float32(DK))
        scores = jnp.where(mask == 0, jnp.float32(-1000000000.0), scores)
        attn = jax.nn.softmax(scores, axis=-1)
        out = jnp.einsum('bhqk,bhkd->bhqd', attn, v)
        out = out.transpose(0, 2, 1, 3).reshape(b, tq, c)
        return out @ Wo_w + Wo_b

    def _L0_ffn_ref(x, gate_w, experts_gate_up, experts_down, shared_gate_w, shared_up_w, shared_down_w, shared_expert_gate_w):
        import jax, jax.numpy as jnp
        import numpy as np
        HIDDEN_SIZE = 256
        NUM_EXPERTS = 8
        MOE_INTERMEDIATE_SIZE = 352
        NUM_EXPERTS_PER_TOK = 2
        SHARED_EXPERT_INTERMEDIATE_SIZE = 704
        B, T = (2, 256)
        W_SCALE = 0.02
        Bx, Tx, H = x.shape
        E = gate_w.shape[0]
        I = experts_down.shape[2]
        x_flat = x.reshape(Bx * Tx, H)
        logits = x_flat @ gate_w.T
        scores = jax.nn.softmax(logits, axis=-1)
        _, topk_ids = jax.lax.top_k(scores, NUM_EXPERTS_PER_TOK)
        in_topk = jax.nn.one_hot(topk_ids, E, dtype=x.dtype).sum(axis=1)
        w = scores * in_topk
        gu = jnp.einsum('nh,eih->nei', x_flat, experts_gate_up)
        g, u = (gu[..., :I], gu[..., I:])
        h = jax.nn.silu(g) * u
        expert_out = jnp.einsum('nei,ehi->neh', h, experts_down)
        out = jnp.einsum('neh,ne->nh', expert_out, w)
        shared = jax.nn.silu(x_flat @ shared_gate_w.T) * (x_flat @ shared_up_w.T) @ shared_down_w.T
        shared_weight = jax.nn.sigmoid(x_flat @ shared_expert_gate_w.T)
        out = out + shared_weight * shared
        return out.reshape(Bx, Tx, H)
    x = x + _L0_xattn_ref(_layernorm(x, axis=-1), ctx_1024, ctx_1024, mask_1x1xSxS2_ik0, L0_xattn_Wq_w, L0_xattn_Wq_b, L0_xattn_Wk_w, L0_xattn_Wk_b, L0_xattn_Wv_w, L0_xattn_Wv_b, L0_xattn_Wo_w, L0_xattn_Wo_b)
    x = x + _L0_ffn_ref(_layernorm(x, axis=-1), L0_ffn_gate_w, L0_ffn_experts_gate_up, L0_ffn_experts_down, L0_ffn_shared_gate_w, L0_ffn_shared_up_w, L0_ffn_shared_down_w, L0_ffn_shared_expert_gate_w)
    return x

_drawn_inputs = setup_inputs


def setup_inputs(seed=0):
    import zlib

    import numpy as np

    out = dict(_drawn_inputs(seed))
    spreads = {}
    factors = {'L0_xattn_Wq_b': 4.012,
     'L0_xattn_Wk_b': 8.0,
     'L0_ffn_gate_w': 8.0,
     'L0_ffn_experts_gate_up': 8.0,
     'L0_ffn_experts_down': 8.0,
     'L0_ffn_shared_gate_w': 4.693,
     'L0_ffn_shared_up_w': 4.608,
     'L0_ffn_shared_down_w': 4.634,
     'L0_ffn_shared_expert_gate_w': 8.0}
    for name, (base, spread) in spreads.items():
        noise = np.random.default_rng([zlib.crc32(name.encode()), seed]).standard_normal(out[name].shape)
        drawn = base * np.exp(spread * noise) if base else spread * noise
        out[name] = jnp.asarray(drawn.astype(out[name].dtype))
    for name, factor in factors.items():
        out[name] = (out[name] * factor).astype(out[name].dtype)
    return out
```

```python
import concourse.bass as bass
from concourse import mybir
from contextlib import ExitStack

FP32 = mybir.dt.float32
FP16 = mybir.dt.float16
BF16 = mybir.dt.bfloat16
INT32 = mybir.dt.int32
ALU = mybir.AluOpType
ACT = mybir.ActivationFunctionType
AX = mybir.AxisListType

P = 128
D = 256
NB = 16
SEQ = 256
TOK = NB * SEQ
NT = TOK // P
TT = SEQ // P
DC = D // P
H = 16
DK = D // H
NP = H // 2
HG = 4
NE = 8
INTER = 352
NX = NE + 2
IC = [128, 128, 96]
FW = 2 * DC * INTER + len(IC) * D
UP0 = DC * INTER
DOWN0 = 2 * DC * INTER
ROWS = 48
EPS = 1e-5
MASKED = 2.0 ** 30
SCALE = DK ** -0.5
BLK = 512
NBLK = TOK // BLK
BT = BLK // P

TERMS = ((0, 0), (1, 0), (0, 1))


def block_kernel(nc, x, ctx, mask, w_in, bias_in, w_o, ffn_in, gate_in, ident_in, out, qk_scratch, m_scratch):
    with ExitStack() as life:
        sb = lambda stack, n, s, t: stack.enter_context(nc.sbuf_tensor(n, s, t))
        sem = lambda n: life.enter_context(nc.semaphore(n))

        xr = sb(life, "xr", [P, NT, D], FP32)
        fwh = sb(life, "fwh", [P, NE, FW], FP16)
        fwl = sb(life, "fwl", [P, NE, FW], FP16)
        ident = sb(life, "ident", [P, P], FP32)
        neghalf = sb(life, "neghalf", [P, BT], FP32)
        attention(nc, sb, sem, life, xr, fwh, fwl, ident, neghalf,
                  x, ctx, mask, w_in, bias_in, w_o, ffn_in, ident_in, qk_scratch, m_scratch)
        ffn(nc, sb, sem, life, xr, fwh, fwl, ident, neghalf, ffn_in, gate_in, out)


def attention(nc, sb, sem, life, xr, fwh, fwl, ident, neghalf,
              x, ctx, mask, w_in, bias_in, w_o, ffn_in, ident_in, qk_scratch, m_scratch):
    with ExitStack() as here:
        t = lambda n, s, d: sb(here, n, s, d)
        pt = lambda n, s: here.enter_context(nc.psum_tensor(n, s, FP32))
        WA = 3 * DC * D + HG * D
        aw32 = t("aw32", [P, 2176], FP32)
        awh = t("awh", [P, WA], FP16)
        awl = t("awl", [P, WA], FP16)
        bhl = t("bhl", [33, 4 * D], FP16)
        ones33 = t("ones33", [33, SEQ], FP16)
        any33 = t("any33", [33, SEQ], FP16)
        identb = t("identb", [P, P], BF16)
        anyq = t("anyq", [P, TT], FP32)
        mb_q = t("mb_q", [P, TT, 2, SEQ], BF16)
        mb_k = t("mb_k", [P, TT, 2, SEQ], BF16)
        c32 = [t(f"c32_{i}", [P, TT, D], FP32) for i in range(2)]
        xn = t("xn", [P, TT, D], FP32)
        st6 = t("st6", [P, TT, 6], FP32)
        mv = [t(f"mv{i}", [P, TT, 2], FP32) for i in range(2)]
        ve = [t(f"ve{i}", [P, TT], FP32) for i in range(2)]
        rstd = [t(f"rstd{i}", [P, TT], FP32) for i in range(2)]
        rsa = t("rsa", [P, TT], FP32)
        xT = [t("xTh", [P, DC * SEQ], FP16), t("xTl", [P, DC * SEQ], FP16)]
        cT = [t("cTh", [P, DC * SEQ], FP16), t("cTl", [P, DC * SEQ], FP16)]
        qhl = t("qhl", [P, 2, 2, SEQ], FP16)
        khl = t("khl", [P, 2, 2, SEQ], FP16)
        qs = [t(f"qs{i}", [P, NP, SEQ], FP16) for i in range(3)]
        ks = [t(f"ks{i}", [P, NP, SEQ], FP16) for i in range(3)]
        vx = [t(f"vx{i}", [P, TT, H, 32], FP32) for i in range(3)]
        mx = [t(f"mx{i}", [P, TT, H], FP32) for i in range(2)]
        nm = t("nm", [H, SEQ], FP16)
        pe_ = [t(f"p{i}", [P, 4, SEQ], FP32) for i in range(4)]
        mi = pe_[0][:, 0:TT, :].bitcast(INT32)
        nz = pe_[1][:, 0:TT, :]
        b32 = pe_[2][0:33, :, :].rearrange("p a b -> p (a b)")
        bh2 = pe_[3][0:33, 0:2, :].rearrange("p a b -> p (a b)").bitcast(FP16)
        r1 = t("r1", [P, 2 * SEQ], FP32)
        r2 = t("r2", [P, 2 * SEQ], FP32)
        on = [t(f"on{i}", [P, 2 * SEQ], FP32) for i in range(2)]
        onh = t("onh", [P, HG, SEQ], FP16)
        onl = t("onl", [P, HG, SEQ], FP16)

        ps_s = pt("ps_s", [P, 4 * SEQ])
        ps_t = pt("ps_t", [P, 4 * SEQ])
        ps_o = pt("ps_o", [P, HG * SEQ])
        ps_m = [pt(f"ps_m{i}", [P, 2 * SEQ]) for i in range(2)]

        WQ, WK, WV, WO = 0, DC * D, 2 * DC * D, 3 * DC * D

        s_x = [sem(f"s_x{i}") for i in range(8)]
        s_c = [sem(f"s_c{i}") for i in range(2)]
        s_aw = sem("s_aw"); s_bias = sem("s_bias"); s_mi = sem("s_mi"); s_id = sem("s_id")
        s_fw = sem("s_fw"); s_fwd = sem("s_fwd"); s_wo = sem("s_wo")
        s_awh = sem("s_awh"); s_awl = sem("s_awl")
        s_const = sem("s_const")
        s_bh = sem("s_bh"); s_bl = sem("s_bl")
        s_idb = sem("s_idb")
        s_nz = sem("s_nz"); s_mbf = sem("s_mbf"); s_mbq = sem("s_mbq"); s_mbT = sem("s_mbT"); s_mbk = sem("s_mbk")
        s_anyb = sem("s_anyb"); s_any33 = sem("s_any33")
        s_stat = sem("s_stat"); s_pow = sem("s_pow"); s_xn = sem("s_xn")
        s_xt = sem("s_xt"); s_ct = sem("s_ct")
        s_xh = sem("s_xh"); s_xl = sem("s_xl"); s_ch = sem("s_ch"); s_cl = sem("s_cl")
        s_q = sem("s_q"); s_k = sem("s_k"); s_v = sem("s_v")
        s_qh = sem("s_qh"); s_ql = sem("s_ql"); s_kh = sem("s_kh"); s_kl = sem("s_kl"); s_vx = sem("s_vx")
        s_qw = sem("s_qw"); s_kw = sem("s_kw")
        s_qk = [sem(f"s_qk{i}") for i in range(3)]
        s_s = sem("s_s"); s_mx = sem("s_mx"); s_mt = sem("s_mt"); s_nm = sem("s_nm"); s_mw = sem("s_mw")
        s_mr = [sem(f"s_mr{i}") for i in range(3)]
        s_st = sem("s_st"); s_e = sem("s_e"); s_pv = sem("s_pv")
        s_n = sem("s_n"); s_onh = sem("s_onh"); s_onl = sem("s_onl")
        s_o = sem("s_o"); s_res = sem("s_res")
        s_free = [sem(f"s_free{i}") for i in range(2)]
        s_dch = sem("s_dch"); s_pch = sem("s_pch"); s_ach = sem("s_ach")

        order = ["mask", "any"]
        slots = {0: "mt", 1: "o", 2: "xt", 3: "ct", 4: "q", 5: "k", 6: "v"}
        lag = {"o": 4, "mt": 2, "xt": 0, "ct": 0, "q": 0, "k": 0, "v": 0}
        ITER = NB + 5
        for i in range(ITER):
            for u in range(8):
                kind = slots.get(u)
                if kind and 0 <= i - lag[kind] < NB:
                    order.append((kind, i - lag[kind]))
        use = {k: n for n, k in enumerate(order)}
        bank = lambda k: ps_m[use[k] % 2]

        def wait_bank(eng, k):
            if use[k] // 2:
                eng.wait_ge(s_free[use[k] % 2], use[k] // 2)

        free = lambda k: s_free[use[k] % 2]

        def units(i, u):
            g = 8 * i + u
            found = []
            for late in (8, 20, 21):
                found.append(divmod(g - late, 8) if 0 <= g - late < 8 * NB else None)
            return found

        block = here.enter_context(nc.Block())

        @block.sync
        def _(eng):
            eng.dma_start(ident[:, :], ident_in).then_inc(s_id, 16)
            eng.dma_start(mi[:, :, :], mask.rearrange("(t p) k -> p t k", p=P)).then_inc(s_mi, 16)
            eng.dma_start(aw32[:, 0:3 * DC * D], w_in).then_inc(s_aw, 16)
            xv = x.rearrange("(n p) d -> p n d", p=P)
            cv = ctx.rearrange("(b t p) d -> b p t d", p=P, t=TT)

            def load_c(b):
                if b >= 2:
                    eng.wait_ge(s_ct, b - 1)
                eng.dma_start(c32[b % 2][:, :, :], cv[b, :, :, :]).then_inc(s_c[b % 2], 16)

            eng.dma_start(xr[:, 0:4, :], xv[:, 0:4, :]).then_inc(s_x[0], 16)
            load_c(0)
            eng.dma_start(b32[0:1, :], bias_in).then_inc(s_bias, 16)
            eng.dma_start(b32[32:33, :], bias_in).then_inc(s_bias, 16)
            load_c(1)
            for n in range(1, 8):
                eng.dma_start(xr[:, 4 * n:4 * n + 4, :], xv[:, 4 * n:4 * n + 4, :]).then_inc(s_x[n], 16)
            eng.wait_ge(s_awh, 1)
            eng.wait_ge(s_awl, 1)
            eng.dma_start(aw32[:, 0:HG * D], w_o).then_inc(s_wo, 16)
            for i in range(ITER):
                if 0 < i <= NE:
                    eng.wait_ge(s_awl, 1 + i)
                    eng.dma_start(aw32[:, :], ffn_in[i - 1, :, :]).then_inc(s_fw, 16)
                b = i - 2
                if 0 <= b < NB:
                    eng.wait_ge(s_nm, b + 1)
                    eng.dma_start(m_scratch[b, :, :], nm[:, :]).then_inc(s_mw, 16)
                    eng.wait_ge(s_mw, 16 * (b + 1))
                    mv_ = m_scratch[b, :, :].rearrange("(h p) t -> h p t", h=2)
                    for hh in range(2):
                        eng.dma_start(qs[b % 3][64 * hh + ROWS:64 * hh + ROWS + 1, :, :],
                                      mv_[hh:hh + 1, :, :]).then_inc(s_mr[b % 3], 16)
                if i < NB:
                    if i + 1 < NB and i >= 1:
                        load_c(i + 1)
                    for what, hl, s_lo, s_w in ((0, qhl, s_ql, s_qw), (1, khl, s_kl, s_kw)):
                        eng.wait_ge(s_lo, i + 1)
                        eng.dma_start(qk_scratch[i, what, :, :, :, :].rearrange("l h r t -> r l h t"),
                                      hl[:, :, :, :]).then_inc(s_w, 16)
                    if i >= 3:
                        eng.wait_ge(s_st, 8 * (i - 2))
                    for what, dst, s_w, parts in ((0, qs[i % 3], s_qw, (0, 0, 1)), (1, ks[i % 3], s_kw, (0, 1, 0))):
                        eng.wait_ge(s_w, 16 * (i + 1))
                        for hh in range(2):
                            for n, part in enumerate(parts):
                                row = 64 * hh + 16 * n
                                src = qk_scratch[i, what, part, hh, :, :].rearrange("(p d) t -> d p t", d=DK)
                                eng.dma_start(dst[row:row + DK, :, :], src).then_inc(s_qk[i % 3], 16)

        @block.gpsimd
        def _(eng):
            chain = [0]

            def link(ins):
                chain[0] += 1
                ins.then_inc(s_pch, 1)
                eng.wait_ge(s_pch, chain[0])

            eng.memset(neghalf[:, :], -0.5)
            eng.memset(ones33[:, :], 1.0).then_inc(s_const, 1)
            eng.memset(bhl[:, :], 0.0).then_inc(s_const, 1)
            for i in range(3):
                eng.memset(vx[i][:, :, :, :], 1.0).then_inc(s_const, 1)
                last = eng.memset(ks[i][:, :, :], 1.0)
                last.then_inc(s_const, 1)
            eng.wait_ge(s_const, 8)

            def split(src, hi, lo, loaded, need, s_hi):
                eng.wait_ge(loaded, need)
                eng.tensor_copy(hi, src).then_inc(s_hi, 1)
                return hi, lo

            def power(b):
                eng.wait_ge(s_stat, b + 1)
                if b >= 2:
                    eng.wait_ge(s_xn, b - 1)
                link(eng.tensor_scalar(ve[b % 2][:, :], mv[b % 2][:, :, 1], EPS, None, ALU.add))
                eng.tensor_tensor(rstd[b % 2][:, :], ve[b % 2][:, :], neghalf[:, 0:TT], ALU.pow).then_inc(s_pow, 1)

            power(0)
            eng.wait_ge(s_awh, 1)
            eng.tensor_tensor(awl[:, 0:3 * DC * D], aw32[:, 0:3 * DC * D], awh[:, 0:3 * DC * D],
                              ALU.subtract).then_inc(s_awl, 1)
            power(1)
            eng.wait_ge(s_wo, 16)
            link(eng.tensor_copy(awh[:, WO:WA], aw32[:, 0:HG * D]))
            eng.tensor_tensor(awl[:, WO:WA], aw32[:, 0:HG * D], awh[:, WO:WA], ALU.subtract).then_inc(s_awl, 1)
            for i in range(ITER):
                if 2 <= i + 1 < NB:
                    power(i + 1)
                for half in range(2):
                    b = i - 3 if half == 0 else i - 4
                    if half == 0 and 0 <= i - 4 < NB or half == 1 and 0 <= i - 3 < NB:
                        b, part = (i - 4, 1) if half == 0 else (i - 3, 0)
                        n = 2 * b + part
                        eng.wait_ge(s_n, n + 1)
                        if b >= 1:
                            eng.wait_ge(s_o, b)
                        cols = slice(2 * part, 2 * part + 2)
                        src = on[part][:, :].rearrange("p (g t) -> p g t", g=2)
                        eng.tensor_copy(onh[:, cols, :], src).then_inc(s_onh, 1)
                        eng.wait_ge(s_onh, n + 1)
                        eng.tensor_tensor(onl[:, cols, :], src, onh[:, cols, :], ALU.subtract).then_inc(s_onl, 1)
                    if half == 0 and 0 < i <= NE:
                        e = i - 1
                        eng.wait_ge(s_fw, 16 * i)
                        eng.tensor_copy(fwh[:, e, :], aw32[:, :]).then_inc(s_fwd, 1)
                        eng.wait_ge(s_fwd, i)
                        eng.tensor_tensor(fwl[:, e, :], aw32[:, :], fwh[:, e, :], ALU.subtract).then_inc(s_awl, 1)

        @block.scalar
        def _(eng):
            eng.wait_ge(s_aw, 16)
            eng.activation(awh[:, 0:3 * DC * D], aw32[:, 0:3 * DC * D], ACT.Copy).then_inc(s_awh, 1)
            eng.wait_ge(s_bias, 32)
            eng.wait_ge(s_const, 2)
            eng.activation(bhl[0:1, :], b32[0:1, :], ACT.Copy).then_inc(s_bh, 1)
            eng.activation(bh2[32:33, :], b32[32:33, :], ACT.Copy).then_inc(s_bh, 1)
            eng.wait_ge(s_id, 16)
            eng.activation(identb[:, :], ident[:, :], ACT.Copy).then_inc(s_idb, 1)
            eng.wait_ge(s_mbT, 1)
            for r in range(2):
                last = eng.activation(mb_k[:, :, r, :], bank("mask")[:, :].rearrange("p (t q) -> p t q", t=TT), ACT.Copy)
                last.then_inc(s_mbk, 1)
            eng.wait_ge(s_anyb, 1)
            eng.activation(any33[:, :], bank("any")[0:33, 0:SEQ], ACT.Copy).then_inc(s_any33, 1)
            eng.wait_ge(s_mbk, 2)
            eng.wait_ge(s_any33, 1)
            eng.nop().then_inc(s_free[0], 1)
            eng.nop().then_inc(s_free[1], 1)
            for i in range(ITER):
                for u in range(8):
                    kind = slots.get(u)
                    b = i - lag[kind] if kind else -1
                    if 0 <= b < NB:
                        if kind == "mt":
                            eng.wait_ge(s_mt, b + 1)
                            if b:
                                eng.wait_ge(s_mw, 16 * b)
                            eng.activation(nm[:, :], bank((kind, b))[0:H, 0:SEQ], ACT.Copy, scale=-1.0).then_inc(s_nm, 1)
                            eng.wait_ge(s_nm, b + 1)
                            eng.nop().then_inc(free((kind, b)), 1)
                        elif kind in ("xt", "ct"):
                            s_in, dst, s_out, s_used = (s_xt, xT[0], s_xh, s_q) if kind == "xt" else (s_ct, cT[0], s_ch, s_v)
                            eng.wait_ge(s_in, b + 1)
                            if b:
                                eng.wait_ge(s_used, b)
                            eng.activation(dst[:, :], bank((kind, b))[:, :], ACT.Copy).then_inc(s_out, 1)
                        elif kind in ("q", "k"):
                            s_in, dst, s_out, s_used = (s_q, qhl, s_qh, s_qw) if kind == "q" else (s_k, khl, s_kh, s_kw)
                            eng.wait_ge(s_in, b + 1)
                            if b:
                                eng.wait_ge(s_used, 16 * b)
                            eng.activation(dst[:, 0, :, :], bank((kind, b))[:, :].rearrange("p (h t) -> p h t", h=2),
                                           ACT.Copy).then_inc(s_out, 1)
                        elif kind == "v":
                            eng.wait_ge(s_v, b + 1)
                            if b >= 3:
                                eng.wait_ge(s_pv, 4 * (b - 2))
                            for tt in range(TT):
                                last = eng.activation(vx[b % 3][:, tt, :, 0:DK],
                                                      bank((kind, b))[:, tt * D:(tt + 1) * D].rearrange("p (h d) -> p h d", h=H),
                                                      ACT.Copy)
                                last.then_inc(s_vx, 1)
                            eng.wait_ge(s_vx, 2 * b + 2)
                            eng.nop().then_inc(free((kind, b)), 1)
                    _, st, _ = units(i, u)
                    if st:
                        n = 8 * st[0] + st[1]
                        eng.wait_ge(s_st, n + 1)
                        if n >= 4:
                            eng.wait_ge(s_pv, (n - 4) // 2 + 1)
                        eng.activation(pe_[n % 4][:, :, :], ps_t[:, :].rearrange("p (h q) -> p h q", h=4), ACT.Exp,
                                       scale=SCALE).then_inc(s_e, 1)

        @block.vector
        def _(eng):
            chain = [0]

            def link(ins):
                chain[0] += 1
                ins.then_inc(s_dch, 1)
                eng.wait_ge(s_dch, chain[0])

            def stats(b):
                eng.wait_ge(s_x[b // 2], 16)
                if b >= 2:
                    eng.wait_ge(s_pow, b - 1)
                for tt in range(TT):
                    last = eng.bn_stats(st6[:, tt, :], xr[:, TT * b + tt, :])
                link(last)
                for tt in range(TT):
                    last = eng.bn_aggr(mv[b % 2][:, tt, :], st6[:, tt, :])
                link(last)
                eng.nop().then_inc(s_stat, 1)

            def normalise(b):
                eng.wait_ge(s_pow, b + 1)
                link(eng.tensor_tensor(rsa[:, :], rstd[b % 2][:, :], anyq[:, :], ALU.mult))
                if b:
                    eng.wait_ge(s_xt, b)
                for tt in range(TT):
                    last = eng.tensor_scalar(xn[:, tt, :], xr[:, TT * b + tt, :], mv[b % 2][:, tt, 0:1],
                                             rsa[:, tt:tt + 1], ALU.subtract, ALU.mult)
                last.then_inc(s_xn, 1)
                eng.wait_ge(s_xn, b + 1)

            stats(0)
            stats(1)
            eng.wait_ge(s_mi, 16)
            link(eng.tensor_scalar(nz[:, :, :], mi[:, :, :], 0, None, ALU.not_equal))
            link(eng.tensor_reduce(anyq[:, :], nz[:, :, :], axis=AX.X, op=ALU.max))
            link(eng.tensor_scalar(nz[:, :, :], nz[:, :, :], 1.0, MASKED, ALU.subtract, ALU.mult))
            for tt in range(TT):
                last = eng.tensor_scalar(nz[:, tt, :], nz[:, tt, :], anyq[:, tt:tt + 1], None, ALU.mult)
            last.then_inc(s_mbf, 1)
            eng.wait_ge(s_mbf, 1)
            for r in range(2):
                last = eng.tensor_copy(mb_q[:, :, r, :], nz[:, :, :])
            last.then_inc(s_mbq, 1)
            eng.wait_ge(s_bh, 2)
            eng.tensor_tensor(bhl[32:33, :], b32[32:33, :], bh2[32:33, :], ALU.subtract).then_inc(s_bl, 1)
            for i in range(ITER):
                for u in range(8):
                    kind = slots.get(u)
                    b = i - lag[kind] if kind else -1
                    if u == 0 and i == 0:
                        normalise(0)
                    if u == 7 and i + 1 < NB:
                        normalise(i + 1)
                    if u == 3 and 2 <= i + 2 < NB:
                        stats(i + 2)
                    if 0 <= b < NB:
                        if kind == "o":
                            eng.wait_ge(s_o, b + 1)
                            tiles = xr[:, TT * b:TT * b + TT, :]
                            eng.tensor_tensor(tiles, bank((kind, b))[:, :].rearrange("p (t d) -> p t d", t=TT), tiles,
                                              ALU.add).then_inc(free((kind, b)), 1)
                        elif kind in ("xt", "ct"):
                            s_in, (hi, lo), s_out, s_used = (s_xh, xT, s_xl, s_q) if kind == "xt" else (s_ch, cT, s_cl, s_v)
                            eng.wait_ge(s_in, b + 1)
                            eng.tensor_tensor(lo[:, :], bank((kind, b))[:, :], hi[:, :], ALU.subtract).then_inc(s_out, 1)
                            eng.wait_ge(s_out, b + 1)
                            eng.nop().then_inc(free((kind, b)), 1)
                        elif kind in ("q", "k"):
                            s_in, hl, s_out = (s_qh, qhl, s_ql) if kind == "q" else (s_kh, khl, s_kl)
                            eng.wait_ge(s_in, b + 1)
                            eng.tensor_tensor(hl[:, 1, :, :], bank((kind, b))[:, :].rearrange("p (h t) -> p h t", h=2),
                                              hl[:, 0, :, :], ALU.subtract).then_inc(s_out, 1)
                            eng.wait_ge(s_out, b + 1)
                            eng.nop().then_inc(free((kind, b)), 1)
                    s, _, pv = units(i, u)
                    if s:
                        b, n = s
                        qt, hg = divmod(n, HG)
                        eng.wait_ge(s_s, 8 * b + n + 1)
                        if n == 0 and b >= 2:
                            eng.wait_ge(s_mt, b - 1)
                        eng.tensor_reduce(mx[b % 2][:, qt, :].rearrange("p (h g j) -> p h g j", h=2, g=HG)[:, :, hg, :], ps_s[:, :].rearrange("p (h j k) -> p h j k", h=2, j=2),
                                          axis=AX.X, op=ALU.max).then_inc(s_mx, 1)
                    if pv and pv[1] % 4 == 3:
                        b, part = pv[0], pv[1] // 4
                        n = 2 * b + part
                        eng.wait_ge(s_pv, 2 * n + 2)
                        heads = ps_o[:, 2 * part * SEQ:(2 * part + 2) * SEQ]
                        link(eng.reciprocal(r1[:, :], heads))
                        link(eng.stream_shuffle(r2[:, :], r1[:, :], [16 + j % 16 for j in range(32)]))
                        if b:
                            eng.wait_ge(s_onl, n - 1)
                        eng.tensor_tensor(on[part][:, :], heads, r2[:, :], ALU.mult).then_inc(s_n, 1)
                        eng.wait_ge(s_n, n + 1)

        @block.tensor
        def _(eng):
            mm = eng.matmul

            def scores(b, n):
                qt, hg = divmod(n, HG)
                if n == 0:
                    eng.wait_ge(s_qk[b % 3], 192 * (b // 3 + 1))
                eng.wait_ge(s_mx, 8 * b + n)
                for hh in range(2):
                    mm(ps_s[:, hh * 2 * SEQ:(hh + 1) * 2 * SEQ], identb[:, :], mb_q[:, qt, :, :], start=True, stop=False)
                for pp in range(2):
                    for hh in range(2):
                        rows = slice(64 * hh, 64 * hh + ROWS)
                        at = (2 * hh + pp) * SEQ
                        last = mm(ps_s[:, at:at + SEQ], qs[b % 3][rows, 2 * hg + pp, qt * P:(qt + 1) * P],
                                  ks[b % 3][rows, 2 * hg + pp, :], start=False, stop=pp == 1)
                last.then_inc(s_s, 1)

            def scores_t(b, n):
                hg, kt = divmod(n, TT)
                if n == 0:
                    eng.wait_ge(s_mr[b % 3], 32 * (b // 3 + 1))
                eng.wait_ge(s_e, 8 * b + n)
                for hh in range(2):
                    mm(ps_t[:, hh * 2 * SEQ:(hh + 1) * 2 * SEQ], identb[:, :], mb_k[:, kt, :, :], start=True, stop=False)
                for pp in range(2):
                    for hh in range(2):
                        rows = slice(64 * hh, 64 * hh + ROWS + 1)
                        at = (2 * hh + pp) * SEQ
                        last = mm(ps_t[:, at:at + SEQ], ks[b % 3][rows, 2 * hg + pp, kt * P:(kt + 1) * P],
                                  qs[b % 3][rows, 2 * hg + pp, :], start=False, stop=pp == 1)
                last.then_inc(s_st, 1)

            def values(b, hg):
                eng.wait_ge(s_e, 8 * b + 2 * hg + 2)
                if hg == 0:
                    eng.wait_ge(s_vx, 2 * b + 2)
                if hg % 2 == 0 and b:
                    eng.wait_ge(s_n, 2 * (b - 1) + hg // 2 + 1)
                for kt in range(TT):
                    for j in range(4):
                        last = mm(ps_o[32 * j:32 * j + 32, hg * SEQ:(hg + 1) * SEQ], vx[b % 3][:, kt, 4 * hg + j, :],
                                  pe_[(8 * b + 2 * hg + kt) % 4][:, 2 * (j % 2) + j // 2, :], start=kt == 0, stop=kt == TT - 1)
                last.then_inc(s_pv, 1)

            def transposes(kind, b, src):
                wait_bank(eng, (kind, b))
                o = bank((kind, b))
                for dc in range(DC):
                    for tt in range(TT):
                        at = dc * SEQ + tt * P
                        last = eng.transpose(o[:, at:at + P], src[:, tt, dc * P:(dc + 1) * P], ident[:, :])
                return last

            def project(kind, b, w0, srcT, ones, bias):
                wait_bank(eng, (kind, b))
                o = bank((kind, b))
                for hh in range(2):
                    oo = o[:, hh * SEQ:(hh + 1) * SEQ]
                    mm(oo, bhl[:, bias * D + hh * P:bias * D + (hh + 1) * P], ones, start=True, stop=False)
                    for dc in range(DC):
                        at = w0 + dc * D + hh * P
                        for wl, xl in TERMS:
                            w = (awh, awl)[wl]
                            last = mm(oo, w[:, at:at + P], srcT[xl][:, dc * SEQ:(dc + 1) * SEQ], start=False,
                                      stop=dc == DC - 1 and xl == 1)
                return last

            eng.wait_ge(s_id, 16)
            eng.wait_ge(s_mbf, 1)
            for kt in range(TT):
                for qt in range(TT):
                    at = kt * SEQ + qt * P
                    last = eng.transpose(bank("mask")[:, at:at + P], nz[:, qt, kt * P:(kt + 1) * P], ident[:, :])
            last.then_inc(s_mbT, 1)
            for qt in range(TT):
                last = mm(bank("any")[:, qt * P:(qt + 1) * P], anyq[:, qt:qt + 1].broadcast_to([P, P]), ident[:, :],
                          start=True, stop=True)
            last.then_inc(s_anyb, 1)
            eng.wait_ge(s_idb, 1)
            eng.wait_ge(s_mbq, 1)
            for i in range(ITER):
                for u in range(8):
                    s, st, pv = units(i, u)
                    if s:
                        scores(*s)
                    kind = slots.get(u)
                    b = i - lag[kind] if kind else -1
                    if 0 <= b < NB:
                        if kind == "o":
                            wait_bank(eng, (kind, b))
                            eng.wait_ge(s_onl, 2 * b + 2)
                            for tt in range(TT):
                                o = bank((kind, b))[:, tt * D:(tt + 1) * D]
                                mm(o, ones33[:, 0:P], bhl[:, 3 * D:4 * D], start=True, stop=False)
                                for hg in range(HG):
                                    for wl, xl in TERMS:
                                        w = (awh, awl)[wl]
                                        last = mm(o, (onh, onl)[xl][:, hg, tt * P:(tt + 1) * P],
                                                  w[:, WO + hg * D:WO + (hg + 1) * D], start=False,
                                                  stop=hg == HG - 1 and xl == 1)
                            last.then_inc(s_o, 1)
                        elif kind == "mt":
                            wait_bank(eng, (kind, b))
                            eng.wait_ge(s_mx, 8 * b + 8)
                            for tt in range(TT):
                                last = eng.transpose(bank((kind, b))[0:H, tt * P:(tt + 1) * P], mx[b % 2][:, tt, :], ident[:, :])
                            last.then_inc(s_mt, 1)
                        elif kind == "xt":
                            eng.wait_ge(s_xn, b + 1)
                            transposes(kind, b, xn).then_inc(s_xt, 1)
                        elif kind == "ct":
                            eng.wait_ge(s_c[b % 2], 16 * (b // 2 + 1))
                            transposes(kind, b, c32[b % 2]).then_inc(s_ct, 1)
                        elif kind == "q":
                            if b == 0:
                                eng.wait_ge(s_awl, 1)
                                eng.wait_ge(s_bl, 1)
                                eng.wait_ge(s_any33, 1)
                            eng.wait_ge(s_xl, b + 1)
                            project(kind, b, WQ, xT, any33[:, :], 0).then_inc(s_q, 1)
                        elif kind == "k":
                            eng.wait_ge(s_cl, b + 1)
                            project(kind, b, WK, cT, ones33[:, :], 1).then_inc(s_k, 1)
                        elif kind == "v":
                            wait_bank(eng, (kind, b))
                            for tt in range(TT):
                                o = bank((kind, b))[:, tt * D:(tt + 1) * D]
                                mm(o, ones33[:, 0:P], bhl[:, 2 * D:3 * D], start=True, stop=False)
                                for dc in range(DC):
                                    for wl, xl in TERMS:
                                        w = (awh, awl)[wl]
                                        at = dc * SEQ + tt * P
                                        last = mm(o, cT[xl][:, at:at + P], w[:, WV + dc * D:WV + (dc + 1) * D],
                                                  start=False, stop=dc == DC - 1 and xl == 1)
                            last.then_inc(s_v, 1)
                    if st:
                        scores_t(*st)
                    if pv and pv[1] % 2 == 1:
                        values(pv[0], pv[1] // 2)


def ffn(nc, sb, sem, life, xr, fwh, fwl, ident, neghalf, ffn_in, gate_in, out):
    NG = NE + 1
    with ExitStack() as here:
        t = lambda n, s, d: sb(here, n, s, d)
        pt = lambda n, s: here.enter_context(nc.psum_tensor(n, s, FP32))
        w32 = t("w32", [P, 2, FW], FP32)
        swh = t("swh", [P, 2, FW], FP16)
        swl = t("swl", [P, 2, FW], FP16)
        g32 = t("g32", [P, DC, NG], FP32)
        gh = t("gh", [P, DC, NG], FP16)
        gl = t("gl", [P, DC, NG], FP16)
        st6 = t("f_st6", [P, BT, 6], FP32)
        mv = [t(f"f_mv{i}", [P, BT, 2], FP32) for i in range(2)]
        ve = t("f_ve", [P, BT], FP32)
        rstd = [t(f"f_rstd{i}", [P, BT], FP32) for i in range(2)]
        hn = t("hn", [P, BT, D], FP32)
        hT = [t("hTh", [P, NBLK, DC, BLK], FP16), t("hTl", [P, NBLK, DC, BLK], FP16)]
        lg = t("lg", [P, NT, NG], FP32)
        ex = t("ex", [P, NT, NG], FP32)
        m8 = t("m8", [P, NT], FP32)
        den = t("den", [P, NT], FP32)
        cmp_ = t("cmp_", [P, NT, NE, NE], FP32)
        rank = t("rank", [P, NT, NE], FP32)
        rank2 = t("rank2", [P, NT, NE], FP32)
        wt = t("wt", [P, NT, NX], FP32)
        gs = [t(f"gs{i}", [P, BLK], FP32) for i in range(2)]
        hf = [t(f"hf{i}", [P, BLK], FP32) for i in range(2)]
        hh = [t(f"hh{i}", [P, 3, BLK], FP16) for i in range(2)]
        hl = [t(f"hl{i}", [P, 3, BLK], FP16) for i in range(2)]
        ps_g = [pt(f"ps_g{i}", [P, BLK]) for i in range(2)]
        ps_u = [pt(f"ps_u{i}", [P, BLK]) for i in range(2)]
        ps_d = [pt(f"ps_d{i}", [P, 2 * D]) for i in range(4)]

        f_sw = sem("f_sw"); f_swh = sem("f_swh"); f_swl = sem("f_swl"); f_g = sem("f_g"); f_gh = sem("f_gh"); f_gl = sem("f_gl")
        f_stat = sem("f_stat"); f_pow = sem("f_pow"); f_hn = sem("f_hn"); f_t = sem("f_t")
        f_h = sem("f_h"); f_l = sem("f_l"); f_lg = sem("f_lg"); f_lgc = sem("f_lgc")
        f_sub = sem("f_sub"); f_ex = sem("f_ex"); f_w = sem("f_w")
        f_gd = sem("f_gd"); f_ud = sem("f_ud"); f_si = sem("f_si"); f_hf = sem("f_hf"); f_hh = sem("f_hh")
        f_hl = sem("f_hl"); f_dn = sem("f_dn"); f_acc = sem("f_acc"); f_out = sem("f_out")
        f_dch = sem("f_dch"); f_pch = sem("f_pch")
        steps = [(blk, e) for blk in range(NBLK) for e in range(NX)]
        NC = len(IC)
        block = here.enter_context(nc.Block())

        @block.sync
        def _(eng):
            eng.dma_start(w32[:, :, :], ffn_in[NE:NX, :, :].rearrange("e p w -> p e w")).then_inc(f_sw, 16)
            eng.dma_start(g32[:, :, :], gate_in.rearrange("(c p) e -> p c e", p=P)).then_inc(f_g, 16)
            ov = out.rearrange("(n p) d -> p n d", p=P)
            for blk in range(NBLK):
                eng.wait_ge(f_acc, NX * 2 * (blk + 1))
                eng.dma_start(ov[:, BT * blk:BT * (blk + 1), :], xr[:, BT * blk:BT * (blk + 1), :]).then_inc(f_out, 16)
            eng.wait_ge(f_out, 16 * NBLK)

        @block.gpsimd
        def _(eng):
            for k in range(NBLK):
                eng.wait_ge(f_stat, k + 1)
                if k >= 2:
                    eng.wait_ge(f_hn, k - 1)
                eng.tensor_scalar(ve[:, :], mv[k % 2][:, :, 1], EPS, None, ALU.add).then_inc(f_pch, 1)
                eng.wait_ge(f_pch, k + 1)
                eng.tensor_tensor(rstd[k % 2][:, :], ve[:, :], neghalf[:, :], ALU.pow).then_inc(f_pow, 1)
                eng.wait_ge(f_pow, k + 1)
            eng.wait_ge(f_sw, 16)
            eng.tensor_copy(swh[:, :, :], w32[:, :, :]).then_inc(f_swh, 1)
            eng.wait_ge(f_swh, 1)
            eng.tensor_tensor(swl[:, :, :], w32[:, :, :], swh[:, :, :], ALU.subtract).then_inc(f_swl, 1)
            for n, (blk, e) in enumerate(steps):
                for c, m in enumerate(IC):
                    k = NC * n + c
                    eng.wait_ge(f_hf, k + 1)
                    if n >= 2:
                        eng.wait_ge(f_dn, 2 * (n - 1))
                    eng.tensor_copy(hh[n % 2][0:m, c, :], hf[k % 2][0:m, :]).then_inc(f_hh, 1)
                    eng.wait_ge(f_hh, k + 1)
                    eng.tensor_tensor(hl[n % 2][0:m, c, :], hf[k % 2][0:m, :], hh[n % 2][0:m, c, :],
                                      ALU.subtract).then_inc(f_hl, 1)

        @block.scalar
        def _(eng):
            eng.wait_ge(f_g, 16)
            eng.activation(gh[:, :, :], g32[:, :, :], ACT.Copy).then_inc(f_gh, 1)
            for k in range(NBLK):
                eng.wait_ge(f_t, k + 1)
                for dc in range(DC):
                    last = eng.activation(hT[0][:, k, dc, :], (ps_g[0], ps_u[0])[dc][:, :], ACT.Copy)
                    last.then_inc(f_h, 1)
            eng.wait_ge(f_sub, 1)
            eng.activation(ex[:, :, 0:NE], ex[:, :, 0:NE], ACT.Exp).then_inc(f_ex, 1)
            eng.activation(ex[:, :, NE:NG], lg[:, :, NE:NG], ACT.Exp, scale=-1.0).then_inc(f_ex, 1)
            for n, (blk, e) in enumerate(steps):
                for c, m in enumerate(IC):
                    k = NC * n + c
                    eng.wait_ge(f_gd, k + 1)
                    if k >= 2:
                        eng.wait_ge(f_hf, k - 1)
                    eng.activation(gs[k % 2][0:m, :], ps_g[k % 2][0:m, :], ACT.Silu).then_inc(f_si, 1)

        @block.vector
        def _(eng):
            chain = [0]

            def link(ins):
                chain[0] += 1
                ins.then_inc(f_dch, 1)
                eng.wait_ge(f_dch, chain[0])

            eng.wait_ge(f_gh, 1)
            eng.tensor_tensor(gl[:, :, :], g32[:, :, :], gh[:, :, :], ALU.subtract).then_inc(f_gl, 1)

            def stats(k):
                for j in range(BT):
                    last = eng.bn_stats(st6[:, j, :], xr[:, BT * k + j, :])
                link(last)
                for j in range(BT):
                    last = eng.bn_aggr(mv[k % 2][:, j, :], st6[:, j, :])
                last.then_inc(f_stat, 1)
                eng.wait_ge(f_stat, k + 1)

            stats(0)
            for k in range(NBLK):
                if k + 1 < NBLK:
                    stats(k + 1)
                eng.wait_ge(f_pow, k + 1)
                if k:
                    eng.wait_ge(f_t, k)
                for j in range(BT):
                    last = eng.tensor_scalar(hn[:, j, :], xr[:, BT * k + j, :], mv[k % 2][:, j, 0:1],
                                             rstd[k % 2][:, j:j + 1], ALU.subtract, ALU.mult)
                last.then_inc(f_hn, 1)
                eng.wait_ge(f_hn, k + 1)
                eng.wait_ge(f_h, 2 * k + 2)
                for dc in range(DC):
                    last = eng.tensor_tensor(hT[1][:, k, dc, :], (ps_g[0], ps_u[0])[dc][:, :], hT[0][:, k, dc, :],
                                             ALU.subtract)
                last.then_inc(f_l, 1)
                eng.wait_ge(f_lg, k + 1)
                eng.tensor_copy(lg[:, BT * k:BT * k + BT, :],
                                ps_d[0][:, 0:16 * BT].rearrange("p (j c) -> p j c", c=16)[:, :, 0:NG]).then_inc(f_lgc, 1)
            eng.wait_ge(f_lgc, NBLK)
            link(eng.tensor_reduce(m8[:, :], lg[:, :, 0:NE], axis=AX.X, op=ALU.max))
            b8 = lambda a: a.unsqueeze(2).broadcast_to([P, NT, NE])
            eng.tensor_tensor(ex[:, :, 0:NE], lg[:, :, 0:NE], b8(m8[:, :]), ALU.subtract).then_inc(f_sub, 1)
            eng.wait_ge(f_ex, 2)
            link(eng.tensor_reduce(den[:, :], ex[:, :, 0:NE], axis=AX.X, op=ALU.add))
            link(eng.reciprocal(den[:, :], den[:, :]))
            sc = lg[:, :, 0:NE]
            link(eng.tensor_tensor(sc, ex[:, :, 0:NE], b8(den[:, :]), ALU.mult))
            by_e = sc.unsqueeze(3).broadcast_to([P, NT, NE, NE])
            by_j = sc.unsqueeze(2).broadcast_to([P, NT, NE, NE])
            link(eng.tensor_tensor(cmp_[:, :, :, :], by_j, by_e, ALU.is_gt))
            link(eng.tensor_reduce(rank[:, :, :], cmp_[:, :, :, :], axis=AX.X, op=ALU.add))
            link(eng.tensor_tensor(cmp_[:, :, :, :], by_j, by_e, ALU.is_equal))
            link(eng.memset(rank2[:, :, 0:1], 0.0))
            for e in range(1, NE):
                last = eng.tensor_reduce(rank2[:, :, e:e + 1], cmp_[:, :, e, 0:e], axis=AX.X, op=ALU.add)
            link(last)
            link(eng.tensor_tensor(rank[:, :, :], rank[:, :, :], rank2[:, :, :], ALU.add))
            link(eng.tensor_scalar(rank[:, :, :], rank[:, :, :], 2.0, None, ALU.is_lt))
            link(eng.tensor_tensor(wt[:, :, 0:NE], rank[:, :, :], sc, ALU.mult))
            link(eng.tensor_scalar(ex[:, :, NE:NG], ex[:, :, NE:NG], 1.0, None, ALU.add))
            link(eng.reciprocal(ex[:, :, NE:NG], ex[:, :, NE:NG]))
            for j in range(2):
                last = eng.tensor_copy(wt[:, :, NE + j:NE + j + 1], ex[:, :, NE:NG])
            link(last)
            nacc = [0]

            def combine(n):
                blk, e = steps[n]
                for j in range(BT):
                    if j % 2 == 0:
                        eng.wait_ge(f_dn, 2 * n + j // 2 + 1)
                    if j == 0 and n:
                        eng.wait_ge(f_acc, 2 * n)
                    tile = xr[:, BT * blk + j, :]
                    src = ps_d[2 * (n % 2) + j // 2][:, (j % 2) * D:(j % 2 + 1) * D]
                    last = eng.scalar_tensor_tensor(tile, src, wt[:, BT * blk + j, e:e + 1], tile, ALU.mult, ALU.add)
                    if j % 2:
                        last.then_inc(f_acc, 1)

            for n in range(len(steps)):
                for c, m in enumerate(IC):
                    k = NC * n + c
                    eng.wait_ge(f_si, k + 1)
                    eng.wait_ge(f_ud, k + 1)
                    if k >= 2:
                        eng.wait_ge(f_hl, k - 1)
                    eng.tensor_tensor(hf[k % 2][0:m, :], ps_u[k % 2][0:m, :], gs[k % 2][0:m, :], ALU.mult).then_inc(f_hf, 1)
                    if c == 0 and n >= 2:
                        combine(n - 2)
            combine(len(steps) - 2)
            combine(len(steps) - 1)

        @block.tensor
        def _(eng):
            mm = eng.matmul
            for k in range(NBLK):
                eng.wait_ge(f_hn, k + 1)
                if k:
                    eng.wait_ge(f_l, k)
                for dc in range(DC):
                    for j in range(BT):
                        last = eng.transpose((ps_g[0], ps_u[0])[dc][:, j * P:(j + 1) * P], hn[:, j, dc * P:(dc + 1) * P],
                                             ident[:, :])
                last.then_inc(f_t, 1)
                eng.wait_ge(f_l, k + 1)
                if k == 0:
                    eng.wait_ge(f_gl, 1)
                else:
                    eng.wait_ge(f_lgc, k)
                for j in range(BT):
                    for dc in range(DC):
                        for wl, xl in TERMS:
                            last = mm(ps_d[0][:, 16 * j:16 * j + NG], hT[xl][:, k, dc, j * P:(j + 1) * P],
                                      (gh, gl)[wl][:, dc, :], start=dc == 0 and (wl, xl) == (0, 0),
                                      stop=dc == DC - 1 and xl == 1)
                last.then_inc(f_lg, 1)
            eng.wait_ge(f_lgc, NBLK)

            def weights(e):
                return ((fwh, fwl), e) if e < NE else ((swh, swl), e - NE)

            def up(n):
                blk, e = steps[n]
                if n == NE:
                    eng.wait_ge(f_swl, 1)
                parts, e = weights(e)
                for c, m in enumerate(IC):
                    k = NC * n + c
                    for w0, o, s_out in ((0, ps_g[k % 2], f_gd), (UP0, ps_u[k % 2], f_ud)):
                        if k >= 2:
                            eng.wait_ge(f_si if w0 == 0 else f_hf, k - 1)
                        for dc in range(DC):
                            at = w0 + dc * INTER + P * c
                            for wl, xl in TERMS:
                                last = mm(o[0:m, :], parts[wl][:, e, at:at + m], hT[xl][:, blk, dc, :],
                                          start=dc == 0 and (wl, xl) == (0, 0), stop=dc == DC - 1 and xl == 1)
                        last.then_inc(s_out, 1)

            def down(n):
                blk, e = steps[n]
                parts, e = weights(e)
                eng.wait_ge(f_hl, NC * n + NC)
                if n >= 2:
                    eng.wait_ge(f_acc, 2 * (n - 1))
                for j in range(BT):
                    o = ps_d[2 * (n % 2) + j // 2][:, (j % 2) * D:(j % 2 + 1) * D]
                    for c, m in enumerate(IC):
                        at = DOWN0 + c * D
                        for wl, xl in TERMS:
                            last = mm(o, (hh, hl)[xl][n % 2][0:m, c, j * P:(j + 1) * P], parts[wl][0:m, e, at:at + D],
                                      start=c == 0 and (wl, xl) == (0, 0), stop=c == NC - 1 and xl == 1)
                    if j % 2:
                        last.then_inc(f_dn, 1)

            for n in range(len(steps)):
                up(n)
                if n:
                    down(n - 1)
            down(len(steps) - 1)


def kernel(x, ctx_1024, mask_1x1xSxS2_ik0, L0_xattn_Wq_w, L0_xattn_Wq_b, L0_xattn_Wk_w, L0_xattn_Wk_b,
           L0_xattn_Wv_w, L0_xattn_Wv_b, L0_xattn_Wo_w, L0_xattn_Wo_b, L0_ffn_gate_w, L0_ffn_experts_gate_up,
           L0_ffn_experts_down, L0_ffn_shared_gate_w, L0_ffn_shared_up_w, L0_ffn_shared_down_w,
           L0_ffn_shared_expert_gate_w):
    import numpy as np
    import concourse.bacc as bacc
    from concourse.bass_utils import run_bass_kernel_spmd

    a = np.asarray
    halves = np.concatenate([np.arange(h * DK, (h + 1) * DK) for hh in range(2) for h in range(hh, H, 2)])

    def rows(w):
        return a(w).reshape(DC, P, -1).transpose(1, 0, 2).reshape(P, -1)

    w_in = np.concatenate([rows(a(L0_xattn_Wq_w)[:, halves]), rows(a(L0_xattn_Wk_w)[:, halves]), rows(L0_xattn_Wv_w)], 1)
    bias = np.concatenate([a(L0_xattn_Wq_b)[halves], a(L0_xattn_Wk_b)[halves], a(L0_xattn_Wv_b), a(L0_xattn_Wo_b)])[None]
    w_o = np.zeros((HG, 4, 32, D), np.float32)
    w_o[:, :, 0:DK] = a(L0_xattn_Wo_w).reshape(HG, 4, DK, D)
    w_o = w_o.reshape(HG, P, D).transpose(1, 0, 2).reshape(P, HG * D)
    gate = np.concatenate([a(L0_ffn_experts_gate_up)[:, :INTER], a(L0_ffn_shared_gate_w).reshape(2, INTER, D)])
    up = np.concatenate([a(L0_ffn_experts_gate_up)[:, INTER:], a(L0_ffn_shared_up_w).reshape(2, INTER, D)])
    down = np.concatenate([a(L0_ffn_experts_down), a(L0_ffn_shared_down_w).reshape(D, 2, INTER).transpose(1, 0, 2)])
    ffn_w = np.zeros((NX, P, FW), np.float32)
    for e in range(NX):
        ffn_w[e, :, 0:UP0] = rows(gate[e].T)
        ffn_w[e, :, UP0:DOWN0] = rows(up[e].T)
        padded = np.zeros((len(IC) * P, D), np.float32)
        padded[0:INTER] = down[e].T
        ffn_w[e, :, DOWN0:] = padded.reshape(len(IC), P, D).transpose(1, 0, 2).reshape(P, -1)
    router = np.concatenate([a(L0_ffn_gate_w), a(L0_ffn_shared_expert_gate_w)]).T
    arrays = {
        "x_dram": a(x).reshape(TOK, D), "ctx_dram": a(ctx_1024).reshape(TOK, D),
        "mask_dram": a(mask_1x1xSxS2_ik0).reshape(SEQ, SEQ), "w_in_dram": w_in, "bias_dram": bias, "w_o_dram": w_o,
        "ffn_dram": ffn_w, "router_dram": router, "ident_dram": np.eye(P, dtype=np.float32),
    }
    arrays = {k: np.ascontiguousarray(v) for k, v in arrays.items()}
    nc = bacc.Bacc("TRN2", target_bir_lowering=False, num_devices=1)
    d = {k: nc.dram_tensor(k, v.shape, mybir.dt.from_np(v.dtype), kind="ExternalInput").ap() for k, v in arrays.items()}
    out = nc.dram_tensor("out_dram", (TOK, D), FP32, kind="ExternalOutput").ap()
    qk_scratch = nc.dram_tensor("qk_scratch", (NB, 2, 2, 2, P, SEQ), FP16, kind="Internal").ap()
    m_scratch = nc.dram_tensor("m_scratch", (NB, H, SEQ), FP16, kind="Internal").ap()
    block_kernel(nc, d["x_dram"], d["ctx_dram"], d["mask_dram"], d["w_in_dram"], d["bias_dram"], d["w_o_dram"],
                 d["ffn_dram"], d["router_dram"], d["ident_dram"], out, qk_scratch, m_scratch)
    r = run_bass_kernel_spmd(nc, [arrays], core_ids=[0])
    return r.results[0]["out_dram"].reshape(NB, SEQ, D)
```

```python
import concourse.bass as bass
from concourse import mybir
from contextlib import ExitStack

FP32 = mybir.dt.float32
FP16 = mybir.dt.float16
BF16 = mybir.dt.bfloat16
INT32 = mybir.dt.int32
UINT32 = mybir.dt.uint32
ALU = mybir.AluOpType
ACT = mybir.ActivationFunctionType
AX = mybir.AxisListType

P = 128
D = 256
NB = 16
SEQ = 256
TOK = NB * SEQ
NT = TOK // P
TT = SEQ // P
DC = D // P
H = 16
DK = D // H
NP = H // 2
HG = 4
NE = 8
INTER = 352
NX = NE + 2
IC = [128, 128, 96]
FW = 2 * DC * INTER + len(IC) * D
UP0 = DC * INTER
DOWN0 = 2 * DC * INTER
ROWS = 48
EPS = 1e-5
MASKED = 2.0 ** 30
SCALE = DK ** -0.5
BLK = 512
NBLK = TOK // BLK
BT = BLK // P
TOPK = 2
NTILE = TOPK * TOK // P + NE - 1

TERMS = ((0, 0), (1, 0), (0, 1))


def block_kernel(nc, x, ctx, mask, w_in, bias_in, w_o, ffn_in, gate_in, ident_in, consts_in, out, qk_scratch, m_scratch, den_scratch,
                 sorted_rows, sorted_out):
    with ExitStack() as life:
        sb = lambda stack, n, s, t: stack.enter_context(nc.sbuf_tensor(n, s, t))
        sem = lambda n: life.enter_context(nc.semaphore(n))

        xr = sb(life, "xr", [P, NT, D], FP32)
        fwh = sb(life, "fwh", [P, NE, FW], FP16)
        fwl = sb(life, "fwl", [P, NE, FW], FP16)
        ident = sb(life, "ident", [P, P], FP32)
        neghalf = sb(life, "neghalf", [P, BT], FP32)
        attention(nc, sb, sem, life, xr, fwh, fwl, ident, neghalf,
                  x, ctx, mask, w_in, bias_in, w_o, ffn_in, ident_in, qk_scratch, m_scratch, den_scratch)
        ffn(nc, sb, sem, life, xr, fwh, fwl, ident, neghalf, ffn_in, gate_in, consts_in, sorted_rows, sorted_out, out)


def attention(nc, sb, sem, life, xr, fwh, fwl, ident, neghalf,
              x, ctx, mask, w_in, bias_in, w_o, ffn_in, ident_in, qk_scratch, m_scratch, den_scratch):
    with ExitStack() as here:
        t = lambda n, s, d: sb(here, n, s, d)
        pt = lambda n, s: here.enter_context(nc.psum_tensor(n, s, FP32))
        WA = 3 * DC * D + HG * D
        STAGE = FW // 2
        aw32 = t("aw32", [P, STAGE], FP32)
        awh = t("awh", [P, WA], FP16)
        awl = t("awl", [P, WA], FP16)
        bhl = t("bhl", [33, 4 * D], FP16)
        ones33 = t("ones33", [33, SEQ], FP16)
        any33 = t("any33", [33, SEQ], FP16)
        identb = t("identb", [P, P], BF16)
        anyq = t("anyq", [P, TT], FP32)
        mb_q = t("mb_q", [P, TT, SEQ], BF16)
        mb_k = t("mb_k", [P, TT, SEQ], BF16)
        c32 = [t(f"c32_{i}", [P, TT, D], FP32) for i in range(2)]
        xn = t("xn", [P, TT, D], FP32)
        st6 = t("st6", [P, TT, 6], FP32)
        mv = [t(f"mv{i}", [P, TT, 2], FP32) for i in range(2)]
        ve = [t(f"ve{i}", [P, TT], FP32) for i in range(2)]
        rstd = [t(f"rstd{i}", [P, TT], FP32) for i in range(2)]
        rsa = t("rsa", [P, TT], FP32)
        xT = [t("xTh", [P, DC * SEQ], FP16), t("xTl", [P, DC * SEQ], FP16)]
        cT = [t("cTh", [P, DC * SEQ], FP16), t("cTl", [P, DC * SEQ], FP16)]
        qhl = t("qhl", [P, 2, 2, SEQ], FP16)
        khl = t("khl", [P, 2, 2, SEQ], FP16)
        qs = [t(f"qs{i}", [P, NP, SEQ], FP16) for i in range(3)]
        ks = [t(f"ks{i}", [P, NP, SEQ], FP16) for i in range(3)]
        vx = [t(f"vx{i}", [P, TT, H, 32], FP32) for i in range(3)]
        mx = [t(f"mx{i}", [P, TT, H], FP32) for i in range(2)]
        nm = t("nm", [H, SEQ], FP16)
        pe_ = [t(f"p{i}", [P, 4, SEQ], FP32) for i in range(4)]
        mi = pe_[0][:, 0:TT, :].bitcast(INT32)
        nz = pe_[1][:, 0:TT, :]
        b32 = pe_[2][0:33, :, :].rearrange("p a b -> p (a b)")
        bh2 = pe_[3][0:33, 0:2, :].rearrange("p a b -> p (a b)").bitcast(FP16)
        o32 = [t(f"o32_{i}", [P, HG * SEQ], FP32) for i in range(2)]
        den = t("sums", [P, H * SEQ // P], FP32)
        rb = t("rb", [P, HG * SEQ], FP32)
        onh = t("onh", [P, HG, SEQ], FP16)
        onl = t("onl", [P, HG, SEQ], FP16)

        ps_s = pt("ps_s", [P, 4 * SEQ])
        ps_t = pt("ps_t", [P, 4 * SEQ])
        ps_o = pt("ps_o", [P, HG * SEQ])
        ps_m = [pt(f"ps_m{i}", [P, 2 * SEQ]) for i in range(2)]

        WQ, WK, WV, WO = 0, DC * D, 2 * DC * D, 3 * DC * D

        s_x = [sem(f"s_x{i}") for i in range(8)]
        s_c = [sem(f"s_c{i}") for i in range(2)]
        s_aw = sem("s_aw"); s_bias = sem("s_bias"); s_mi = sem("s_mi"); s_id = sem("s_id")
        s_fw = sem("s_fw"); s_fwd = sem("s_fwd"); s_wo = sem("s_wo")
        s_awh = sem("s_awh"); s_awl = sem("s_awl")
        s_const = sem("s_const")
        s_bh = sem("s_bh"); s_bl = sem("s_bl")
        s_idb = sem("s_idb")
        s_nz = sem("s_nz"); s_mbf = sem("s_mbf"); s_mbq = sem("s_mbq"); s_mbT = sem("s_mbT"); s_mbk = sem("s_mbk")
        s_anyb = sem("s_anyb"); s_any33 = sem("s_any33")
        s_stat = sem("s_stat"); s_pow = sem("s_pow"); s_xn = sem("s_xn")
        s_xt = sem("s_xt"); s_ct = sem("s_ct")
        s_xh = sem("s_xh"); s_xl = sem("s_xl"); s_ch = sem("s_ch"); s_cl = sem("s_cl")
        s_q = sem("s_q"); s_k = sem("s_k"); s_v = sem("s_v")
        s_qh = sem("s_qh"); s_ql = sem("s_ql"); s_kh = sem("s_kh"); s_kl = sem("s_kl"); s_vx = sem("s_vx")
        s_qw = sem("s_qw"); s_kw = sem("s_kw")
        s_qk = [sem(f"s_qk{i}") for i in range(3)]
        s_s = sem("s_s"); s_mx = sem("s_mx"); s_mt = sem("s_mt"); s_nm = sem("s_nm"); s_mw = sem("s_mw")
        s_mr = [sem(f"s_mr{i}") for i in range(3)]
        s_st = sem("s_st"); s_e = sem("s_e"); s_pv = sem("s_pv")
        s_oc = sem("s_oc"); s_dw = sem("s_dw"); s_dr = sem("s_dr"); s_rc = sem("s_rc"); s_rw = sem("s_rw"); s_rr = sem("s_rr")
        s_n = sem("s_n"); s_onh = sem("s_onh"); s_onl = sem("s_onl")
        s_o = sem("s_o"); s_res = sem("s_res")
        s_free = [sem(f"s_free{i}") for i in range(2)]
        s_dch = sem("s_dch"); s_pch = sem("s_pch"); s_ach = sem("s_ach")

        order = ["mask", "any"]
        slots = {0: "mt", 1: "xt", 2: "ct", 3: "q", 4: "k", 5: "v", 7: "o"}
        lag = {"o": 4, "mt": 2, "xt": 0, "ct": 0, "q": 0, "k": 0, "v": 0}
        ITER = NB + 5
        for i in range(ITER):
            for u in range(8):
                kind = slots.get(u)
                if kind and 0 <= i - lag[kind] < NB:
                    order.append((kind, i - lag[kind]))
        use = {k: n for n, k in enumerate(order)}
        bank = lambda k: ps_m[use[k] % 2]

        def wait_bank(eng, k):
            if use[k] // 2:
                eng.wait_ge(s_free[use[k] % 2], use[k] // 2)

        def dividing(i, u):
            g = 8 * i + u - 28
            return [(b, g - 8 * b) for b in range(max(0, g // 8 - 1), min(NB, g // 8 + 1)) if 0 <= g - 8 * b <= 6]

        free = lambda k: s_free[use[k] % 2]

        def units(i, u):
            g = 8 * i + u
            found = []
            for late in (8, 20, 21):
                found.append(divmod(g - late, 8) if 0 <= g - late < 8 * NB else None)
            return found

        block = here.enter_context(nc.Block())

        @block.sync
        def _(eng):
            eng.dma_start(ident[:, :], ident_in).then_inc(s_id, 16)
            eng.dma_start(mi[:, :, :], mask.rearrange("(t p) k -> p t k", p=P)).then_inc(s_mi, 16)
            eng.dma_start(aw32[:, 0:WV], w_in[:, 0:WV]).then_inc(s_aw, 16)
            xv = x.rearrange("(n p) d -> p n d", p=P)
            cv = ctx.rearrange("(b t p) d -> b p t d", p=P, t=TT)

            def load_c(b):
                if b >= 2:
                    eng.wait_ge(s_ct, b - 1)
                eng.dma_start(c32[b % 2][:, :, :], cv[b, :, :, :]).then_inc(s_c[b % 2], 16)

            eng.dma_start(xr[:, 0:4, :], xv[:, 0:4, :]).then_inc(s_x[0], 16)
            load_c(0)
            eng.dma_start(b32[0:1, :], bias_in).then_inc(s_bias, 16)
            eng.dma_start(b32[32:33, :], bias_in).then_inc(s_bias, 16)
            load_c(1)
            for n in range(1, 8):
                eng.dma_start(xr[:, 4 * n:4 * n + 4, :], xv[:, 4 * n:4 * n + 4, :]).then_inc(s_x[n], 16)
            eng.wait_ge(s_awl, 1)
            eng.dma_start(aw32[:, 0:WO - WV], w_in[:, WV:WO]).then_inc(s_aw, 16)
            eng.wait_ge(s_awl, 2)
            eng.dma_start(aw32[:, 0:HG * D], w_o).then_inc(s_wo, 16)
            for i in range(ITER):
                if 0 < i <= 2 * NE:
                    e, part = divmod(i - 1, 2)
                    eng.wait_ge(s_awl, 2 + i)
                    eng.dma_start(aw32[:, :], ffn_in[e, :, part * STAGE:(part + 1) * STAGE]).then_inc(s_fw, 16)
                b = i - 2
                if 0 <= b < NB:
                    eng.wait_ge(s_nm, b + 1)
                    eng.dma_start(m_scratch[b, :, :], nm[:, :]).then_inc(s_mw, 16)
                    eng.wait_ge(s_mw, 16 * (b + 1))
                    mv_ = m_scratch[b, :, :].rearrange("(h p) t -> h p t", h=2)
                    for hh in range(2):
                        eng.dma_start(qs[b % 3][64 * hh + ROWS:64 * hh + ROWS + 1, :, :],
                                      mv_[hh:hh + 1, :, :]).then_inc(s_mr[b % 3], 16)
                if i < NB:
                    if i + 1 < NB and i >= 1:
                        load_c(i + 1)
                    for what, hl, s_lo, s_w in ((0, qhl, s_ql, s_qw), (1, khl, s_kl, s_kw)):
                        eng.wait_ge(s_lo, i + 1)
                        eng.dma_start(qk_scratch[i, what, :, :, :, :].rearrange("l h r t -> r l h t"),
                                      hl[:, :, :, :]).then_inc(s_w, 16)
                    if i >= 3:
                        eng.wait_ge(s_st, 8 * (i - 2))
                    for what, dst, s_w, parts in ((0, qs[i % 3], s_qw, (0, 0, 1)), (1, ks[i % 3], s_kw, (0, 1, 0))):
                        eng.wait_ge(s_w, 16 * (i + 1))
                        for hh in range(2):
                            for n, part in enumerate(parts):
                                row = 64 * hh + 16 * n
                                src = qk_scratch[i, what, part, hh, :, :].rearrange("(p d) t -> d p t", d=DK)
                                eng.dma_start(dst[row:row + DK, :, :], src).then_inc(s_qk[i % 3], 16)

        @block.gpsimd
        def _(eng):
            chain = [0]

            def link(ins):
                chain[0] += 1
                ins.then_inc(s_pch, 1)
                eng.wait_ge(s_pch, chain[0])

            eng.memset(neghalf[:, :], -0.5)
            eng.memset(ones33[:, :], 1.0).then_inc(s_const, 1)
            eng.memset(bhl[:, :], 0.0).then_inc(s_const, 1)
            for i in range(3):
                eng.memset(vx[i][:, :, :, :], 1.0).then_inc(s_const, 1)
                last = eng.memset(ks[i][:, :, :], 1.0)
                last.then_inc(s_const, 1)
            eng.memset(rb[:, :], 0.0).then_inc(s_const, 1)
            eng.wait_ge(s_const, 9)

            def split(src, hi, lo, loaded, need, s_hi):
                eng.wait_ge(loaded, need)
                eng.tensor_copy(hi, src).then_inc(s_hi, 1)
                return hi, lo

            def power(b):
                eng.wait_ge(s_stat, b + 1)
                if b >= 2:
                    eng.wait_ge(s_xn, b - 1)
                link(eng.tensor_scalar(ve[b % 2][:, :], mv[b % 2][:, :, 1], EPS, None, ALU.add))
                eng.tensor_tensor(rstd[b % 2][:, :], ve[b % 2][:, :], neghalf[:, 0:TT], ALU.pow).then_inc(s_pow, 1)

            power(0)
            eng.wait_ge(s_awh, 1)
            eng.tensor_tensor(awl[:, 0:WV], aw32[:, 0:WV], awh[:, 0:WV], ALU.subtract).then_inc(s_awl, 1)
            power(1)
            eng.wait_ge(s_awh, 2)
            eng.tensor_tensor(awl[:, WV:WO], aw32[:, 0:WO - WV], awh[:, WV:WO], ALU.subtract).then_inc(s_awl, 1)
            eng.wait_ge(s_wo, 16)
            link(eng.tensor_copy(awh[:, WO:WA], aw32[:, 0:HG * D]))
            eng.tensor_tensor(awl[:, WO:WA], aw32[:, 0:HG * D], awh[:, WO:WA], ALU.subtract).then_inc(s_awl, 1)
            for i in range(ITER):
                if 2 <= i + 1 < NB:
                    power(i + 1)
                if 0 < i <= 2 * NE:
                    e, part = divmod(i - 1, 2)
                    cols = slice(part * STAGE, (part + 1) * STAGE)
                    eng.wait_ge(s_fw, 16 * i)
                    eng.tensor_copy(fwh[:, e, cols], aw32[:, :]).then_inc(s_fwd, 1)
                    eng.wait_ge(s_fwd, i)
                    eng.tensor_tensor(fwl[:, e, cols], aw32[:, :], fwh[:, e, cols], ALU.subtract).then_inc(s_awl, 1)
                b = i - 4
                if 0 <= b < NB:
                    heads = o32[b % 2]
                    eng.wait_ge(s_rr, 64 * (b + 1))
                    eng.wait_ge(s_oc, 2 * b + 2)
                    eng.tensor_tensor(heads[:, :], heads[:, :], rb[:, :], ALU.mult).then_inc(s_n, 1)
                    eng.wait_ge(s_onh, b + 1)
                    eng.tensor_tensor(onl[:, :, :], heads[:, :].rearrange("p (g t) -> p g t", g=HG), onh[:, :, :],
                                      ALU.subtract).then_inc(s_onl, 1)
        @block.scalar
        def _(eng):
            eng.wait_ge(s_aw, 16)
            eng.activation(awh[:, 0:WV], aw32[:, 0:WV], ACT.Copy).then_inc(s_awh, 1)
            eng.wait_ge(s_bias, 32)
            eng.wait_ge(s_const, 2)
            eng.activation(bhl[0:1, :], b32[0:1, :], ACT.Copy).then_inc(s_bh, 1)
            eng.activation(bh2[32:33, :], b32[32:33, :], ACT.Copy).then_inc(s_bh, 1)
            eng.wait_ge(s_id, 16)
            eng.activation(identb[:, :], ident[:, :], ACT.Copy).then_inc(s_idb, 1)
            eng.wait_ge(s_mbT, 1)
            eng.activation(mb_k[:, :, :], bank("mask")[:, :].rearrange("p (t q) -> p t q", t=TT), ACT.Copy).then_inc(s_mbk, 1)
            eng.wait_ge(s_anyb, 1)
            eng.activation(any33[:, :], bank("any")[0:33, 0:SEQ], ACT.Copy).then_inc(s_any33, 1)
            eng.wait_ge(s_mbk, 1)
            eng.wait_ge(s_any33, 1)
            eng.nop().then_inc(s_free[0], 1)
            eng.nop().then_inc(s_free[1], 1)
            eng.wait_ge(s_aw, 32)
            eng.activation(awh[:, WV:WO], aw32[:, 0:WO - WV], ACT.Copy).then_inc(s_awh, 1)
            for i in range(ITER):
                for u in range(8):
                    kind = slots.get(u)
                    b = i - lag[kind] if kind else -1
                    if 0 <= b < NB:
                        if kind == "mt":
                            eng.wait_ge(s_mt, b + 1)
                            if b:
                                eng.wait_ge(s_mw, 16 * b)
                            eng.activation(nm[:, :], bank((kind, b))[0:H, 0:SEQ], ACT.Copy, scale=-1.0).then_inc(s_nm, 1)
                            eng.wait_ge(s_nm, b + 1)
                            eng.nop().then_inc(free((kind, b)), 1)
                        elif kind in ("xt", "ct"):
                            s_in, dst, s_out, s_used = (s_xt, xT[0], s_xh, s_q) if kind == "xt" else (s_ct, cT[0], s_ch, s_v)
                            eng.wait_ge(s_in, b + 1)
                            if b:
                                eng.wait_ge(s_used, b)
                            eng.activation(dst[:, :], bank((kind, b))[:, :], ACT.Copy).then_inc(s_out, 1)
                        elif kind in ("q", "k"):
                            s_in, dst, s_out, s_used = (s_q, qhl, s_qh, s_qw) if kind == "q" else (s_k, khl, s_kh, s_kw)
                            eng.wait_ge(s_in, b + 1)
                            if b:
                                eng.wait_ge(s_used, 16 * b)
                            eng.activation(dst[:, 0, :, :], bank((kind, b))[:, :].rearrange("p (h t) -> p h t", h=2),
                                           ACT.Copy).then_inc(s_out, 1)
                        elif kind == "v":
                            eng.wait_ge(s_v, b + 1)
                            if b >= 3:
                                eng.wait_ge(s_pv, 4 * (b - 2))
                            for tt in range(TT):
                                last = eng.activation(vx[b % 3][:, tt, :, 0:DK],
                                                      bank((kind, b))[:, tt * D:(tt + 1) * D].rearrange("p (h d) -> p h d", h=H),
                                                      ACT.Copy)
                                last.then_inc(s_vx, 1)
                            eng.wait_ge(s_vx, 2 * b + 2)
                            eng.nop().then_inc(free((kind, b)), 1)
                    _, st, pv = units(i, u)
                    if st:
                        n = 8 * st[0] + st[1]
                        eng.wait_ge(s_st, n + 1)
                        if n >= 4:
                            eng.wait_ge(s_pv, (n - 4) // 2 + 1)
                        eng.activation(pe_[n % 4][:, :, :], ps_t[:, :].rearrange("p (h q) -> p h q", h=4), ACT.Exp,
                                       scale=SCALE).then_inc(s_e, 1)
                    if pv and pv[1] % 4 == 3:
                        b, part = pv[0], pv[1] // 4
                        cols = slice(2 * part * SEQ, (2 * part + 2) * SEQ)
                        eng.wait_ge(s_pv, 4 * b + 2 * part + 2)
                        if b >= 2 and part == 0:
                            eng.wait_ge(s_onl, b - 1)
                        eng.activation(o32[b % 2][:, cols], ps_o[:, cols], ACT.Copy).then_inc(s_oc, 1)
                    for b, step in dividing(i, u):
                        if step == 0:
                            eng.wait_ge(s_oc, 2 * b + 2)
                            eng.dma_start(den_scratch[b, 0, :].rearrange("(j c) -> j c", j=4),
                                          o32[b % 2][DK:P:32, :]).then_inc(s_dw, 16)
                        elif step == 1:
                            eng.wait_ge(s_dw, 16 * (b + 1))
                            if b:
                                eng.wait_ge(s_rw, 16 * b)
                            eng.dma_start(den[:, :], den_scratch[b, 0, :].rearrange("(p c) -> p c", p=P)).then_inc(s_dr, 16)
                        elif step == 3:
                            eng.wait_ge(s_rc, b + 1)
                            eng.dma_start(den_scratch[b, 1, :].rearrange("(p c) -> p c", p=P), den[:, :]).then_inc(s_rw, 16)
                        elif step == 4:
                            eng.wait_ge(s_rw, 16 * (b + 1))
                            if b:
                                eng.wait_ge(s_n, b)
                            for j in range(4):
                                row = den_scratch[b, 1:2, j * HG * SEQ:(j + 1) * HG * SEQ]
                                eng.dma_start(rb[32 * j:32 * j + DK, :], row.broadcast_to([DK, HG * SEQ])).then_inc(s_rr, 16)
                        elif step == 6:
                            eng.wait_ge(s_n, b + 1)
                            if b:
                                eng.wait_ge(s_o, b)
                            eng.activation(onh[:, :, :], o32[b % 2][:, :].rearrange("p (g t) -> p g t", g=HG),
                                           ACT.Copy).then_inc(s_onh, 1)

        @block.vector
        def _(eng):
            chain = [0]

            def link(ins):
                chain[0] += 1
                ins.then_inc(s_dch, 1)
                eng.wait_ge(s_dch, chain[0])

            def stats(b):
                eng.wait_ge(s_x[b // 2], 16)
                if b >= 2:
                    eng.wait_ge(s_pow, b - 1)
                for tt in range(TT):
                    last = eng.bn_stats(st6[:, tt, :], xr[:, TT * b + tt, :])
                link(last)
                for tt in range(TT):
                    last = eng.bn_aggr(mv[b % 2][:, tt, :], st6[:, tt, :])
                link(last)
                eng.nop().then_inc(s_stat, 1)

            def normalise(b):
                eng.wait_ge(s_pow, b + 1)
                link(eng.tensor_tensor(rsa[:, :], rstd[b % 2][:, :], anyq[:, :], ALU.mult))
                if b:
                    eng.wait_ge(s_xt, b)
                for tt in range(TT):
                    last = eng.tensor_scalar(xn[:, tt, :], xr[:, TT * b + tt, :], mv[b % 2][:, tt, 0:1],
                                             rsa[:, tt:tt + 1], ALU.subtract, ALU.mult)
                last.then_inc(s_xn, 1)
                eng.wait_ge(s_xn, b + 1)

            stats(0)
            stats(1)
            eng.wait_ge(s_mi, 16)
            link(eng.tensor_scalar(nz[:, :, :], mi[:, :, :], 0, None, ALU.not_equal))
            link(eng.tensor_reduce(anyq[:, :], nz[:, :, :], axis=AX.X, op=ALU.max))
            link(eng.tensor_scalar(nz[:, :, :], nz[:, :, :], 1.0, MASKED, ALU.subtract, ALU.mult))
            for tt in range(TT):
                last = eng.tensor_scalar(nz[:, tt, :], nz[:, tt, :], anyq[:, tt:tt + 1], None, ALU.mult)
            last.then_inc(s_mbf, 1)
            eng.wait_ge(s_mbf, 1)
            eng.tensor_copy(mb_q[:, :, :], nz[:, :, :]).then_inc(s_mbq, 1)
            eng.wait_ge(s_bh, 2)
            eng.tensor_tensor(bhl[32:33, :], b32[32:33, :], bh2[32:33, :], ALU.subtract).then_inc(s_bl, 1)
            for i in range(ITER):
                for u in range(8):
                    s, _, _ = units(i, u)
                    if s:
                        b, n = s
                        qt, hg = divmod(n, HG)
                        eng.wait_ge(s_s, 8 * b + n + 1)
                        if n == 0 and b >= 2:
                            eng.wait_ge(s_mt, b - 1)
                        eng.tensor_reduce(mx[b % 2][:, qt, :].rearrange("p (h g j) -> p h g j", h=2, g=HG)[:, :, hg, :],
                                          ps_s[:, :].rearrange("p (h j k) -> p h j k", h=2, j=2),
                                          axis=AX.X, op=ALU.max).then_inc(s_mx, 1)
                    kind = slots.get(u)
                    b = i - lag[kind] if kind else -1
                    if u == 0 and i == 0:
                        normalise(0)
                    if u == 7 and i + 1 < NB:
                        normalise(i + 1)
                    if u == 3 and 2 <= i + 2 < NB:
                        stats(i + 2)
                    if 0 <= b < NB:
                        if kind == "o":
                            eng.wait_ge(s_o, b + 1)
                            tiles = xr[:, TT * b:TT * b + TT, :]
                            eng.tensor_tensor(tiles, bank((kind, b))[:, :].rearrange("p (t d) -> p t d", t=TT), tiles,
                                              ALU.add).then_inc(free((kind, b)), 1)
                        elif kind in ("xt", "ct"):
                            s_in, (hi, lo), s_out, s_used = (s_xh, xT, s_xl, s_q) if kind == "xt" else (s_ch, cT, s_cl, s_v)
                            eng.wait_ge(s_in, b + 1)
                            eng.tensor_tensor(lo[:, :], bank((kind, b))[:, :], hi[:, :], ALU.subtract).then_inc(s_out, 1)
                            eng.wait_ge(s_out, b + 1)
                            eng.nop().then_inc(free((kind, b)), 1)
                        elif kind in ("q", "k"):
                            s_in, hl, s_out = (s_qh, qhl, s_ql) if kind == "q" else (s_kh, khl, s_kl)
                            eng.wait_ge(s_in, b + 1)
                            eng.tensor_tensor(hl[:, 1, :, :], bank((kind, b))[:, :].rearrange("p (h t) -> p h t", h=2),
                                              hl[:, 0, :, :], ALU.subtract).then_inc(s_out, 1)
                            eng.wait_ge(s_out, b + 1)
                            eng.nop().then_inc(free((kind, b)), 1)
                    for b, step in dividing(i, u):
                        if step == 2:
                            eng.wait_ge(s_dr, 16 * (b + 1))
                            eng.reciprocal(den[:, :], den[:, :]).then_inc(s_rc, 1)

        @block.tensor
        def _(eng):
            mm = eng.matmul

            def scores(b, n):
                qt, hg = divmod(n, HG)
                if n == 0:
                    eng.wait_ge(s_qk[b % 3], 192 * (b // 3 + 1))
                eng.wait_ge(s_mx, 8 * b + n)
                for hh in range(2):
                    mm(ps_s[:, hh * 2 * SEQ:(hh + 1) * 2 * SEQ], identb[:, :], mb_q[:, qt, :].unsqueeze(1).broadcast_to([P, 2, SEQ]), start=True, stop=False)
                for pp in range(2):
                    for hh in range(2):
                        rows = slice(64 * hh, 64 * hh + ROWS)
                        at = (2 * hh + pp) * SEQ
                        last = mm(ps_s[:, at:at + SEQ], qs[b % 3][rows, 2 * hg + pp, qt * P:(qt + 1) * P],
                                  ks[b % 3][rows, 2 * hg + pp, :], start=False, stop=pp == 1)
                last.then_inc(s_s, 1)

            def scores_t(b, n):
                hg, kt = divmod(n, TT)
                if n == 0:
                    eng.wait_ge(s_mr[b % 3], 32 * (b // 3 + 1))
                eng.wait_ge(s_e, 8 * b + n)
                for hh in range(2):
                    mm(ps_t[:, hh * 2 * SEQ:(hh + 1) * 2 * SEQ], identb[:, :], mb_k[:, kt, :].unsqueeze(1).broadcast_to([P, 2, SEQ]), start=True, stop=False)
                for pp in range(2):
                    for hh in range(2):
                        rows = slice(64 * hh, 64 * hh + ROWS + 1)
                        at = (2 * hh + pp) * SEQ
                        last = mm(ps_t[:, at:at + SEQ], ks[b % 3][rows, 2 * hg + pp, kt * P:(kt + 1) * P],
                                  qs[b % 3][rows, 2 * hg + pp, :], start=False, stop=pp == 1)
                last.then_inc(s_st, 1)

            def values(b, hg):
                eng.wait_ge(s_e, 8 * b + 2 * hg + 2)
                if hg == 0:
                    eng.wait_ge(s_vx, 2 * b + 2)
                if hg % 2 == 0 and b:
                    eng.wait_ge(s_oc, 2 * (b - 1) + hg // 2 + 1)
                for kt in range(TT):
                    for j in range(4):
                        last = mm(ps_o[32 * j:32 * j + 32, hg * SEQ:(hg + 1) * SEQ], vx[b % 3][:, kt, 4 * hg + j, :],
                                  pe_[(8 * b + 2 * hg + kt) % 4][:, 2 * (j % 2) + j // 2, :], start=kt == 0, stop=kt == TT - 1)
                last.then_inc(s_pv, 1)

            def transposes(kind, b, src):
                wait_bank(eng, (kind, b))
                o = bank((kind, b))
                for dc in range(DC):
                    for tt in range(TT):
                        at = dc * SEQ + tt * P
                        last = eng.transpose(o[:, at:at + P], src[:, tt, dc * P:(dc + 1) * P], ident[:, :])
                return last

            def project(kind, b, w0, srcT, ones, bias):
                wait_bank(eng, (kind, b))
                o = bank((kind, b))
                for hh in range(2):
                    oo = o[:, hh * SEQ:(hh + 1) * SEQ]
                    mm(oo, bhl[:, bias * D + hh * P:bias * D + (hh + 1) * P], ones, start=True, stop=False)
                    for dc in range(DC):
                        at = w0 + dc * D + hh * P
                        for wl, xl in TERMS:
                            w = (awh, awl)[wl]
                            last = mm(oo, w[:, at:at + P], srcT[xl][:, dc * SEQ:(dc + 1) * SEQ], start=False,
                                      stop=dc == DC - 1 and xl == 1)
                return last

            eng.wait_ge(s_id, 16)
            eng.wait_ge(s_mbf, 1)
            for kt in range(TT):
                for qt in range(TT):
                    at = kt * SEQ + qt * P
                    last = eng.transpose(bank("mask")[:, at:at + P], nz[:, qt, kt * P:(kt + 1) * P], ident[:, :])
            last.then_inc(s_mbT, 1)
            for qt in range(TT):
                last = mm(bank("any")[:, qt * P:(qt + 1) * P], anyq[:, qt:qt + 1].broadcast_to([P, P]), ident[:, :],
                          start=True, stop=True)
            last.then_inc(s_anyb, 1)
            eng.wait_ge(s_idb, 1)
            eng.wait_ge(s_mbq, 1)
            for i in range(ITER):
                for u in range(8):
                    s, st, pv = units(i, u)
                    if s:
                        scores(*s)
                    kind = slots.get(u)
                    b = i - lag[kind] if kind else -1
                    if 0 <= b < NB:
                        if kind == "o":
                            wait_bank(eng, (kind, b))
                            eng.wait_ge(s_onl, b + 1)
                            for tt in range(TT):
                                o = bank((kind, b))[:, tt * D:(tt + 1) * D]
                                mm(o, ones33[:, 0:P], bhl[:, 3 * D:4 * D], start=True, stop=False)
                                for hg in range(HG):
                                    for wl, xl in TERMS:
                                        w = (awh, awl)[wl]
                                        last = mm(o, (onh, onl)[xl][:, hg, tt * P:(tt + 1) * P],
                                                  w[:, WO + hg * D:WO + (hg + 1) * D], start=False,
                                                  stop=hg == HG - 1 and xl == 1)
                            last.then_inc(s_o, 1)
                        elif kind == "mt":
                            wait_bank(eng, (kind, b))
                            eng.wait_ge(s_mx, 8 * b + 8)
                            for tt in range(TT):
                                last = eng.transpose(bank((kind, b))[0:H, tt * P:(tt + 1) * P], mx[b % 2][:, tt, :], ident[:, :])
                            last.then_inc(s_mt, 1)
                        elif kind == "xt":
                            eng.wait_ge(s_xn, b + 1)
                            transposes(kind, b, xn).then_inc(s_xt, 1)
                        elif kind == "ct":
                            eng.wait_ge(s_c[b % 2], 16 * (b // 2 + 1))
                            transposes(kind, b, c32[b % 2]).then_inc(s_ct, 1)
                        elif kind == "q":
                            if b == 0:
                                eng.wait_ge(s_awl, 1)
                                eng.wait_ge(s_bl, 1)
                                eng.wait_ge(s_any33, 1)
                            eng.wait_ge(s_xl, b + 1)
                            project(kind, b, WQ, xT, any33[:, :], 0).then_inc(s_q, 1)
                        elif kind == "k":
                            eng.wait_ge(s_cl, b + 1)
                            project(kind, b, WK, cT, ones33[:, :], 1).then_inc(s_k, 1)
                        elif kind == "v":
                            wait_bank(eng, (kind, b))
                            if b == 0:
                                eng.wait_ge(s_awl, 2)
                            for tt in range(TT):
                                o = bank((kind, b))[:, tt * D:(tt + 1) * D]
                                mm(o, ones33[:, 0:P], bhl[:, 2 * D:3 * D], start=True, stop=False)
                                for dc in range(DC):
                                    for wl, xl in TERMS:
                                        w = (awh, awl)[wl]
                                        at = dc * SEQ + tt * P
                                        last = mm(o, cT[xl][:, at:at + P], w[:, WV + dc * D:WV + (dc + 1) * D],
                                                  start=False, stop=dc == DC - 1 and xl == 1)
                            last.then_inc(s_v, 1)
                    if st:
                        scores_t(*st)
                    if pv and pv[1] % 2 == 1:
                        values(pv[0], pv[1] // 2)


def ffn(nc, sb, sem, life, xr, fwh, fwl, ident, neghalf, ffn_in, gate_in, consts_in, sorted_rows, sorted_out, out):
    NG = NE + 1
    with ExitStack() as here:
        t = lambda n, s, d: sb(here, n, s, d)
        pt = lambda n, s: here.enter_context(nc.psum_tensor(n, s, FP32))
        NGB = 4
        staged = t("staged", [P, FW], FP32)
        w32 = staged
        ya = [staged[:, 2 * D * i:2 * D * (i + 1)].rearrange("p (j d) -> p j d", j=2) for i in range(NGB)]
        swh = t("swh", [P, 2, FW], FP16)
        swl = t("swl", [P, 2, FW], FP16)
        g32 = t("g32", [P, DC, NG], FP32)
        gh = t("gh", [P, DC, NG], FP16)
        gl = t("gl", [P, DC, NG], FP16)
        consts = t("consts", [P, 2 * P + NT + NTILE], FP32)
        identh = t("identh", [P, P], FP16)
        below = consts[:, 0:P]
        ones = consts[:, P:2 * P]
        tile_starts = consts[:, 2 * P:2 * P + NT]
        tile_ids = consts[:, 2 * P + NT:]
        st6 = t("f_st6", [P, BT, 6], FP32)
        mv = [t(f"f_mv{i}", [P, BT, 2], FP32) for i in range(2)]
        ve = t("f_ve", [P, BT], FP32)
        rstd = [t(f"f_rstd{i}", [P, BT], FP32) for i in range(2)]
        hn = t("hn", [P, BT, D], FP32)
        hrow = t("hrow", [P, NT, 2 * D], FP16)
        hT = [t("hTh", [P, 2, DC, BLK], FP16), t("hTl", [P, 2, DC, BLK], FP16)]
        lg = t("lg", [P, NT, NG], FP32)
        ex = t("ex", [P, NT, NG], FP32)
        m8 = t("m8", [P, NT], FP32)
        den = t("den", [P, NT], FP32)
        cmp_ = hn[:, :, :].rearrange("p a b -> p (a b)")
        rank = t("rank", [P, NT, NE], FP32)
        chosen = [t(f"chosen{i}", [P, NT, NE], FP32) for i in range(2)]
        sel = t("sel", [P, NT, NE], FP32)
        scan = [t(f"scan{i}", [P, NT, NE], FP32) for i in range(2)]
        ends = [t(f"ends{i}", [P, NE], FP32) for i in range(2)]
        ntl = t("ntl", [P, NE], FP32)
        emapf = t("emapf", [1, NTILE], FP32)
        emap = t("emap", [1, NTILE], INT32)
        slotf = t("slotf", [P, 2, NT], FP32)
        slot = t("slot", [P, 2, NT], UINT32)
        wsel = t("wsel", [P, 2, NT], FP32)
        gs = [hn[:, 2 * i:2 * i + 2, :].rearrange("p a b -> p (a b)") for i in range(2)]
        hf = [t(f"hf{i}", [P, BLK], FP32) for i in range(2)]
        hh = [t(f"hh{i}", [P, 3, BLK], FP16) for i in range(2)]
        hl = [t(f"hl{i}", [P, 3, BLK], FP16) for i in range(2)]
        xg = [t(f"xg{i}", [P, 2 * D], FP16) for i in range(3)]
        xgT = [t(f"xgT{i}", [P, 2, DC, P], FP16) for i in range(2)]
        ys = [t(f"ys{i}", [P, D], FP32) for i in range(3)]
        ps_g = [pt(f"ps_g{i}", [P, BLK]) for i in range(2)]
        ps_u = [pt(f"ps_u{i}", [P, BLK]) for i in range(2)]
        ps_d = [pt(f"ps_d{i}", [P, 2 * D]) for i in range(4)]
        half_of = lambda ps: ps[:, :].bitcast(FP16)

        f_sw = sem("f_sw"); f_swh = sem("f_swh"); f_swl = sem("f_swl"); f_g = sem("f_g"); f_gh = sem("f_gh")
        f_gl = sem("f_gl"); f_c = sem("f_c"); f_idh = sem("f_idh")
        f_stat = sem("f_stat"); f_pow = sem("f_pow"); f_hn = sem("f_hn"); f_t = sem("f_t")
        f_rh = sem("f_rh"); f_rl = sem("f_rl")
        f_h = sem("f_h"); f_l = sem("f_l"); f_lg = sem("f_lg"); f_lgc = sem("f_lgc")
        f_sub = sem("f_sub"); f_ex = sem("f_ex"); f_sel = sem("f_sel"); f_cnt = sem("f_cnt"); f_slot = sem("f_slot")
        f_emap = sem("f_emap"); f_w = sem("f_w")
        f_gd = sem("f_gd"); f_ud = sem("f_ud"); f_si = sem("f_si"); f_hf = sem("f_hf"); f_hh = sem("f_hh")
        f_hl = sem("f_hl"); f_dn = sem("f_dn"); f_acc = sem("f_acc"); f_out = sem("f_out")
        f_dch = sem("f_dch"); f_pch = sem("f_pch")
        f_zero = sem("f_zero"); f_zs = sem("f_zs"); f_sc = sem("f_sc")
        r_x = [sem(f"r_x{i}") for i in range(3)]
        r_t = sem("r_t"); r_tx = sem("r_tx"); r_g = sem("r_g"); r_u = sem("r_u"); r_si = sem("r_si"); r_hf = sem("r_hf")
        r_ht = sem("r_ht"); r_hh = sem("r_hh"); r_hl = sem("r_hl"); r_y = sem("r_y"); r_ys = sem("r_ys")
        r_pad = sem("r_pad"); f_bt = sem("f_bt"); f_bh = sem("f_bh"); f_bl = sem("f_bl")
        r_st = [sem(f"r_st{i}") for i in range(3)]
        r_ga = [sem(f"r_ga{i}") for i in range(NGB)]
        r_add = sem("r_add")
        HB = NBLK // 2
        steps = [(blk, e) for blk in range(NBLK) for e in range(2)]
        half_steps = len(steps) // 2
        NC = len(IC)
        block = here.enter_context(nc.Block())

        @block.sync
        def _(eng):
            eng.dma_start(g32[:, :, :], gate_in.rearrange("(c p) e -> p c e", p=P)).then_inc(f_g, 16)
            eng.dma_start(consts[:, :], consts_in).then_inc(f_c, 16)
            for e in range(2):
                if e:
                    eng.wait_ge(f_swl, e)
                eng.dma_start(w32[:, :], ffn_in[NE + e, :, :]).then_inc(f_sw, 16)
            eng.wait_ge(f_zero, 1)
            eng.dma_start(sorted_rows.rearrange("(n p) w -> p n w", p=P),
                          xg[0][:, :].unsqueeze(1).broadcast_to([P, NTILE, 2 * D])).then_inc(f_zs, 16)

            def load(k):
                if k == 0:
                    eng.wait_ge(f_sc, 16 * 2 * NT)
                if k >= 3:
                    eng.wait_ge(r_t, k - 2)
                eng.dma_start(xg[k % 3][:, :], sorted_rows[k * P:(k + 1) * P, :]).then_inc(r_x[k % 3], 16)

            for k in range(NTILE):
                load(k)
            ov = out.rearrange("(n p) d -> p n d", p=P)
            for blk in range(NBLK):
                eng.wait_ge(r_add, BT * (blk + 1))
                eng.wait_ge(f_acc, 4 * (blk + 1))
                eng.dma_start(ov[:, BT * blk:BT * (blk + 1), :], xr[:, BT * blk:BT * (blk + 1), :]).then_inc(f_out, 16)
            eng.wait_ge(f_out, 16 * NBLK)

        @block.gpsimd
        def _(eng):
            eng.memset(xg[0][:, :], 0.0).then_inc(f_zero, 1)
            for k in range(NBLK):
                eng.wait_ge(f_stat, k + 1)
                if k >= 2:
                    eng.wait_ge(f_hn, k - 1)
                eng.tensor_scalar(ve[:, :], mv[k % 2][:, :, 1], EPS, None, ALU.add).then_inc(f_pch, 1)
                eng.wait_ge(f_pch, k + 1)
                eng.tensor_tensor(rstd[k % 2][:, :], ve[:, :], neghalf[:, :], ALU.pow).then_inc(f_pow, 1)
                eng.wait_ge(f_pow, k + 1)
                if k < 2:
                    eng.wait_ge(f_swh, k + 1)
                    eng.tensor_tensor(swl[:, k, :], w32[:, :], swh[:, k, :], ALU.subtract).then_inc(f_swl, 1)
            eng.wait_ge(f_zs, 16)
            eng.wait_ge(f_slot, 2)
            eng.wait_ge(f_rl, NBLK)
            eng.wait_ge(f_rh, NBLK)
            for n in range(NT):
                for j in range(2):
                    eng.indirect_dma_start(sorted_rows, bass.IndirectOffsetOnAxis(slot[:, j, n:n + 1], 0),
                                           hrow[:, n, :], None).then_inc(f_sc, 16)
            for k in range(NTILE):
                eng.wait_ge(r_ys, k + 1)
                eng.dma_start(sorted_out[k * P:(k + 1) * P, :], ys[k % 3][:, :]).then_inc(r_st[k % 3], 16)
            for i in range(3):
                eng.wait_ge(r_st[i], 16 * len(range(i, NTILE, 3)))
            for n in range(NT):
                if n >= NGB:
                    eng.wait_ge(r_add, n - NGB + 1)
                for j in range(2):
                    eng.indirect_dma_start(ya[n % NGB][:, j, :], None, sorted_out,
                                           bass.IndirectOffsetOnAxis(slot[:, j, n:n + 1], 0)).then_inc(r_ga[n % NGB], 16)

        @block.scalar
        def _(eng):
            eng.wait_ge(f_g, 16)
            eng.activation(gh[:, :, :], g32[:, :, :], ACT.Copy).then_inc(f_gh, 1)
            eng.activation(identh[:, :], ident[:, :], ACT.Copy).then_inc(f_idh, 1)
            for k in range(NBLK):
                if k < 2:
                    eng.wait_ge(f_sw, 16 * (k + 1))
                    eng.activation(swh[:, k, :], w32[:, :], ACT.Copy).then_inc(f_swh, 1)
                eng.wait_ge(f_hn, k + 1)
                eng.activation(hrow[:, BT * k:BT * (k + 1), 0:D], hn[:, :, :], ACT.Copy).then_inc(f_rh, 1)
                eng.wait_ge(f_t, k + 1)
                if k >= 2:
                    eng.wait_ge(f_lg, k - 1)
                eng.activation(hT[0][:, k % 2, :, :], half_of(ps_g[k % 2]).rearrange("p (c t) -> p c t", c=DC),
                               ACT.Copy).then_inc(f_h, 1)
            eng.wait_ge(f_sub, 1)
            eng.activation(ex[:, :, 0:NE], ex[:, :, 0:NE], ACT.Exp).then_inc(f_ex, 1)
            eng.activation(ex[:, :, NE:NG], lg[:, :, NE:NG], ACT.Exp, scale=-1.0).then_inc(f_ex, 1)

            def shared(n):
                for c, m in enumerate(IC):
                    k = NC * n + c
                    eng.wait_ge(f_gd, k + 1)
                    if k >= 2:
                        eng.wait_ge(f_hf, k - 1)
                    eng.activation(gs[k % 2][0:m, :], ps_g[k % 2][0:m, :], ACT.Silu).then_inc(f_si, 1)
                    eng.wait_ge(f_hf, k + 1)
                    if n >= 2:
                        eng.wait_ge(f_dn, 2 * (n - 1))
                    eng.activation(hh[n % 2][0:m, c, :], hf[k % 2][0:m, :], ACT.Copy).then_inc(f_hh, 1)

            def block_T(blk):
                eng.wait_ge(f_bt, blk + 1)
                eng.activation(hT[0][:, blk % 2, :, :], half_of(ps_d[2]).rearrange("p (c t) -> p c t", c=DC),
                               ACT.Copy).then_inc(f_bh, 1)

            block_T(0)
            for n in range(half_steps):
                shared(n)
                if n % 2 and n + 1 < half_steps:
                    block_T((n + 1) // 2)
            for k in range(NTILE + 2):
                if k < NTILE:
                    eng.wait_ge(r_g, k + 1)
                    if k >= 2:
                        eng.wait_ge(r_hf, k - 1)
                    else:
                        eng.wait_ge(f_hf, NC * half_steps)
                    eng.activation(gs[k % 2][:, 0:INTER], ps_g[k % 2][:, 0:INTER], ACT.Silu).then_inc(r_si, 1)
                if 0 <= k - 1 < NTILE:
                    eng.wait_ge(r_ht, k)
                    if k - 1 >= 2:
                        eng.wait_ge(r_y, k - 2)
                    else:
                        eng.wait_ge(f_dn, 2 * half_steps)
                    eng.activation(hh[(k - 1) % 2][:, :, 0:P],
                                   ps_d[1 + (k - 1) % 2][:, 0:3 * P].rearrange("p (c t) -> p c t", c=3),
                                   ACT.Copy).then_inc(r_hh, 1)
                if 0 <= k - 2 < NTILE:
                    eng.wait_ge(r_y, k - 1)
                    if k - 2 >= 3:
                        eng.wait_ge(r_st[(k - 2) % 3], 16 * ((k - 2) // 3))
                    eng.activation(ys[(k - 2) % 3][:, :], ps_d[3][:, 0:D], ACT.Copy).then_inc(r_ys, 1)
            block_T(HB)
            for n in range(half_steps, len(steps)):
                shared(n)
                if n % 2 and n + 1 < len(steps):
                    block_T((n + 1) // 2)

        @block.vector
        def _(eng):
            chain = [0]

            def link(ins):
                chain[0] += 1
                ins.then_inc(f_dch, 1)
                eng.wait_ge(f_dch, chain[0])

            eng.wait_ge(f_gh, 1)
            eng.tensor_tensor(gl[:, :, :], g32[:, :, :], gh[:, :, :], ALU.subtract).then_inc(f_gl, 1)

            def stats(k):
                for j in range(BT):
                    last = eng.bn_stats(st6[:, j, :], xr[:, BT * k + j, :])
                link(last)
                for j in range(BT):
                    last = eng.bn_aggr(mv[k % 2][:, j, :], st6[:, j, :])
                last.then_inc(f_stat, 1)
                eng.wait_ge(f_stat, k + 1)

            stats(0)
            for k in range(NBLK + 1):
                if k + 1 < NBLK:
                    stats(k + 1)
                if k < NBLK:
                    eng.wait_ge(f_pow, k + 1)
                    if k:
                        eng.wait_ge(f_rh, k)
                        eng.wait_ge(f_rl, k)
                    for j in range(BT):
                        last = eng.tensor_scalar(hn[:, j, :], xr[:, BT * k + j, :], mv[k % 2][:, j, 0:1],
                                                 rstd[k % 2][:, j:j + 1], ALU.subtract, ALU.mult)
                    last.then_inc(f_hn, 1)
                    eng.wait_ge(f_hn, k + 1)
                    eng.wait_ge(f_rh, k + 1)
                    eng.tensor_tensor(hrow[:, BT * k:BT * (k + 1), D:2 * D], hn[:, :, :],
                                      hrow[:, BT * k:BT * (k + 1), 0:D], ALU.subtract).then_inc(f_rl, 1)
                if k:
                    b = k - 1
                    eng.wait_ge(f_t, b + 1)
                    if b >= 2:
                        eng.wait_ge(f_lg, b - 1)
                    eng.tensor_copy(hT[1][:, b % 2, :, :],
                                    half_of(ps_u[b % 2]).rearrange("p (c t) -> p c t", c=DC)).then_inc(f_l, 1)
                    eng.wait_ge(f_lg, b + 1)
                    eng.tensor_copy(lg[:, BT * b:BT * b + BT, :],
                                    ps_d[b % 2][:, 0:16 * BT].rearrange("p (j c) -> p j c", c=16)[:, :, 0:NG])\
                        .then_inc(f_lgc, 1)
            eng.wait_ge(f_lgc, NBLK)
            link(eng.tensor_reduce(m8[:, :], lg[:, :, 0:NE], axis=AX.X, op=ALU.max))
            b8 = lambda a: a.unsqueeze(2).broadcast_to([P, NT, NE])
            eng.tensor_tensor(ex[:, :, 0:NE], lg[:, :, 0:NE], b8(m8[:, :]), ALU.subtract).then_inc(f_sub, 1)
            eng.wait_ge(f_ex, 2)
            link(eng.tensor_reduce(den[:, :], ex[:, :, 0:NE], axis=AX.X, op=ALU.add))
            link(eng.reciprocal(den[:, :], den[:, :]))
            sc = lg[:, :, 0:NE]
            link(eng.tensor_tensor(sc, ex[:, :, 0:NE], b8(den[:, :]), ALU.mult))
            for part in range(2):
                rows = slice(part * NT // 2, (part + 1) * NT // 2)
                c4 = cmp_.rearrange("p (n e j) -> p n e j", e=NE, j=NE)
                by_e = sc[:, rows, :].unsqueeze(3).broadcast_to([P, NT // 2, NE, NE])
                by_j = sc[:, rows, :].unsqueeze(2).broadcast_to([P, NT // 2, NE, NE])
                link(eng.tensor_tensor(c4, by_j, by_e, ALU.is_gt))
                link(eng.tensor_reduce(rank[:, rows, :], c4, axis=AX.X, op=ALU.add))
                link(eng.tensor_tensor(c4, by_j, by_e, ALU.is_equal))
                if part == 0:
                    link(eng.memset(sel[:, :, 0:1], 0.0))
                for e in range(1, NE):
                    last = eng.tensor_reduce(sel[:, rows, e:e + 1], c4[:, :, e, 0:e], axis=AX.X, op=ALU.add)
                link(last)
            link(eng.tensor_tensor(rank[:, :, :], rank[:, :, :], sel[:, :, :], ALU.add))
            eng.tensor_scalar(sel[:, :, :], rank[:, :, :], 2.0, None, ALU.is_lt).then_inc(f_sel, 1)
            for j in range(2):
                link(eng.tensor_scalar(chosen[j][:, :, :], rank[:, :, :], float(j), None, ALU.is_equal))
            for j in range(2):
                link(eng.tensor_tensor(ex[:, :, 0:NE], chosen[j][:, :, :], sc, ALU.mult))
                link(eng.tensor_reduce(wsel[:, j, :], ex[:, :, 0:NE], axis=AX.X, op=ALU.add))
            link(eng.tensor_scalar(ex[:, :, NE:NG], ex[:, :, NE:NG], 1.0, None, ALU.add))
            eng.reciprocal(ex[:, :, NE:NG], ex[:, :, NE:NG]).then_inc(f_w, 1)
            eng.wait_ge(f_w, 1)
            eng.wait_ge(f_cnt, 1)
            before = ps_d[2][:, 0:NT * NE].rearrange("p (n e) -> p n e", e=NE)
            total = ps_d[2][:, NT * NE:2 * NT * NE].rearrange("p (n e) -> p n e", e=NE)
            link(eng.tensor_copy(scan[0][:, :, :], total))
            cur, step = 0, 1
            while step < NT:
                eng.tensor_copy(scan[1 - cur][:, 0:step, :], scan[cur][:, 0:step, :])
                link(eng.tensor_tensor(scan[1 - cur][:, step:NT, :], scan[cur][:, step:NT, :],
                                       scan[cur][:, 0:NT - step, :], ALU.add))
                cur, step = 1 - cur, 2 * step
            c3 = cmp_[:, 0:NE * NT].rearrange("p (e n) -> p e n", e=NE)
            link(eng.tensor_tensor(c3, scan[cur][:, NT - 1, :].unsqueeze(2).broadcast_to([P, NE, NT]),
                                   tile_starts.unsqueeze(1).broadcast_to([P, NE, NT]), ALU.is_gt))
            link(eng.tensor_reduce(ntl[:, :], c3, axis=AX.X, op=ALU.add))
            link(eng.tensor_copy(ends[0][:, :], ntl[:, :]))
            at, step = 0, 1
            while step < NE:
                eng.tensor_copy(ends[1 - at][:, 0:step], ends[at][:, 0:step])
                link(eng.tensor_tensor(ends[1 - at][:, step:NE], ends[at][:, step:NE], ends[at][:, 0:NE - step], ALU.add))
                at, step = 1 - at, 2 * step
            ce = cmp_[0:1, 0:NTILE * (NE - 1)].rearrange("p (n e) -> p n e", e=NE - 1)
            link(eng.tensor_tensor(ce, ends[at][0:1, 0:NE - 1].unsqueeze(1).broadcast_to([1, NTILE, NE - 1]),
                                   tile_ids[0:1, :].unsqueeze(2).broadcast_to([1, NTILE, NE - 1]), ALU.is_le))
            link(eng.tensor_reduce(emapf[:, :], ce, axis=AX.X, op=ALU.add))
            eng.tensor_copy(emap[:, :], emapf[:, :]).then_inc(f_emap, 1)
            link(eng.tensor_tensor(ntl[:, :], ends[at][:, :], ntl[:, :], ALU.subtract))
            link(eng.tensor_scalar(ntl[:, :], ntl[:, :], float(P), None, ALU.mult))
            link(eng.tensor_tensor(scan[cur][:, :, :], total, scan[cur][:, :, :], ALU.subtract))
            link(eng.tensor_tensor(scan[cur][:, :, :], before, scan[cur][:, :, :], ALU.subtract))
            link(eng.tensor_tensor(scan[cur][:, :, :], scan[cur][:, :, :],
                                   ntl[:, :].unsqueeze(1).broadcast_to([P, NT, NE]), ALU.add))
            for j in range(2):
                link(eng.tensor_tensor(ex[:, :, 0:NE], chosen[j][:, :, :], scan[cur][:, :, :], ALU.mult))
                link(eng.tensor_reduce(slotf[:, j, :], ex[:, :, 0:NE], axis=AX.X, op=ALU.add))
                eng.tensor_copy(slot[:, j, :], slotf[:, j, :]).then_inc(f_slot, 1)

            def combine(n):
                blk, e = steps[n]
                for j in range(BT):
                    if j % 2 == 0:
                        eng.wait_ge(f_dn, 2 * n + j // 2 + 1)
                    if j == 0 and n:
                        eng.wait_ge(f_acc, 2 * n)
                    tile = xr[:, BT * blk + j, :]
                    src = ps_d[2 * (n % 2) + j // 2][:, (j % 2) * D:(j % 2 + 1) * D]
                    last = eng.scalar_tensor_tensor(tile, src, ex[:, BT * blk + j, NE:NG], tile, ALU.mult, ALU.add)
                    if j % 2:
                        last.then_inc(f_acc, 1)

            def shared(n):
                for c, m in enumerate(IC):
                    k = NC * n + c
                    eng.wait_ge(f_si, k + 1)
                    eng.wait_ge(f_ud, k + 1)
                    if k >= 2:
                        eng.wait_ge(f_hl, k - 1)
                    eng.tensor_tensor(hf[k % 2][0:m, :], ps_u[k % 2][0:m, :], gs[k % 2][0:m, :], ALU.mult).then_inc(f_hf, 1)
                    eng.wait_ge(f_hh, k + 1)
                    eng.tensor_tensor(hl[n % 2][0:m, c, :], hf[k % 2][0:m, :], hh[n % 2][0:m, c, :],
                                      ALU.subtract).then_inc(f_hl, 1)

            def gathered(n):
                eng.wait_ge(r_ga[n % NGB], 32 * (n // NGB + 1))
                tile = xr[:, n, :]
                if n >= BT * HB and n % BT == 0:
                    eng.wait_ge(f_acc, 4 * (n // BT + 1))
                link(eng.scalar_tensor_tensor(tile, ya[n % NGB][:, 0, :], wsel[:, 0, n:n + 1], tile, ALU.mult, ALU.add))
                eng.scalar_tensor_tensor(tile, ya[n % NGB][:, 1, :], wsel[:, 1, n:n + 1], tile, ALU.mult, ALU.add)\
                    .then_inc(r_add, 1)

            def block_T(blk):
                eng.wait_ge(f_bt, blk + 1)
                eng.tensor_copy(hT[1][:, blk % 2, :, :],
                                half_of(ps_d[3]).rearrange("p (c t) -> p c t", c=DC)).then_inc(f_bl, 1)

            block_T(0)
            for n in range(half_steps):
                shared(n)
                if n % 2 and n + 1 < half_steps:
                    block_T((n + 1) // 2)
                if n:
                    combine(n - 1)
            combine(half_steps - 1)
            for i in range(2):
                eng.memset(hf[i][:, INTER:3 * P], 0.0).then_inc(r_pad, 1)
            eng.wait_ge(r_pad, 2)

            def transposed(k):
                eng.wait_ge(r_t, k + 1)
                if k >= 2:
                    eng.wait_ge(r_u, k - 1)
                eng.tensor_copy(xgT[k % 2][:, :, :, :],
                                half_of(ps_d[0])[:, 0:4 * P].rearrange("p (l c t) -> p l c t", l=2, c=DC)).then_inc(r_tx, 1)

            transposed(0)
            for k in range(NTILE + 1):
                if k < NTILE:
                    eng.wait_ge(r_si, k + 1)
                    eng.wait_ge(r_u, k + 1)
                    if k >= 2:
                        eng.wait_ge(r_ht, k - 1)
                    eng.tensor_tensor(hf[k % 2][:, 0:INTER], ps_u[k % 2][:, 0:INTER], gs[k % 2][:, 0:INTER],
                                      ALU.mult).then_inc(r_hf, 1)
                if k:
                    b = k - 1
                    eng.wait_ge(r_hh, b + 1)
                    eng.tensor_tensor(hl[b % 2][:, :, 0:P], ps_d[1 + b % 2][:, 0:3 * P].rearrange("p (c t) -> p c t", c=3),
                                      hh[b % 2][:, :, 0:P], ALU.subtract).then_inc(r_hl, 1)
                if k + 1 < NTILE:
                    transposed(k + 1)
            done = 0
            block_T(HB)
            for n in range(half_steps, len(steps)):
                shared(n)
                if n % 2 and n + 1 < len(steps):
                    block_T((n + 1) // 2)
                if n > half_steps:
                    combine(n - 1)
                ready = BT * HB if n == half_steps else BT * (steps[n - 1][0] + steps[n - 1][1])
                for _ in range(4):
                    if done < ready:
                        gathered(done)
                        done += 1
            combine(len(steps) - 1)
            while done < NT:
                gathered(done)
                done += 1

        @block.tensor
        def _(eng):
            mm = eng.matmul
            eng.wait_ge(f_idh, 1)
            for k in range(NBLK + 1):
                if k < NBLK:
                    eng.wait_ge(f_rh, k + 1)
                    eng.wait_ge(f_rl, k + 1)
                    if k >= 2:
                        eng.wait_ge(f_h, k - 1)
                        eng.wait_ge(f_l, k - 1)
                    for ps, part in ((ps_g[k % 2], 0), (ps_u[k % 2], 1)):
                        for dc in range(DC):
                            for j in range(BT):
                                at = part * D + dc * P
                                last = eng.transpose(half_of(ps)[:, dc * BLK + j * P:dc * BLK + (j + 1) * P],
                                                     hrow[:, BT * k + j, at:at + P], identh[:, :])
                    last.then_inc(f_t, 1)
                if k:
                    b = k - 1
                    eng.wait_ge(f_h, b + 1)
                    eng.wait_ge(f_l, b + 1)
                    if b == 0:
                        eng.wait_ge(f_gl, 1)
                    if b >= 2:
                        eng.wait_ge(f_lgc, b - 1)
                    for j in range(BT):
                        for dc in range(DC):
                            for wl, xl in TERMS:
                                last = mm(ps_d[b % 2][:, 16 * j:16 * j + NG], hT[xl][:, b % 2, dc, j * P:(j + 1) * P],
                                          (gh, gl)[wl][:, dc, :], start=dc == 0 and (wl, xl) == (0, 0),
                                          stop=dc == DC - 1 and xl == 1)
                    last.then_inc(f_lg, 1)

            def up(n):
                blk, e = steps[n]
                eng.wait_ge(f_bh, blk + 1)
                eng.wait_ge(f_bl, blk + 1)
                for c, m in enumerate(IC):
                    k = NC * n + c
                    for w0, o, s_out in ((0, ps_g[k % 2], f_gd), (UP0, ps_u[k % 2], f_ud)):
                        if n == half_steps and c < 2:
                            eng.wait_ge(r_hf, NTILE)
                        elif k >= 2:
                            eng.wait_ge(f_si if w0 == 0 else f_hf, k - 1)
                        for dc in range(DC):
                            at = w0 + dc * INTER + P * c
                            for wl, xl in TERMS:
                                last = mm(o[0:m, :], (swh, swl)[wl][:, e, at:at + m], hT[xl][:, blk % 2, dc, :],
                                          start=dc == 0 and (wl, xl) == (0, 0), stop=dc == DC - 1 and xl == 1)
                        last.then_inc(s_out, 1)

            def down(n):
                blk, e = steps[n]
                eng.wait_ge(f_hl, NC * n + NC)
                if n >= 2:
                    eng.wait_ge(f_acc, 2 * (n - 1))
                if n == half_steps:
                    eng.wait_ge(r_ys, NTILE)
                    eng.wait_ge(r_hl, NTILE)
                for j in range(BT):
                    o = ps_d[2 * (n % 2) + j // 2][:, (j % 2) * D:(j % 2 + 1) * D]
                    for c, m in enumerate(IC):
                        at = DOWN0 + c * D
                        for wl, xl in TERMS:
                            last = mm(o, (hh, hl)[xl][n % 2][0:m, c, j * P:(j + 1) * P], (swh, swl)[wl][0:m, e, at:at + D],
                                      start=c == 0 and (wl, xl) == (0, 0), stop=c == NC - 1 and xl == 1)
                    if j % 2:
                        last.then_inc(f_dn, 1)

            eng.wait_ge(f_swl, 2)
            eng.wait_ge(f_lgc, NBLK)
            eng.wait_ge(f_c, 16)
            eng.wait_ge(f_sel, 1)
            for lhs, at in ((below, 0), (ones, NT * NE)):
                last = mm(ps_d[2][:, at:at + NT * NE], lhs, sel[:, :, :], start=True, stop=True)
            last.then_inc(f_cnt, 1)
            eng.wait_ge(f_slot, 2)
            def block_T(blk):
                n = 2 * blk
                if n == half_steps:
                    eng.wait_ge(r_ys, NTILE)
                    eng.wait_ge(r_hl, NTILE)
                elif n:
                    eng.wait_ge(f_acc, 2 * (n - 2))
                else:
                    eng.wait_ge(f_lgc, NBLK)
                for part in range(2):
                    for dc in range(DC):
                        for j in range(BT):
                            at = part * D + dc * P
                            last = eng.transpose(half_of(ps_d[2 + part])[:, dc * BLK + j * P:dc * BLK + (j + 1) * P],
                                                 hrow[:, BT * blk + j, at:at + P], identh[:, :])
                last.then_inc(f_bt, 1)

            block_T(0)
            for n in range(half_steps):
                up(n)
                if n % 2 and n + 1 < half_steps:
                    block_T((n + 1) // 2)
                if n:
                    down(n - 1)
            down(half_steps - 1)

            expert = [None]

            def rows_T(k):
                eng.wait_ge(r_x[k % 3], 16 * (k // 3 + 1))
                if k:
                    eng.wait_ge(r_tx, k)
                else:
                    eng.wait_ge(f_acc, 2 * half_steps)
                for part in range(2):
                    for dc in range(DC):
                        at = part * DC + dc
                        last = eng.transpose(half_of(ps_d[0])[:, at * P:(at + 1) * P],
                                             xg[k % 3][:, at * P:(at + 1) * P], identh[:, :])
                last.then_inc(r_t, 1)

            eng.wait_ge(f_emap, 1)
            experts = {}
            rows_T(0)
            for k in range(NTILE + 2):
                if k < NTILE:
                    experts[k] = e = eng.value_load(emap[0:1, k:k + 1], min_val=0, max_val=NE - 1)
                    eng.wait_ge(r_tx, k + 1)
                    for w0, o, s_out in ((0, ps_g[k % 2], r_g), (UP0, ps_u[k % 2], r_u)):
                        if k >= 2:
                            eng.wait_ge(r_si if w0 == 0 else r_hf, k - 1)
                        else:
                            eng.wait_ge(f_hf, NC * half_steps)
                        for dc in range(DC):
                            for wl, xl in TERMS:
                                last = mm(o[:, 0:INTER], xgT[k % 2][:, xl, dc, :],
                                          (fwh, fwl)[wl][:, bass.ds(e, 1), w0 + dc * INTER:w0 + (dc + 1) * INTER],
                                          start=dc == 0 and (wl, xl) == (0, 0), stop=dc == DC - 1 and xl == 1)
                        last.then_inc(s_out, 1)
                if 0 <= k - 1 < NTILE:
                    b = k - 1
                    eng.wait_ge(r_hf, b + 1)
                    if b >= 2:
                        eng.wait_ge(r_hl, b - 1)
                    for c in range(3):
                        last = eng.transpose(ps_d[1 + b % 2][:, c * P:(c + 1) * P], hf[b % 2][:, c * P:(c + 1) * P],
                                             ident[:, :])
                    last.then_inc(r_ht, 1)
                if k + 1 < NTILE:
                    rows_T(k + 1)
                if 0 <= k - 2 < NTILE:
                    b = k - 2
                    eng.wait_ge(r_hl, b + 1)
                    if b:
                        eng.wait_ge(r_ys, b)
                    e = experts.pop(b)
                    for c in range(3):
                        at = DOWN0 + c * D
                        for wl, xl in TERMS:
                            last = mm(ps_d[3][:, 0:D], (hh, hl)[xl][b % 2][:, c, 0:P],
                                      (fwh, fwl)[wl][:, bass.ds(e, 1), at:at + D],
                                      start=c == 0 and (wl, xl) == (0, 0), stop=c == 2 and xl == 1)
                    last.then_inc(r_y, 1)
            block_T(HB)
            for n in range(half_steps, len(steps)):
                up(n)
                if n % 2 and n + 1 < len(steps):
                    block_T((n + 1) // 2)
                if n > half_steps:
                    down(n - 1)
            down(len(steps) - 1)


def kernel(x, ctx_1024, mask_1x1xSxS2_ik0, L0_xattn_Wq_w, L0_xattn_Wq_b, L0_xattn_Wk_w, L0_xattn_Wk_b,
           L0_xattn_Wv_w, L0_xattn_Wv_b, L0_xattn_Wo_w, L0_xattn_Wo_b, L0_ffn_gate_w, L0_ffn_experts_gate_up,
           L0_ffn_experts_down, L0_ffn_shared_gate_w, L0_ffn_shared_up_w, L0_ffn_shared_down_w,
           L0_ffn_shared_expert_gate_w):
    import numpy as np
    import concourse.bacc as bacc
    from concourse.bass_utils import run_bass_kernel_spmd

    a = np.asarray
    halves = np.concatenate([np.arange(h * DK, (h + 1) * DK) for hh in range(2) for h in range(hh, H, 2)])

    def rows(w):
        return a(w).reshape(DC, P, -1).transpose(1, 0, 2).reshape(P, -1)

    w_in = np.concatenate([rows(a(L0_xattn_Wq_w)[:, halves]), rows(a(L0_xattn_Wk_w)[:, halves]), rows(L0_xattn_Wv_w)], 1)
    bias = np.concatenate([a(L0_xattn_Wq_b)[halves], a(L0_xattn_Wk_b)[halves], a(L0_xattn_Wv_b), a(L0_xattn_Wo_b)])[None]
    w_o = np.zeros((HG, 4, 32, D), np.float32)
    w_o[:, :, 0:DK] = a(L0_xattn_Wo_w).reshape(HG, 4, DK, D)
    w_o = w_o.reshape(HG, P, D).transpose(1, 0, 2).reshape(P, HG * D)
    gate = np.concatenate([a(L0_ffn_experts_gate_up)[:, :INTER], a(L0_ffn_shared_gate_w).reshape(2, INTER, D)])
    up = np.concatenate([a(L0_ffn_experts_gate_up)[:, INTER:], a(L0_ffn_shared_up_w).reshape(2, INTER, D)])
    down = np.concatenate([a(L0_ffn_experts_down), a(L0_ffn_shared_down_w).reshape(D, 2, INTER).transpose(1, 0, 2)])
    ffn_w = np.zeros((NX, P, FW), np.float32)
    for e in range(NX):
        ffn_w[e, :, 0:UP0] = rows(gate[e].T)
        ffn_w[e, :, UP0:DOWN0] = rows(up[e].T)
        padded = np.zeros((len(IC) * P, D), np.float32)
        padded[0:INTER] = down[e].T
        ffn_w[e, :, DOWN0:] = padded.reshape(len(IC), P, D).transpose(1, 0, 2).reshape(P, -1)
    router = np.concatenate([a(L0_ffn_gate_w), a(L0_ffn_shared_expert_gate_w)]).T
    consts = np.concatenate([np.triu(np.ones((P, P)), 1), np.ones((P, P)),
                             np.broadcast_to(np.arange(NT) * P, (P, NT)), np.broadcast_to(np.arange(NTILE), (P, NTILE))],
                            1).astype(np.float32)
    arrays = {
        "x_dram": a(x).reshape(TOK, D), "ctx_dram": a(ctx_1024).reshape(TOK, D),
        "mask_dram": a(mask_1x1xSxS2_ik0).reshape(SEQ, SEQ), "w_in_dram": w_in, "bias_dram": bias, "w_o_dram": w_o,
        "ffn_dram": ffn_w, "router_dram": router, "ident_dram": np.eye(P, dtype=np.float32), "consts_dram": consts,
    }
    arrays = {k: np.ascontiguousarray(v) for k, v in arrays.items()}
    nc = bacc.Bacc("TRN2", target_bir_lowering=False, num_devices=1)
    d = {k: nc.dram_tensor(k, v.shape, mybir.dt.from_np(v.dtype), kind="ExternalInput").ap() for k, v in arrays.items()}
    out = nc.dram_tensor("out_dram", (TOK, D), FP32, kind="ExternalOutput").ap()
    qk_scratch = nc.dram_tensor("qk_scratch", (NB, 2, 2, 2, P, SEQ), FP16, kind="Internal").ap()
    m_scratch = nc.dram_tensor("m_scratch", (NB, H, SEQ), FP16, kind="Internal").ap()
    den_scratch = nc.dram_tensor("den_scratch", (NB, 2, H * SEQ), FP32, kind="Internal").ap()
    sorted_rows = nc.dram_tensor("sorted_rows", (NTILE * P, 2 * D), FP16, kind="Internal").ap()
    sorted_out = nc.dram_tensor("sorted_out", (NTILE * P, D), FP32, kind="Internal").ap()
    block_kernel(nc, d["x_dram"], d["ctx_dram"], d["mask_dram"], d["w_in_dram"], d["bias_dram"], d["w_o_dram"],
                 d["ffn_dram"], d["router_dram"], d["ident_dram"], d["consts_dram"], out, qk_scratch, m_scratch, den_scratch,
                 sorted_rows, sorted_out)
    r = run_bass_kernel_spmd(nc, [arrays], core_ids=[0])
    return r.results[0]["out_dram"].reshape(NB, SEQ, D)
```

```python
import concourse.bass as bass
from concourse import mybir
from contextlib import ExitStack

FP32 = mybir.dt.float32
FP16 = mybir.dt.float16
BF16 = mybir.dt.bfloat16
INT32 = mybir.dt.int32
UINT32 = mybir.dt.uint32
ALU = mybir.AluOpType
ACT = mybir.ActivationFunctionType
AX = mybir.AxisListType

P = 128
D = 256
NB = 16
SEQ = 256
TOK = NB * SEQ
NT = TOK // P
TT = SEQ // P
DC = D // P
H = 16
DK = D // H
NP = H // 2
HG = 4
NE = 8
INTER = 352
NX = NE + 2
IC = [128, 128, 96]
FW = 2 * DC * INTER + len(IC) * D
UP0 = DC * INTER
DOWN0 = 2 * DC * INTER
ROWS = 48
EPS = 1e-5
MASKED = 2.0 ** 30
SCALE = DK ** -0.5
BLK = 512
NBLK = TOK // BLK
BT = BLK // P
TOPK = 2
NTILE = TOPK * TOK // P + NE - 1

NG = NE + 1

TERMS = ((0, 0), (1, 0), (0, 1))


class Routing:
    pass


def block_kernel(nc, x, ctx, mask, w_in, bias_in, w_o, ffn_in, gate_in, ident_in, consts_in, out, qk_scratch, m_scratch,
                 den_scratch, hrow_dram, hT_dram, sw_dram, sorted_rows, sorted_out):
    with ExitStack() as life:
        sb = lambda stack, n, s, t: stack.enter_context(nc.sbuf_tensor(n, s, t))
        sem = lambda n: life.enter_context(nc.semaphore(n))

        xr = sb(life, "xr", [P, NT, D], FP32)
        fwh = sb(life, "fwh", [P, NE, FW], FP16)
        fwl = sb(life, "fwl", [P, NE, FW], FP16)
        ident = sb(life, "ident", [P, P], FP32)
        moe = Routing()
        moe.identh = sb(life, "identh", [P, P], FP16)
        moe.neghalf = sb(life, "neghalf", [P, TT], FP32)
        moe.gh = sb(life, "gh", [P, DC, NG], FP16)
        moe.gl = sb(life, "gl", [P, DC, NG], FP16)
        moe.lg = sb(life, "lg", [P, TT, NG], FP32)
        moe.ex = sb(life, "ex", [P, TT, NG], FP32)
        moe.top = sb(life, "top", [P, TT], FP32)
        moe.tot = sb(life, "tot", [P, TT], FP32)
        moe.cmp_ = sb(life, "cmp", [P, TT, NE, NE], FP32)
        moe.rank = sb(life, "rank", [P, TT, NE], FP32)
        moe.sel = sb(life, "sel", [P, NT, NE], FP32)
        moe.chosen = [sb(life, f"chosen{i}", [P, NT, NE], FP32) for i in range(TOPK)]
        moe.wsel = sb(life, "wsel", [P, TOPK, NT], FP32)
        moe.wshared = sb(life, "wshared", [P, NT], FP32)
        moe.s_ex = sem("s_ex")
        attention(nc, sb, sem, xr, fwh, fwl, ident, moe, x, ctx, mask, w_in, bias_in, w_o, ffn_in, gate_in, ident_in,
                  qk_scratch, m_scratch, den_scratch, hrow_dram, hT_dram, sw_dram, sorted_rows)
        ffn(nc, sb, sem, xr, fwh, fwl, ident, moe, consts_in, hrow_dram, hT_dram, sw_dram, sorted_rows, sorted_out, out)


def attention(nc, sb, sem, xr, fwh, fwl, ident, moe, x, ctx, mask, w_in, bias_in, w_o, ffn_in, gate_in, ident_in,
              qk_scratch, m_scratch, den_scratch, hrow_dram, hT_dram, sw_dram, sorted_rows):
    identh, neghalf, gh, gl = moe.identh, moe.neghalf, moe.gh, moe.gl
    with ExitStack() as here:
        t = lambda n, s, d: sb(here, n, s, d)
        pt = lambda n, s: here.enter_context(nc.psum_tensor(n, s, FP32))
        WA = 3 * DC * D + HG * D
        STAGE = FW // 2
        aw32 = t("aw32", [P, STAGE], FP32)
        awh = t("awh", [P, WA], FP16)
        awl = t("awl", [P, WA], FP16)
        bhl = t("bhl", [33, 4 * D], FP16)
        ones33 = t("ones33", [33, SEQ], FP16)
        any33 = t("any33", [33, SEQ], FP16)
        identb = t("identb", [P, P], BF16)
        anyq = t("anyq", [P, TT], FP32)
        mb_q = t("mb_q", [P, TT, SEQ], BF16)
        mb_k = t("mb_k", [P, TT, SEQ], BF16)
        c32 = t("c32", [P, TT, D], FP32)
        xn = t("xn", [P, TT, D], FP32)
        st6 = t("st6", [P, TT, 6], FP32)
        mv = [t(f"mv{i}", [P, TT, 2], FP32) for i in range(2)]
        ve = [t(f"ve{i}", [P, TT], FP32) for i in range(2)]
        rstd = [t(f"rstd{i}", [P, TT], FP32) for i in range(2)]
        rsa = t("rsa", [P, TT], FP32)
        xT = [t("xTh", [P, DC * SEQ], FP16), t("xTl", [P, DC * SEQ], FP16)]
        cT = [t("cTh", [P, DC * SEQ], FP16), t("cTl", [P, DC * SEQ], FP16)]
        qhl = t("qhl", [P, 2, 2, SEQ], FP16)
        khl = t("khl", [P, 2, 2, SEQ], FP16)
        qs = [t(f"qs{i}", [P, NP, SEQ], FP16) for i in range(3)]
        ks = [t(f"ks{i}", [P, NP, SEQ], FP16) for i in range(3)]
        vx = [t(f"vx{i}", [P, TT, H, 32], FP32) for i in range(3)]
        mx = [t(f"mx{i}", [P, TT, H], FP32) for i in range(2)]
        nm = t("nm", [H, SEQ], FP16)
        expo = [t(f"p{i}", [P, 4, SEQ], FP32) for i in range(4)]
        mi = expo[0][:, 0:TT, :].bitcast(INT32)
        nz = expo[1][:, 0:TT, :]
        wv32 = expo[0][:, 2:4, :].rearrange("p a b -> p (a b)")
        b32 = expo[2][0:33, :, :].rearrange("p a b -> p (a b)")
        bh2 = expo[3][0:33, 0:2, :].rearrange("p a b -> p (a b)").bitcast(FP16)
        o32 = t("o32", [P, HG * SEQ], FP32)
        den = t("sums", [P, H * SEQ // P], FP32)
        rb = t("rb", [P, HG * SEQ], FP32)
        onh = t("onh", [P, HG, SEQ], FP16)
        onl = t("onl", [P, HG, SEQ], FP16)

        f6 = t("f6", [P, TT, 6], FP32)
        fmv = [t(f"fmv{i}", [P, TT, 2], FP32) for i in range(2)]
        fve = t("fve", [P, TT], FP32)
        frstd = [t(f"frstd{i}", [P, TT], FP32) for i in range(2)]
        hn = xn
        hrow = t("hrow", [P, TT, 2 * D], FP16)
        hT = t("hT", [P, 2, DC, SEQ], FP16)
        g32 = t("g32", [P, DC, NG], FP32)
        zeros = t("zeros", [P, D], FP16)

        ps_st = [pt(f"ps_st{i}", [P, 4 * SEQ]) for i in range(2)]
        ps_o = pt("ps_o", [P, HG * SEQ])
        ps_m = [pt(f"ps_m{i}", [P, 2 * SEQ]) for i in range(2)]

        WQ, WK, WV, WO = 0, DC * D, 2 * DC * D, 3 * DC * D

        s_x = [sem(f"s_x{i}") for i in range(8)]
        s_c = sem("s_c")
        s_aw = sem("s_aw"); s_bias = sem("s_bias"); s_mi = sem("s_mi"); s_id = sem("s_id")
        s_fw = sem("s_fw"); s_sw = sem("s_sw"); s_fwd = sem("s_fwd"); s_wo = sem("s_wo")
        s_awh = sem("s_awh"); s_awl = sem("s_awl")
        s_const = sem("s_const"); s_ones = sem("s_ones")
        s_wv = sem("s_wv")
        s_bh = sem("s_bh"); s_bl = sem("s_bl")
        s_idb = sem("s_idb")
        s_mbf = sem("s_mbf"); s_mbq = sem("s_mbq"); s_mbT = sem("s_mbT"); s_mbk = sem("s_mbk")
        s_anyb = sem("s_anyb"); s_any33 = sem("s_any33")
        s_stat = sem("s_stat"); s_pow = sem("s_pow"); s_xn = sem("s_xn")
        s_xt = sem("s_xt"); s_ct = sem("s_ct")
        s_xh = sem("s_xh"); s_xl = sem("s_xl"); s_ch = sem("s_ch"); s_cl = sem("s_cl")
        s_q = sem("s_q"); s_k = sem("s_k"); s_v = sem("s_v")
        s_qh = sem("s_qh"); s_ql = sem("s_ql"); s_kh = sem("s_kh"); s_kl = sem("s_kl"); s_vx = sem("s_vx")
        s_qw = sem("s_qw"); s_kw = sem("s_kw")
        s_qk = [sem(f"s_qk{i}") for i in range(3)]
        s_s = sem("s_s"); s_mx = sem("s_mx"); s_mt = sem("s_mt"); s_nm = sem("s_nm"); s_mw = sem("s_mw")
        s_mr = [sem(f"s_mr{i}") for i in range(3)]
        s_st = sem("s_st"); s_e = sem("s_e"); s_pv = sem("s_pv")
        s_oc = sem("s_oc"); s_dw = sem("s_dw"); s_dr = sem("s_dr")
        s_rc = sem("s_rc"); s_rw = sem("s_rw"); s_rr = sem("s_rr")
        s_n = sem("s_n"); s_onh = sem("s_onh"); s_onl = sem("s_onl")
        s_o = sem("s_o"); s_res = sem("s_res")
        s_free = [sem(f"s_free{i}") for i in range(2)]
        s_dch = sem("s_dch"); s_pch = sem("s_pch")

        s_g = sem("s_g"); s_gh = sem("s_gh"); s_gl = sem("s_gl")
        s_idh = sem("s_idh"); s_zero = sem("s_zero"); s_zs = sem("s_zs")
        s_st2 = sem("s_st2"); s_pow2 = sem("s_pow2"); s_hn = sem("s_hn"); s_rh = sem("s_rh"); s_rl = sem("s_rl")
        s_hw = sem("s_hw"); s_ht = sem("s_ht"); s_th = sem("s_th"); s_tw = sem("s_tw"); s_rt = sem("s_rt")
        s_sub = sem("s_sub")

        order = ["mask", "any"]
        slots = {0: ("mt", "rt"), 1: ("xt",), 2: ("ct",), 3: ("q",), 4: ("k",), 5: ("v",), 6: ("ht",), 7: ("o",)}
        lag = {"mt": 2, "xt": 0, "ct": 0, "q": 0, "k": 0, "v": 0, "o": 4, "ht": 5, "rt": 6}
        ITER = NB + 5

        LATE = 2
        EARLY = NB - 1
        LAG_S, LAG_T, LAG_V = 8, 20, 21

        def uses(i, u):
            last = lambda kind: EARLY if kind in ("ht", "rt") else NB
            return [(kind, i - lag[kind]) for kind in slots[u] if 0 <= i - lag[kind] < last(kind)]

        for i in range(ITER):
            for u in range(8):
                order += uses(i, u)
        use = {k: n for n, k in enumerate(order)}
        bank = lambda k: ps_m[use[k] % 2]

        def wait_bank(eng, k):
            if use[k] // 2:
                eng.wait_ge(s_free[use[k] % 2], use[k] // 2)

        def units(i, u):
            g = 8 * i + u
            found = []
            for late in (LAG_S, LAG_T, LAG_V):
                found.append(divmod(g - late, 8) if 0 <= g - late < 8 * NB else None)
            return found

        pair, before = {}, {}
        held = [None, None]
        for i in range(ITER):
            for u in range(8):
                s, st, _ = units(i, u)
                for kind, unit, alone, own in (("S", s, 8 * i + u < LAG_T, 0), ("T", st, 8 * i + u >= 8 * NB + LAG_S, 1)):
                    if unit:
                        k = (kind, 8 * unit[0] + unit[1])
                        pair[k] = k[1] % 2 if alone else own
                        before[k] = held[pair[k]]
                        held[pair[k]] = k

        def wait_pair(eng, k):
            if before[k]:
                eng.wait_ge(s_mx if before[k][0] == "S" else s_e, before[k][1] + 1)

        halves = [(e, part) for e in [NE, NE + 1, *range(NE)] for part in range(2)]
        EXTRA, EXTRA_FROM = len(halves) - NB, 5
        due, j = {}, 0
        for i in range(ITER):
            due[i] = ([], [])
            if 1 <= i <= NB:
                due[i] = ([j], [j + 1] if EXTRA_FROM <= i < EXTRA_FROM + EXTRA else [])
                j += len(due[i][0]) + len(due[i][1])
        place = lambda e: e if e < NE else e - (NX - NE)

        def dividing(i, u):
            g = 8 * i + u - LAG_V - 7
            return [(b, g - 8 * b) for b in range(max(0, g // 8 - 1), min(NB, g // 8 + 1)) if 0 <= g - 8 * b <= 7]

        free = lambda k: s_free[use[k] % 2]

        block = here.enter_context(nc.Block())

        @block.sync
        def _(eng):
            xv = x.rearrange("(n p) d -> p n d", p=P)
            cv = ctx.rearrange("(b t p) d -> b p t d", p=P, t=TT)

            def load_c(b):
                if b:
                    eng.wait_ge(s_ct, b)
                eng.dma_start(c32[:, :, :], cv[b, :, :, :]).then_inc(s_c, 16)

            eng.dma_start(xr[:, 0:4, :], xv[:, 0:4, :]).then_inc(s_x[0], 16)
            eng.dma_start(mi[:, :, :], mask.rearrange("(t p) k -> p t k", p=P)).then_inc(s_mi, 16)
            eng.dma_start(ident[:, :], ident_in).then_inc(s_id, 16)
            eng.dma_start(aw32[:, 0:WV], w_in[:, 0:WV]).then_inc(s_aw, 16)
            load_c(0)
            eng.dma_start(b32[0:1, :], bias_in).then_inc(s_bias, 16)
            eng.dma_start(b32[32:33, :], bias_in).then_inc(s_bias, 16)
            eng.dma_start(wv32[:, :], w_in[:, WV:WO]).then_inc(s_wv, 16)
            eng.dma_start(g32[:, :, :], gate_in.rearrange("(c p) e -> p c e", p=P)).then_inc(s_g, 16)
            for n in range(1, 8):
                eng.dma_start(xr[:, 4 * n:4 * n + 4, :], xv[:, 4 * n:4 * n + 4, :]).then_inc(s_x[n], 16)
            eng.wait_ge(s_awl, 1)
            eng.dma_start(aw32[:, 0:HG * D], w_o).then_inc(s_wo, 16)

            def load_half(j):
                eng.wait_ge(s_awl, 3 + j)
                if j and halves[j - 1][0] >= NE:
                    e, part = halves[j - 1]
                    cols = slice(part * STAGE, (part + 1) * STAGE)
                    for n, w in enumerate((fwh, fwl)):
                        eng.dma_start(sw_dram[e - NE, n, :, cols], w[:, place(e), cols]).then_inc(s_sw, 16)
                e, part = halves[j]
                eng.dma_start(aw32[:, :], ffn_in[e, :, part * STAGE:(part + 1) * STAGE]).then_inc(s_fw, 16)

            for i in range(ITER):
                for j in due[i][0]:
                    load_half(j)
                if 0 < i <= 2 * NE:
                    if i == 1:
                        eng.wait_ge(s_zero, 1)
                    first, last = ((i - 1) * NTILE) // (2 * NE), (i * NTILE) // (2 * NE)
                    eng.dma_start(sorted_rows[first * P:last * P, :].rearrange("(p n) (l w) -> p (n l) w", p=P, l=2),
                                  zeros[:, :].unsqueeze(1).broadcast_to([P, 2 * (last - first), D])).then_inc(s_zs, 16)
                b = i - 2
                if 0 <= b < NB:
                    eng.wait_ge(s_nm, b + 1)
                    eng.dma_start(m_scratch[b, :, :], nm[:, :]).then_inc(s_mw, 16)
                    eng.wait_ge(s_mw, 16 * (b + 1))
                    mv_ = m_scratch[b, :, :].rearrange("(h p) t -> h p t", h=2)
                    for hh in range(2):
                        eng.dma_start(qs[b % 3][64 * hh + ROWS:64 * hh + ROWS + 1, :, :],
                                      mv_[hh:hh + 1, :, :]).then_inc(s_mr[b % 3], 16)
                if i < NB:
                    if i + 1 < NB:
                        load_c(i + 1)
                    for what, hl, s_lo, s_w in ((0, qhl, s_ql, s_qw), (1, khl, s_kl, s_kw)):
                        eng.wait_ge(s_lo, i + 1)
                        eng.dma_start(qk_scratch[i, what, :, :, :, :].rearrange("l h r t -> r l h t"),
                                      hl[:, :, :, :]).then_inc(s_w, 16)
                    if i == 0:
                        eng.wait_ge(s_const, 8)
                    if i >= 3:
                        eng.wait_ge(s_st, 8 * (i - 2))
                    for what, dst, s_w, parts in ((0, qs[i % 3], s_qw, (0, 0, 1)), (1, ks[i % 3], s_kw, (0, 1, 0))):
                        eng.wait_ge(s_w, 16 * (i + 1))
                        for hh in range(2):
                            for n, part in enumerate(parts):
                                row = 64 * hh + 16 * n
                                src = qk_scratch[i, what, part, hh, :, :].rearrange("(p d) t -> d p t", d=DK)
                                eng.dma_start(dst[row:row + DK, :, :], src).then_inc(s_qk[i % 3], 16)
                for j in due[i][1]:
                    load_half(j)

        @block.gpsimd
        def _(eng):
            chain = [0]

            def link(ins):
                chain[0] += 1
                ins.then_inc(s_pch, 1)
                eng.wait_ge(s_pch, chain[0])

            eng.memset(neghalf[:, :], -0.5).then_inc(s_const, 1)
            eng.wait_ge(s_const, 1)

            def power(b):
                eng.wait_ge(s_stat, b + 1)
                if b >= 2:
                    eng.wait_ge(s_xn, b - 1)
                link(eng.tensor_scalar(ve[b % 2][:, :], mv[b % 2][:, :, 1], EPS, None, ALU.add))
                eng.tensor_tensor(rstd[b % 2][:, :], ve[b % 2][:, :], neghalf[:, 0:TT], ALU.pow).then_inc(s_pow, 1)

            for i in range(2):
                eng.memset(ks[i][:, :, :], 1.0).then_inc(s_const, 1)
                eng.memset(vx[i][:, :, :, :], 1.0).then_inc(s_const, 1)
            eng.memset(zeros[:, :], 0.0).then_inc(s_zero, 1)
            power(0)
            eng.wait_ge(s_awh, 1)
            eng.tensor_tensor(awl[:, 0:WV], aw32[:, 0:WV], awh[:, 0:WV], ALU.subtract).then_inc(s_awl, 1)
            power(1)
            eng.memset(rb[:, :], 0.0).then_inc(s_const, 1)
            eng.memset(ks[2][:, :, :], 1.0).then_inc(s_const, 1)
            eng.memset(vx[2][:, :, :, :], 1.0).then_inc(s_const, 1)
            eng.wait_ge(s_const, 8)
            eng.wait_ge(s_awh, 2)
            eng.tensor_tensor(awl[:, WV:WO], wv32[:, :], awh[:, WV:WO], ALU.subtract).then_inc(s_awl, 1)
            eng.wait_ge(s_wo, 16)
            link(eng.tensor_copy(awh[:, WO:WA], aw32[:, 0:HG * D]))
            eng.tensor_tensor(awl[:, WO:WA], aw32[:, 0:HG * D], awh[:, WO:WA], ALU.subtract).then_inc(s_awl, 1)

            def split_half(j):
                e, part = halves[j]
                hi, lo = (w[:, place(e), part * STAGE:(part + 1) * STAGE] for w in (fwh, fwl))
                eng.wait_ge(s_fw, 16 * (j + 1))
                if e == place(NE):
                    eng.wait_ge(s_sw, 16 * 8)
                eng.tensor_copy(hi, aw32[:, :]).then_inc(s_fwd, 1)
                eng.wait_ge(s_fwd, j + 1)
                eng.tensor_tensor(lo, aw32[:, :], hi, ALU.subtract).then_inc(s_awl, 1)

            for i in range(ITER):
                if 2 <= i + 1 < NB:
                    power(i + 1)
                b = i - 5
                if 0 <= b < EARLY:
                    eng.wait_ge(s_st2, b + 1)
                    if b >= 2:
                        eng.wait_ge(s_hn, b - 1)
                    link(eng.tensor_scalar(fve[:, :], fmv[b % 2][:, :, 1], EPS, None, ALU.add))
                    eng.tensor_tensor(frstd[b % 2][:, :], fve[:, :], neghalf[:, :], ALU.pow).then_inc(s_pow2, 1)
                b = i - 4
                if 0 <= b < NB - LATE:
                    eng.wait_ge(s_rr, 64 * (b + 1))
                    eng.wait_ge(s_oc, b + 1)
                    eng.tensor_tensor(o32[:, :], o32[:, :], rb[:, :], ALU.mult).then_inc(s_n, 1)
                    eng.wait_ge(s_onh, b + 1)
                    eng.tensor_tensor(onl[:, :, :], o32[:, :].rearrange("p (g t) -> p g t", g=HG), onh[:, :, :],
                                      ALU.subtract).then_inc(s_onl, 1)
                for part in due[i]:
                    for j in part:
                        split_half(j)

        @block.scalar
        def _(eng):
            eng.wait_ge(s_aw, 16)
            eng.activation(awh[:, 0:WV], aw32[:, 0:WV], ACT.Copy).then_inc(s_awh, 1)
            eng.wait_ge(s_bias, 32)
            eng.wait_ge(s_ones, 1)
            eng.activation(bhl[0:1, :], b32[0:1, :], ACT.Copy).then_inc(s_bh, 1)
            eng.activation(bh2[32:33, :], b32[32:33, :], ACT.Copy).then_inc(s_bh, 1)
            eng.wait_ge(s_id, 16)
            eng.activation(identb[:, :], ident[:, :], ACT.Copy).then_inc(s_idb, 1)
            eng.activation(identh[:, :], ident[:, :], ACT.Copy).then_inc(s_idh, 1)
            eng.wait_ge(s_mbT, 1)
            eng.activation(mb_k[:, :, :], bank("mask")[:, :].rearrange("p (t q) -> p t q", t=TT), ACT.Copy).then_inc(s_mbk, 1)
            eng.wait_ge(s_anyb, 1)
            eng.activation(any33[:, :], bank("any")[0:33, 0:SEQ], ACT.Copy).then_inc(s_any33, 1)
            eng.wait_ge(s_mbk, 1)
            eng.wait_ge(s_any33, 1)
            eng.nop().then_inc(s_free[0], 1)
            eng.nop().then_inc(s_free[1], 1)
            for i in range(ITER):
                for u in range(8):
                    if i == 0 and u == 3:
                        eng.wait_ge(s_wv, 16)
                        eng.activation(awh[:, WV:WO], wv32[:, :], ACT.Copy).then_inc(s_awh, 1)
                        eng.wait_ge(s_g, 16)
                        eng.activation(gh[:, :, :], g32[:, :, :], ACT.Copy).then_inc(s_gh, 1)
                    for kind, b in uses(i, u):
                        if kind == "ht":
                            eng.wait_ge(s_ht, b + 1)
                            if b:
                                eng.wait_ge(s_rt, b)
                                eng.wait_ge(s_tw, 16 * b)
                            eng.activation(hT[:, :, :, :].rearrange("p l c t -> p (l c t)"),
                                           bank((kind, b))[:, :].bitcast(FP16), ACT.Copy).then_inc(s_th, 1)
                            eng.wait_ge(s_th, b + 1)
                            eng.nop().then_inc(free((kind, b)), 1)
                        elif kind == "mt":
                            eng.wait_ge(s_mt, b + 1)
                            if b:
                                eng.wait_ge(s_mw, 16 * b)
                            eng.activation(nm[:, :], bank((kind, b))[0:H, 0:SEQ], ACT.Copy, scale=-1.0).then_inc(s_nm, 1)
                            eng.wait_ge(s_nm, b + 1)
                            eng.nop().then_inc(free((kind, b)), 1)
                        elif kind in ("xt", "ct"):
                            s_in, dst, s_out, s_used = (s_xt, xT[0], s_xh, s_q) if kind == "xt" else (s_ct, cT[0], s_ch, s_v)
                            eng.wait_ge(s_in, b + 1)
                            if b:
                                eng.wait_ge(s_used, b)
                            eng.activation(dst[:, :], bank((kind, b))[:, :], ACT.Copy).then_inc(s_out, 1)
                        elif kind in ("q", "k"):
                            s_in, dst, s_out, s_used = (s_q, qhl, s_qh, s_qw) if kind == "q" else (s_k, khl, s_kh, s_kw)
                            eng.wait_ge(s_in, b + 1)
                            if b:
                                eng.wait_ge(s_used, 16 * b)
                            eng.activation(dst[:, 0, :, :], bank((kind, b))[:, :].rearrange("p (h t) -> p h t", h=2),
                                           ACT.Copy).then_inc(s_out, 1)
                        elif kind == "v":
                            eng.wait_ge(s_v, b + 1)
                            if b == 0:
                                eng.wait_ge(s_const, 8)
                            if b >= 3:
                                eng.wait_ge(s_pv, 4 * (b - 2))
                            for tt in range(TT):
                                last = eng.activation(vx[b % 3][:, tt, :, 0:DK],
                                                      bank((kind, b))[:, tt * D:(tt + 1) * D].rearrange("p (h d) -> p h d", h=H),
                                                      ACT.Copy)
                                last.then_inc(s_vx, 1)
                            eng.wait_ge(s_vx, 2 * b + 2)
                            eng.nop().then_inc(free((kind, b)), 1)
                    _, st, pv = units(i, u)
                    if st:
                        n = 8 * st[0] + st[1]
                        eng.wait_ge(s_st, n + 1)
                        if n >= 4:
                            eng.wait_ge(s_pv, (n - 4) // 2 + 1)
                        eng.activation(expo[n % 4][:, :, :], ps_st[pair["T", n]][:, :].rearrange("p (h q) -> p h q", h=4), ACT.Exp,
                                       scale=SCALE).then_inc(s_e, 1)
                    if pv and pv[1] == 7:
                        b = pv[0]
                        eng.wait_ge(s_pv, 4 * b + 4)
                        if b:
                            eng.wait_ge(s_onl, b)
                        eng.activation(o32[:, :], ps_o[:, :], ACT.Copy).then_inc(s_oc, 1)
                    b = i - 5
                    if u == 3 and 0 <= b < EARLY:
                        eng.wait_ge(s_hn, b + 1)
                        if b:
                            eng.wait_ge(s_hw, 16 * b)
                            eng.wait_ge(s_ht, b)
                        eng.activation(hrow[:, :, 0:D], hn[:, :, :], ACT.Copy).then_inc(s_rh, 1)
                    if u == 5 and 0 <= b < EARLY:
                        eng.wait_ge(s_rh, b + 1)
                        eng.wait_ge(s_rl, b + 1)
                        eng.dma_start(hrow_dram.rearrange("(n p) c -> p n c", p=P)[:, TT * b:TT * b + TT, :],
                                      hrow[:, :, :]).then_inc(s_hw, 16)
                    if u == 7 and 0 <= b < EARLY:
                        eng.dma_start(hT_dram[b, :, :], hT[:, :, :, :].rearrange("p l c t -> p (l c t)"))\
                            .then_inc(s_tw, 16)
                    b = i - 6
                    if u == 1 and 0 <= b < EARLY:
                        eng.wait_ge(s_sub, b + 1)
                        exponentials(eng, moe)
                    for b, step in dividing(i, u):
                        if step == 0:
                            eng.wait_ge(s_oc, b + 1)
                            eng.dma_start(den_scratch[b, 0, :].rearrange("(j c) -> j c", j=4),
                                          o32[DK:P:32, :]).then_inc(s_dw, 16)
                        elif step == 1:
                            eng.wait_ge(s_dw, 16 * (b + 1))
                            if b:
                                eng.wait_ge(s_rw, 16 * b)
                            eng.dma_start(den[:, :], den_scratch[b, 0, :].rearrange("(p c) -> p c", p=P)).then_inc(s_dr, 16)
                        elif step == 3:
                            eng.wait_ge(s_rc, b + 1)
                            eng.dma_start(den_scratch[b, 1, :].rearrange("(p c) -> p c", p=P), den[:, :]).then_inc(s_rw, 16)
                        elif step == 4:
                            eng.wait_ge(s_rw, 16 * (b + 1))
                            if b:
                                eng.wait_ge(s_n, b)
                            for j in range(4):
                                row = den_scratch[b, 1:2, j * HG * SEQ:(j + 1) * HG * SEQ]
                                eng.dma_start(rb[32 * j:32 * j + DK, :], row.broadcast_to([DK, HG * SEQ])).then_inc(s_rr, 16)
                        elif step == (6 if b < NB - LATE else 7):
                            eng.wait_ge(s_n, b + 1)
                            if b:
                                eng.wait_ge(s_o, b)
                            eng.activation(onh[:, :, :], o32[:, :].rearrange("p (g t) -> p g t", g=HG),
                                           ACT.Copy).then_inc(s_onh, 1)
            eng.wait_ge(s_hw, 16 * EARLY)
            eng.wait_ge(s_tw, 16 * EARLY)
            eng.wait_ge(s_zs, 16 * 2 * NE)
            eng.wait_ge(s_sw, 16 * 8)

        @block.vector
        def _(eng):
            chain = [0]

            def link(ins):
                chain[0] += 1
                ins.then_inc(s_dch, 1)
                eng.wait_ge(s_dch, chain[0])

            def stats(b):
                eng.wait_ge(s_x[b // 2], 16)
                if b >= 2:
                    eng.wait_ge(s_pow, b - 1)
                for tt in range(TT):
                    last = eng.bn_stats(st6[:, tt, :], xr[:, TT * b + tt, :])
                link(last)
                for tt in range(TT):
                    last = eng.bn_aggr(mv[b % 2][:, tt, :], st6[:, tt, :])
                link(last)
                eng.nop().then_inc(s_stat, 1)

            def normalise(b):
                eng.wait_ge(s_pow, b + 1)
                link(eng.tensor_tensor(rsa[:, :], rstd[b % 2][:, :], anyq[:, :], ALU.mult))
                if b:
                    eng.wait_ge(s_xt, b)
                if b >= 6:
                    eng.wait_ge(s_rl, b - 5)
                for tt in range(TT):
                    last = eng.tensor_scalar(xn[:, tt, :], xr[:, TT * b + tt, :], mv[b % 2][:, tt, 0:1],
                                             rsa[:, tt:tt + 1], ALU.subtract, ALU.mult)
                last.then_inc(s_xn, 1)
                eng.wait_ge(s_xn, b + 1)

            eng.memset(bhl[:, :], 0.0)
            eng.memset(ones33[:, :], 1.0).then_inc(s_ones, 1)
            stats(0)
            stats(1)
            eng.wait_ge(s_mi, 16)
            link(eng.tensor_scalar(nz[:, :, :], mi[:, :, :], 0, None, ALU.not_equal))
            link(eng.tensor_reduce(anyq[:, :], nz[:, :, :], axis=AX.X, op=ALU.max))
            link(eng.tensor_scalar(nz[:, :, :], nz[:, :, :], 1.0, MASKED, ALU.subtract, ALU.mult))
            for tt in range(TT):
                last = eng.tensor_scalar(nz[:, tt, :], nz[:, tt, :], anyq[:, tt:tt + 1], None, ALU.mult)
            last.then_inc(s_mbf, 1)
            eng.wait_ge(s_mbf, 1)
            eng.tensor_copy(mb_q[:, :, :], nz[:, :, :]).then_inc(s_mbq, 1)
            eng.wait_ge(s_bh, 2)
            eng.tensor_tensor(bhl[32:33, :], b32[32:33, :], bh2[32:33, :], ALU.subtract).then_inc(s_bl, 1)
            for i in range(ITER):
                for u in range(8):
                    s, _, _ = units(i, u)
                    if s:
                        b, n = s
                        qt, hg = divmod(n, HG)
                        eng.wait_ge(s_s, 8 * b + n + 1)
                        if n == 0 and b >= 2:
                            eng.wait_ge(s_mt, b - 1)
                        eng.tensor_reduce(mx[b % 2][:, qt, :].rearrange("p (h g j) -> p h g j", h=2, g=HG)[:, :, hg, :],
                                          ps_st[pair["S", 8 * b + n]][:, :].rearrange("p (h j k) -> p h j k", h=2, j=2),
                                          axis=AX.X, op=ALU.max).then_inc(s_mx, 1)
                    if u == 0 and i == 0:
                        normalise(0)
                    if u == 6 and i + 1 < NB:
                        normalise(i + 1)
                    if u == 3 and 2 <= i + 2 < NB:
                        stats(i + 2)
                    if i == 1 and u == 0:
                        eng.wait_ge(s_gh, 1)
                        eng.tensor_tensor(gl[:, :, :], g32[:, :, :], gh[:, :, :], ALU.subtract).then_inc(s_gl, 1)
                    for kind, b in uses(i, u):
                        if kind == "o":
                            eng.wait_ge(s_o, b + 1)
                            tiles = xr[:, TT * b:TT * b + TT, :]
                            eng.tensor_tensor(tiles, bank((kind, b))[:, :].rearrange("p (t d) -> p t d", t=TT), tiles,
                                              ALU.add).then_inc(s_res, 1)
                            eng.wait_ge(s_res, b + 1)
                            eng.nop().then_inc(free((kind, b)), 1)
                            if b >= EARLY:
                                continue
                            for tt in range(TT):
                                last = eng.bn_stats(f6[:, tt, :], xr[:, TT * b + tt, :])
                            link(last)
                            if b >= 2:
                                eng.wait_ge(s_pow2, b - 1)
                            for tt in range(TT):
                                last = eng.bn_aggr(fmv[b % 2][:, tt, :], f6[:, tt, :])
                            link(last)
                            eng.nop().then_inc(s_st2, 1)
                        elif kind == "rt":
                            eng.wait_ge(s_rt, b + 1)
                            logits(eng, link, moe, bank((kind, b)), s_sub)
                            eng.nop().then_inc(free((kind, b)), 1)
                        elif kind in ("xt", "ct"):
                            s_in, (hi, lo), s_out, s_used = (s_xh, xT, s_xl, s_q) if kind == "xt" else (s_ch, cT, s_cl, s_v)
                            eng.wait_ge(s_in, b + 1)
                            eng.tensor_tensor(lo[:, :], bank((kind, b))[:, :], hi[:, :], ALU.subtract).then_inc(s_out, 1)
                            eng.wait_ge(s_out, b + 1)
                            eng.nop().then_inc(free((kind, b)), 1)
                        elif kind in ("q", "k"):
                            s_in, hl, s_out = (s_qh, qhl, s_ql) if kind == "q" else (s_kh, khl, s_kl)
                            eng.wait_ge(s_in, b + 1)
                            eng.tensor_tensor(hl[:, 1, :, :], bank((kind, b))[:, :].rearrange("p (h t) -> p h t", h=2),
                                              hl[:, 0, :, :], ALU.subtract).then_inc(s_out, 1)
                            eng.wait_ge(s_out, b + 1)
                            eng.nop().then_inc(free((kind, b)), 1)
                    b = i - 5
                    if u == 2 and 0 <= b < EARLY:
                        eng.wait_ge(s_pow2, b + 1)
                        if i < NB:
                            eng.wait_ge(s_xt, i + 1)
                        if b:
                            eng.wait_ge(s_rl, b)
                        for tt in range(TT):
                            last = eng.tensor_scalar(hn[:, tt, :], xr[:, TT * b + tt, :], fmv[b % 2][:, tt, 0:1],
                                                     frstd[b % 2][:, tt:tt + 1], ALU.subtract, ALU.mult)
                        last.then_inc(s_hn, 1)
                    if u == 4 and 0 <= b < EARLY:
                        eng.wait_ge(s_hn, b + 1)
                        eng.wait_ge(s_rh, b + 1)
                        eng.tensor_tensor(hrow[:, :, D:2 * D], hn[:, :, :], hrow[:, :, 0:D],
                                          ALU.subtract).then_inc(s_rl, 1)
                    b = i - 6
                    if u == 2 and 0 <= b < EARLY - 1:
                        routing = route(eng, link, moe, b)
                    if 2 <= u <= 5 and 0 <= b < EARLY - 1:
                        next(routing, None)
                    for b, step in dividing(i, u):
                        if b >= NB - LATE and step == 6:
                            eng.wait_ge(s_rr, 64 * (b + 1))
                            eng.tensor_tensor(o32[:, :], o32[:, :], rb[:, :], ALU.mult).then_inc(s_n, 1)
                        if b >= NB - LATE and step == 7:
                            eng.wait_ge(s_onh, b + 1)
                            eng.tensor_tensor(onl[:, :, :], o32[:, :].rearrange("p (g t) -> p g t", g=HG), onh[:, :, :],
                                              ALU.subtract).then_inc(s_onl, 1)
                        if step == 2:
                            eng.wait_ge(s_dr, 16 * (b + 1))
                            eng.reciprocal(den[:, :], den[:, :]).then_inc(s_rc, 1)

        @block.tensor
        def _(eng):
            mm = eng.matmul

            def scores(b, n):
                qt, hg = divmod(n, HG)
                if n == 0:
                    eng.wait_ge(s_qk[b % 3], 192 * (b // 3 + 1))
                wait_pair(eng, ("S", 8 * b + n))
                ps_s = ps_st[pair["S", 8 * b + n]]
                bias = mb_q[:, qt, :].unsqueeze(1).broadcast_to([P, 2, SEQ])
                for hh in range(2):
                    mm(ps_s[:, hh * 2 * SEQ:(hh + 1) * 2 * SEQ], identb[:, :], bias, start=True, stop=False)
                for pp in range(2):
                    for hh in range(2):
                        rows = slice(64 * hh, 64 * hh + ROWS)
                        at = (2 * hh + pp) * SEQ
                        last = mm(ps_s[:, at:at + SEQ], qs[b % 3][rows, 2 * hg + pp, qt * P:(qt + 1) * P],
                                  ks[b % 3][rows, 2 * hg + pp, :], start=False, stop=pp == 1)
                last.then_inc(s_s, 1)

            def scores_t(b, n):
                hg, kt = divmod(n, TT)
                if n == 0:
                    eng.wait_ge(s_mr[b % 3], 32 * (b // 3 + 1))
                wait_pair(eng, ("T", 8 * b + n))
                ps_t = ps_st[pair["T", 8 * b + n]]
                bias = mb_k[:, kt, :].unsqueeze(1).broadcast_to([P, 2, SEQ])
                for hh in range(2):
                    mm(ps_t[:, hh * 2 * SEQ:(hh + 1) * 2 * SEQ], identb[:, :], bias, start=True, stop=False)
                for pp in range(2):
                    for hh in range(2):
                        rows = slice(64 * hh, 64 * hh + ROWS + 1)
                        at = (2 * hh + pp) * SEQ
                        last = mm(ps_t[:, at:at + SEQ], ks[b % 3][rows, 2 * hg + pp, kt * P:(kt + 1) * P],
                                  qs[b % 3][rows, 2 * hg + pp, :], start=False, stop=pp == 1)
                last.then_inc(s_st, 1)

            def values(b, hg):
                eng.wait_ge(s_e, 8 * b + 2 * hg + 2)
                if hg == 0:
                    eng.wait_ge(s_vx, 2 * b + 2)
                if hg == 0 and b:
                    eng.wait_ge(s_oc, b)
                for kt in range(TT):
                    for j in range(4):
                        last = mm(ps_o[32 * j:32 * j + 32, hg * SEQ:(hg + 1) * SEQ], vx[b % 3][:, kt, 4 * hg + j, :],
                                  expo[(8 * b + 2 * hg + kt) % 4][:, 2 * (j % 2) + j // 2, :], start=kt == 0, stop=kt == TT - 1)
                last.then_inc(s_pv, 1)

            def transposes(kind, b, src):
                wait_bank(eng, (kind, b))
                o = bank((kind, b))
                for dc in range(DC):
                    for tt in range(TT):
                        at = dc * SEQ + tt * P
                        last = eng.transpose(o[:, at:at + P], src[:, tt, dc * P:(dc + 1) * P], ident[:, :])
                return last

            def project(kind, b, w0, srcT, ones, bias):
                wait_bank(eng, (kind, b))
                o = bank((kind, b))
                for hh in range(2):
                    oo = o[:, hh * SEQ:(hh + 1) * SEQ]
                    mm(oo, bhl[:, bias * D + hh * P:bias * D + (hh + 1) * P], ones, start=True, stop=False)
                    for dc in range(DC):
                        at = w0 + dc * D + hh * P
                        for wl, xl in TERMS:
                            w = (awh, awl)[wl]
                            last = mm(oo, w[:, at:at + P], srcT[xl][:, dc * SEQ:(dc + 1) * SEQ], start=False,
                                      stop=dc == DC - 1 and xl == 1)
                return last

            eng.wait_ge(s_id, 16)
            eng.wait_ge(s_mbf, 1)
            for kt in range(TT):
                for qt in range(TT):
                    at = kt * SEQ + qt * P
                    last = eng.transpose(bank("mask")[:, at:at + P], nz[:, qt, kt * P:(kt + 1) * P], ident[:, :])
            last.then_inc(s_mbT, 1)
            for qt in range(TT):
                last = mm(bank("any")[:, qt * P:(qt + 1) * P], anyq[:, qt:qt + 1].broadcast_to([P, P]), ident[:, :],
                          start=True, stop=True)
            last.then_inc(s_anyb, 1)
            eng.wait_ge(s_idb, 1)
            eng.wait_ge(s_mbq, 1)
            for i in range(ITER):
                for u in range(8):
                    s, st, pv = units(i, u)
                    if s:
                        scores(*s)
                    for kind, b in uses(i, u):
                        if kind == "o":
                            wait_bank(eng, (kind, b))
                            eng.wait_ge(s_onl, b + 1)
                            for tt in range(TT):
                                o = bank((kind, b))[:, tt * D:(tt + 1) * D]
                                mm(o, ones33[:, 0:P], bhl[:, 3 * D:4 * D], start=True, stop=False)
                                for hg in range(HG):
                                    for wl, xl in TERMS:
                                        w = (awh, awl)[wl]
                                        last = mm(o, (onh, onl)[xl][:, hg, tt * P:(tt + 1) * P],
                                                  w[:, WO + hg * D:WO + (hg + 1) * D], start=False,
                                                  stop=hg == HG - 1 and xl == 1)
                            last.then_inc(s_o, 1)
                        elif kind == "ht":
                            wait_bank(eng, (kind, b))
                            eng.wait_ge(s_rh, b + 1)
                            eng.wait_ge(s_rl, b + 1)
                            if b == 0:
                                eng.wait_ge(s_idh, 1)
                            transpose_rows(eng, moe, bank((kind, b)), hrow).then_inc(s_ht, 1)
                        elif kind == "rt":
                            wait_bank(eng, (kind, b))
                            eng.wait_ge(s_th, b + 1)
                            if b == 0:
                                eng.wait_ge(s_gl, 1)
                            router(eng, moe, bank((kind, b)), hT).then_inc(s_rt, 1)
                        elif kind == "mt":
                            wait_bank(eng, (kind, b))
                            eng.wait_ge(s_mx, 8 * b + 8)
                            for tt in range(TT):
                                last = eng.transpose(bank((kind, b))[0:H, tt * P:(tt + 1) * P], mx[b % 2][:, tt, :], ident[:, :])
                            last.then_inc(s_mt, 1)
                        elif kind == "xt":
                            eng.wait_ge(s_xn, b + 1)
                            transposes(kind, b, xn).then_inc(s_xt, 1)
                        elif kind == "ct":
                            eng.wait_ge(s_c, 16 * (b + 1))
                            transposes(kind, b, c32).then_inc(s_ct, 1)
                        elif kind == "q":
                            if b == 0:
                                eng.wait_ge(s_awl, 1)
                                eng.wait_ge(s_bl, 1)
                                eng.wait_ge(s_any33, 1)
                            eng.wait_ge(s_xl, b + 1)
                            project(kind, b, WQ, xT, any33[:, :], 0).then_inc(s_q, 1)
                        elif kind == "k":
                            eng.wait_ge(s_cl, b + 1)
                            project(kind, b, WK, cT, ones33[:, :], 1).then_inc(s_k, 1)
                        elif kind == "v":
                            wait_bank(eng, (kind, b))
                            if b == 0:
                                eng.wait_ge(s_awl, 2)
                            for tt in range(TT):
                                o = bank((kind, b))[:, tt * D:(tt + 1) * D]
                                mm(o, ones33[:, 0:P], bhl[:, 2 * D:3 * D], start=True, stop=False)
                                for dc in range(DC):
                                    for wl, xl in TERMS:
                                        w = (awh, awl)[wl]
                                        at = dc * SEQ + tt * P
                                        last = mm(o, cT[xl][:, at:at + P], w[:, WV + dc * D:WV + (dc + 1) * D],
                                                  start=False, stop=dc == DC - 1 and xl == 1)
                            last.then_inc(s_v, 1)
                    if st:
                        scores_t(*st)
                    if pv and pv[1] % 2 == 1:
                        values(pv[0], pv[1] // 2)


def route(eng, link, moe, b):
    rows = slice(TT * b, TT * b + TT)
    eng.wait_ge(moe.s_ex, 2 * b + 2)
    link(eng.tensor_reduce(moe.tot[:, :], moe.ex[:, :, 0:NE], axis=AX.X, op=ALU.add))
    link(eng.reciprocal(moe.tot[:, :], moe.tot[:, :]))
    sc = moe.lg[:, :, 0:NE]
    link(eng.tensor_tensor(sc, moe.ex[:, :, 0:NE], moe.tot[:, :].unsqueeze(2).broadcast_to([P, TT, NE]), ALU.mult))
    yield
    by_e = sc.unsqueeze(3).broadcast_to([P, TT, NE, NE])
    by_j = sc.unsqueeze(2).broadcast_to([P, TT, NE, NE])
    link(eng.tensor_tensor(moe.cmp_[:, :, :, :], by_j, by_e, ALU.is_gt))
    link(eng.tensor_reduce(moe.rank[:, :, :], moe.cmp_[:, :, :, :], axis=AX.X, op=ALU.add))
    link(eng.tensor_tensor(moe.cmp_[:, :, :, :], by_j, by_e, ALU.is_equal))
    yield
    eng.memset(moe.sel[:, rows, 0:1], 0.0)
    for e in range(1, NE):
        last = eng.tensor_reduce(moe.sel[:, rows, e:e + 1], moe.cmp_[:, :, e, 0:e], axis=AX.X, op=ALU.add)
    link(last)
    link(eng.tensor_tensor(moe.rank[:, :, :], moe.rank[:, :, :], moe.sel[:, rows, :], ALU.add))
    eng.tensor_scalar(moe.sel[:, rows, :], moe.rank[:, :, :], float(TOPK), None, ALU.is_lt)
    for j in range(TOPK):
        last = eng.tensor_scalar(moe.chosen[j][:, rows, :], moe.rank[:, :, :], float(j), None, ALU.is_equal)
    link(last)
    yield
    for j in range(TOPK):
        link(eng.tensor_tensor(moe.ex[:, :, 0:NE], moe.chosen[j][:, rows, :], sc, ALU.mult))
        last = eng.tensor_reduce(moe.wsel[:, j, rows], moe.ex[:, :, 0:NE], axis=AX.X, op=ALU.add)
        link(last)
    link(eng.tensor_scalar(moe.ex[:, :, NE:NG], moe.ex[:, :, NE:NG], 1.0, None, ALU.add))
    link(eng.reciprocal(moe.wshared[:, rows].unsqueeze(2), moe.ex[:, :, NE:NG]))


def logits(eng, link, moe, ps, s_sub):
    link(eng.tensor_copy(moe.lg[:, :, :], ps[:, 0:16 * TT].rearrange("p (t c) -> p t c", c=16)[:, :, 0:NG]))
    link(eng.tensor_reduce(moe.top[:, :], moe.lg[:, :, 0:NE], axis=AX.X, op=ALU.max))
    eng.tensor_tensor(moe.ex[:, :, 0:NE], moe.lg[:, :, 0:NE], moe.top[:, :].unsqueeze(2).broadcast_to([P, TT, NE]),
                      ALU.subtract).then_inc(s_sub, 1)


def exponentials(eng, moe):
    eng.activation(moe.ex[:, :, 0:NE], moe.ex[:, :, 0:NE], ACT.Exp).then_inc(moe.s_ex, 1)
    eng.activation(moe.ex[:, :, NE:NG], moe.lg[:, :, NE:NG], ACT.Exp, scale=-1.0).then_inc(moe.s_ex, 1)


def transpose_rows(eng, moe, ps, hrow):
    o = ps[:, :].bitcast(FP16)
    for part in range(2 * DC):
        for tt in range(TT):
            at = part * SEQ + tt * P
            last = eng.transpose(o[:, at:at + P], hrow[:, tt, part * P:(part + 1) * P], moe.identh[:, :])
    return last


def router(eng, moe, ps, hT):
    for tt in range(TT):
        for dc in range(DC):
            for wl, xl in TERMS:
                last = eng.matmul(ps[:, 16 * tt:16 * tt + NG], hT[:, xl, dc, tt * P:(tt + 1) * P],
                                  (moe.gh, moe.gl)[wl][:, dc, :], start=dc == 0 and (wl, xl) == (0, 0),
                                  stop=dc == DC - 1 and xl == 1)
    return last


def ffn(nc, sb, sem, xr, fwh, fwl, ident, moe, consts_in, hrow_dram, hT_dram, sw_dram, sorted_rows, sorted_out, out):
    identh, sel, chosen, wsel, wshared = moe.identh, moe.sel, moe.chosen, moe.wsel, moe.wshared
    with ExitStack() as here:
        t = lambda n, s, d: sb(here, n, s, d)
        pt = lambda n, s: here.enter_context(nc.psum_tensor(n, s, FP32))
        NGB = 5
        ya = [t(f"ya{i}", [P, TOPK, D], FP32) for i in range(NGB)]
        sw = t("sw", [P, 2, 2, FW], FP16)
        consts = t("consts", [P, 2 * P + NT + NTILE], FP32)
        below = consts[:, 0:P]
        ones = consts[:, P:2 * P]
        tile_starts = consts[:, 2 * P:2 * P + NT]
        tile_ids = consts[:, 2 * P + NT:]
        hrow = t("hrow_all", [P, NT, 2 * D], FP16)
        hT = [t(f"hT_blk{i}", [P, 2, 2, DC, SEQ], FP16) for i in range(2)]
        prod = t("prod", [P, NT, NE], FP32)
        cmp_ = t("cmp_tiles", [P, 2 * DC * SEQ // 2], FP32)
        assert NTILE * (NE - 1) <= 2 * DC * SEQ // 2
        last_T = cmp_[:, :].bitcast(FP16).rearrange("p (l c t) -> p l c t", l=2, c=DC)
        scans = t("scans", [P, 2, NT, NE], FP32)
        scan = [scans[:, i, :, :] for i in range(2)]
        last_n = scans[:, :, :, :].rearrange("p l n e -> p (l n e)").rearrange("p (t d) -> p t d", t=TT)
        f6 = t("last_f6", [P, TT, 6], FP32)
        fmv = t("last_fmv", [P, TT, 2], FP32)
        fve = t("last_fve", [P, TT], FP32)
        frstd = t("last_frstd", [P, TT], FP32)
        ends = [t(f"ends{i}", [P, NE], FP32) for i in range(2)]
        ntl = t("ntl", [P, NE], FP32)
        emapf = t("emapf", [1, NTILE], FP32)
        emap = t("emap", [1, NTILE], INT32)
        slotf = t("slotf", [P, TOPK, NT], FP32)
        slot = t("slot", [P, TOPK, NT], UINT32)
        gs = [t(f"gs{i}", [P, BLK], FP32) for i in range(2)]
        hf = [t(f"hf{i}", [P, BLK], FP32) for i in range(2)]
        hh = [t(f"hh{i}", [P, 3, BLK], FP16) for i in range(2)]
        hl = [t(f"hl{i}", [P, 3, BLK], FP16) for i in range(2)]
        xg = [t(f"xg{i}", [P, 2 * D], FP16) for i in range(3)]
        xgT = [t(f"xgT{i}", [P, 2, DC, P], FP16) for i in range(2)]
        ys = [t(f"ys{i}", [P, D], FP32) for i in range(3)]
        ps_g = [pt(f"ps_g{i}", [P, BLK]) for i in range(2)]
        ps_u = [pt(f"ps_u{i}", [P, BLK]) for i in range(2)]
        ps_d = [pt(f"ps_d{i}", [P, 2 * D]) for i in range(4)]
        half_of = lambda ps: ps[:, :].bitcast(FP16)

        f_c = sem("f_c")
        l_st = sem("l_st"); l_ve = sem("l_ve"); l_pow = sem("l_pow")
        l_hn = sem("l_hn"); l_rh = sem("l_rh"); l_rl = sem("l_rl")
        l_ht = sem("l_ht"); l_th = sem("l_th"); l_tw = sem("l_tw")
        l_rt = sem("l_rt"); l_sub = sem("l_sub"); l_sel = sem("l_sel")
        f_w = [sem(f"f_w{i}") for i in range(4)]
        f_hr = sem("f_hr"); f_ht = [sem(f"f_ht{i}") for i in range(2)]
        f_cnt = sem("f_cnt"); f_read = sem("f_read"); f_slot = sem("f_slot"); f_emap = sem("f_emap")
        f_gd = sem("f_gd"); f_ud = sem("f_ud"); f_si = sem("f_si"); f_hf = sem("f_hf"); f_hh = sem("f_hh")
        f_hl = sem("f_hl"); f_dn = sem("f_dn"); f_acc = sem("f_acc"); f_out = sem("f_out")
        f_dch = sem("f_dch"); f_sc = sem("f_sc")
        r_x = [sem(f"r_x{i}") for i in range(3)]
        r_t = sem("r_t"); r_tx = sem("r_tx"); r_g = sem("r_g"); r_u = sem("r_u"); r_si = sem("r_si"); r_hf = sem("r_hf")
        r_ht = sem("r_ht"); r_hh = sem("r_hh"); r_hl = sem("r_hl"); r_y = sem("r_y"); r_ys = sem("r_ys")
        r_pad = sem("r_pad")
        r_st = [sem(f"r_st{i}") for i in range(3)]
        r_ga = [sem(f"r_ga{i}") for i in range(NGB)]
        r_add = sem("r_add")
        HB = 4
        steps = [(blk, e) for blk in range(NBLK) for e in range(2)]
        half_steps = 2 * HB
        NC = len(IC)
        pieces = [(e, cols) for e in range(2) for cols in (slice(0, DOWN0), slice(DOWN0, FW))]
        block = here.enter_context(nc.Block())

        @block.sync
        def _(eng):
            eng.dma_start(consts[:, :], consts_in).then_inc(f_c, 16)

            def load_w(i):
                e, cols = pieces[i]
                eng.dma_start(sw[:, e, :, cols], sw_dram[e, :, :, cols].rearrange("l p w -> p l w")).then_inc(f_w[i], 16)

            def load_T(blk):
                if blk >= 2:
                    eng.wait_ge(f_ud, NC * 2 * (blk - 1))
                if blk == NBLK - 1:
                    eng.wait_ge(l_tw, 16)
                eng.dma_start(hT[blk % 2][:, :, :, :, :].rearrange("p b l c t -> p b (l c t)"),
                              hT_dram[2 * blk:2 * blk + 2, :, :].rearrange("b p c -> p b c")).then_inc(f_ht[blk % 2], 16)

            load_w(0)
            load_T(0)
            load_w(1)
            eng.dma_start(hrow[:, 0:NT - TT, :], hrow_dram.rearrange("(n p) c -> p n c", p=P)[:, 0:NT - TT, :]).then_inc(f_hr, 16)
            load_w(2)
            load_w(3)
            load_T(1)
            for blk in range(2, HB + 1):
                load_T(blk)

            def load(k):
                if k == 0:
                    eng.wait_ge(f_sc, 16 * 2 * NT)
                if k >= 3:
                    eng.wait_ge(r_t, k - 2)
                eng.dma_start(xg[k % 3][:, :], sorted_rows[k * P:(k + 1) * P, :]).then_inc(r_x[k % 3], 16)

            for k in range(NTILE):
                load(k)
            for blk in range(HB + 1, NBLK):
                load_T(blk)
            ov = out.rearrange("(n p) d -> p n d", p=P)
            for blk in range(NBLK):
                eng.wait_ge(r_add, BT * (blk + 1))
                eng.wait_ge(f_acc, 4 * (blk + 1))
                eng.dma_start(ov[:, BT * blk:BT * (blk + 1), :], xr[:, BT * blk:BT * (blk + 1), :]).then_inc(f_out, 16)
            eng.wait_ge(f_out, 16 * NBLK)

        @block.gpsimd
        def _(eng):
            eng.wait_ge(l_st, 1)
            eng.tensor_scalar(fve[:, :], fmv[:, :, 1], EPS, None, ALU.add).then_inc(l_ve, 1)
            eng.wait_ge(l_ve, 1)
            eng.tensor_tensor(frstd[:, :], fve[:, :], moe.neghalf[:, :], ALU.pow).then_inc(l_pow, 1)
            eng.wait_ge(f_slot, 2)
            eng.wait_ge(f_hr, 16)
            eng.wait_ge(l_rh, 1)
            eng.wait_ge(l_rl, 1)
            for n in range(NT):
                for j in range(2):
                    eng.indirect_dma_start(sorted_rows, bass.IndirectOffsetOnAxis(slot[:, j, n:n + 1], 0),
                                           hrow[:, n, :], None).then_inc(f_sc, 16)
            for k in range(NTILE):
                eng.wait_ge(r_ys, k + 1)
                eng.dma_start(sorted_out[k * P:(k + 1) * P, :], ys[k % 3][:, :]).then_inc(r_st[k % 3], 16)
            for i in range(3):
                eng.wait_ge(r_st[i], 16 * len(range(i, NTILE, 3)))
            for n in range(NT):
                if n >= NGB:
                    eng.wait_ge(r_add, n - NGB + 1)
                for j in range(2):
                    eng.indirect_dma_start(ya[n % NGB][:, j, :], None, sorted_out,
                                           bass.IndirectOffsetOnAxis(slot[:, j, n:n + 1], 0)).then_inc(r_ga[n % NGB], 16)

        @block.scalar
        def _(eng):
            eng.wait_ge(l_hn, 1)
            eng.activation(hrow[:, NT - TT:NT, 0:D], last_n, ACT.Copy).then_inc(l_rh, 1)
            eng.wait_ge(l_ht, 1)
            eng.activation(last_T.rearrange("p l c t -> p (l c t)"), half_of(ps_d[3]), ACT.Copy).then_inc(l_th, 1)
            eng.wait_ge(l_th, 1)
            eng.dma_start(hT_dram[NB - 1, :, :], last_T.rearrange("p l c t -> p (l c t)")).then_inc(l_tw, 16)
            eng.wait_ge(l_sub, 1)
            exponentials(eng, moe)

            def shared(n):
                for c, m in enumerate(IC):
                    k = NC * n + c
                    eng.wait_ge(f_gd, k + 1)
                    if k >= 2:
                        eng.wait_ge(f_hf, k - 1)
                    eng.activation(gs[k % 2][0:m, :], ps_g[k % 2][0:m, :], ACT.Silu).then_inc(f_si, 1)
                    eng.wait_ge(f_hf, k + 1)
                    if n >= 2:
                        eng.wait_ge(f_dn, 2 * (n - 1))
                    eng.activation(hh[n % 2][0:m, c, :], hf[k % 2][0:m, :], ACT.Copy).then_inc(f_hh, 1)

            for n in range(half_steps):
                shared(n)
            for k in range(NTILE + 2):
                if k < NTILE:
                    eng.wait_ge(r_g, k + 1)
                    if k >= 2:
                        eng.wait_ge(r_hf, k - 1)
                    else:
                        eng.wait_ge(f_hf, NC * half_steps)
                    eng.activation(gs[k % 2][:, 0:INTER], ps_g[k % 2][:, 0:INTER], ACT.Silu).then_inc(r_si, 1)
                if 0 <= k - 1 < NTILE:
                    eng.wait_ge(r_ht, k)
                    if k - 1 >= 2:
                        eng.wait_ge(r_y, k - 2)
                    else:
                        eng.wait_ge(f_dn, 2 * half_steps)
                    eng.activation(hh[(k - 1) % 2][:, :, 0:P],
                                   ps_d[1 + (k - 1) % 2][:, 0:3 * P].rearrange("p (c t) -> p c t", c=3),
                                   ACT.Copy).then_inc(r_hh, 1)
                if 0 <= k - 2 < NTILE:
                    eng.wait_ge(r_y, k - 1)
                    if k - 2 >= 3:
                        eng.wait_ge(r_st[(k - 2) % 3], 16 * ((k - 2) // 3))
                    eng.activation(ys[(k - 2) % 3][:, :], ps_d[3][:, 0:D], ACT.Copy).then_inc(r_ys, 1)
            for n in range(half_steps, len(steps)):
                shared(n)

        @block.vector
        def _(eng):
            chain = [0]

            def link(ins):
                chain[0] += 1
                ins.then_inc(f_dch, 1)
                eng.wait_ge(f_dch, chain[0])

            for tt in range(TT):
                last = eng.bn_stats(f6[:, tt, :], xr[:, NT - TT + tt, :])
            link(last)
            for tt in range(TT):
                last = eng.bn_aggr(fmv[:, tt, :], f6[:, tt, :])
            link(last)
            eng.nop().then_inc(l_st, 1)
            left = route(eng, link, moe, NB - 2)
            next(left)
            eng.wait_ge(l_pow, 1)
            for tt in range(TT):
                last = eng.tensor_scalar(last_n[:, tt, :], xr[:, NT - TT + tt, :], fmv[:, tt, 0:1], frstd[:, tt:tt + 1],
                                         ALU.subtract, ALU.mult)
            last.then_inc(l_hn, 1)
            next(left)
            eng.wait_ge(l_hn, 1)
            eng.wait_ge(l_rh, 1)
            eng.tensor_tensor(hrow[:, NT - TT:NT, D:2 * D], last_n, hrow[:, NT - TT:NT, 0:D], ALU.subtract).then_inc(l_rl, 1)
            for _ in left:
                pass
            eng.wait_ge(l_rt, 1)
            logits(eng, link, moe, ps_d[1], l_sub)
            for _ in route(eng, link, moe, NB - 1):
                pass
            eng.nop().then_inc(l_sel, 1)
            eng.wait_ge(l_rl, 1)

            def slots():
                eng.wait_ge(f_cnt, 1)
                before = ps_d[2][:, 0:NT * NE].rearrange("p (n e) -> p n e", e=NE)
                total = ps_d[2][:, NT * NE:2 * NT * NE].rearrange("p (n e) -> p n e", e=NE)
                link(eng.tensor_copy(scan[0][:, :, :], total))
                cur, step = 0, 1
                while step < NT:
                    eng.tensor_copy(scan[1 - cur][:, 0:step, :], scan[cur][:, 0:step, :])
                    link(eng.tensor_tensor(scan[1 - cur][:, step:NT, :], scan[cur][:, step:NT, :],
                                           scan[cur][:, 0:NT - step, :], ALU.add))
                    cur, step = 1 - cur, 2 * step
                    if step in (4, 16, 32):
                        yield
                eng.wait_ge(l_tw, 16)
                c3 = cmp_[:, 0:NE * NT].rearrange("p (e n) -> p e n", e=NE)
                link(eng.tensor_tensor(c3, scan[cur][:, NT - 1, :].unsqueeze(2).broadcast_to([P, NE, NT]),
                                       tile_starts.unsqueeze(1).broadcast_to([P, NE, NT]), ALU.is_gt))
                link(eng.tensor_reduce(ntl[:, :], c3, axis=AX.X, op=ALU.add))
                link(eng.tensor_copy(ends[0][:, :], ntl[:, :]))
                at, step = 0, 1
                while step < NE:
                    eng.tensor_copy(ends[1 - at][:, 0:step], ends[at][:, 0:step])
                    link(eng.tensor_tensor(ends[1 - at][:, step:NE], ends[at][:, step:NE], ends[at][:, 0:NE - step], ALU.add))
                    at, step = 1 - at, 2 * step
                yield
                ce = cmp_[0:1, 0:NTILE * (NE - 1)].rearrange("p (n e) -> p n e", e=NE - 1)
                link(eng.tensor_tensor(ce, ends[at][0:1, 0:NE - 1].unsqueeze(1).broadcast_to([1, NTILE, NE - 1]),
                                       tile_ids[0:1, :].unsqueeze(2).broadcast_to([1, NTILE, NE - 1]), ALU.is_le))
                link(eng.tensor_reduce(emapf[:, :], ce, axis=AX.X, op=ALU.add))
                eng.tensor_copy(emap[:, :], emapf[:, :]).then_inc(f_emap, 1)
                yield
                link(eng.tensor_tensor(ntl[:, :], ends[at][:, :], ntl[:, :], ALU.subtract))
                link(eng.tensor_scalar(ntl[:, :], ntl[:, :], float(P), None, ALU.mult))
                link(eng.tensor_tensor(scan[cur][:, :, :], total, scan[cur][:, :, :], ALU.subtract))
                link(eng.tensor_tensor(scan[cur][:, :, :], before, scan[cur][:, :, :], ALU.subtract))
                eng.nop().then_inc(f_read, 1)
                link(eng.tensor_tensor(scan[cur][:, :, :], scan[cur][:, :, :],
                                       ntl[:, :].unsqueeze(1).broadcast_to([P, NT, NE]), ALU.add))
                yield
                for j in range(2):
                    link(eng.tensor_tensor(prod[:, :, :], chosen[j][:, :, :], scan[cur][:, :, :], ALU.mult))
                    link(eng.tensor_reduce(slotf[:, j, :], prod[:, :, :], axis=AX.X, op=ALU.add))
                    eng.tensor_copy(slot[:, j, :], slotf[:, j, :]).then_inc(f_slot, 1)

            def combine(n):
                blk, e = steps[n]
                for j in range(BT):
                    if j % 2 == 0:
                        eng.wait_ge(f_dn, 2 * n + j // 2 + 1)
                    if j == 0 and n:
                        eng.wait_ge(f_acc, 2 * n)
                    tile = xr[:, BT * blk + j, :]
                    src = ps_d[2 * (n % 2) + j // 2][:, (j % 2) * D:(j % 2 + 1) * D]
                    last = eng.scalar_tensor_tensor(tile, src, wshared[:, BT * blk + j:BT * blk + j + 1], tile, ALU.mult, ALU.add)
                    if j % 2:
                        last.then_inc(f_acc, 1)

            def shared(n):
                for c, m in enumerate(IC):
                    k = NC * n + c
                    eng.wait_ge(f_si, k + 1)
                    eng.wait_ge(f_ud, k + 1)
                    if k >= 2:
                        eng.wait_ge(f_hl, k - 1)
                    eng.tensor_tensor(hf[k % 2][0:m, :], ps_u[k % 2][0:m, :], gs[k % 2][0:m, :], ALU.mult).then_inc(f_hf, 1)
                    eng.wait_ge(f_hh, k + 1)
                    eng.tensor_tensor(hl[n % 2][0:m, c, :], hf[k % 2][0:m, :], hh[n % 2][0:m, c, :],
                                      ALU.subtract).then_inc(f_hl, 1)
                    for _ in range(PARTS.get((n, c), 0)):
                        next(sorting, None)

            def gathered(n):
                eng.wait_ge(r_ga[n % NGB], 32 * (n // NGB + 1))
                tile = xr[:, n, :]
                if n >= BT * HB and n % BT == 0:
                    eng.wait_ge(f_acc, 4 * (n // BT + 1))
                link(eng.scalar_tensor_tensor(tile, ya[n % NGB][:, 0, :], wsel[:, 0, n:n + 1], tile, ALU.mult, ALU.add))
                eng.scalar_tensor_tensor(tile, ya[n % NGB][:, 1, :], wsel[:, 1, n:n + 1], tile, ALU.mult, ALU.add)\
                    .then_inc(r_add, 1)

            PARTS = {(0, 2): 2, (1, 0): 2, (1, 1): 2, (1, 2): 2}
            sorting = slots()
            for n in range(half_steps):
                shared(n)
                if n:
                    combine(n - 1)
            combine(half_steps - 1)
            for i in range(2):
                eng.memset(hf[i][:, INTER:3 * P], 0.0).then_inc(r_pad, 1)
            eng.wait_ge(r_pad, 2)

            def transposed(k):
                eng.wait_ge(r_t, k + 1)
                if k >= 2:
                    eng.wait_ge(r_u, k - 1)
                eng.tensor_copy(xgT[k % 2][:, :, :, :],
                                half_of(ps_d[0])[:, 0:4 * P].rearrange("p (l c t) -> p l c t", l=2, c=DC)).then_inc(r_tx, 1)

            transposed(0)
            for k in range(NTILE + 1):
                if k < NTILE:
                    eng.wait_ge(r_si, k + 1)
                    eng.wait_ge(r_u, k + 1)
                    if k >= 2:
                        eng.wait_ge(r_ht, k - 1)
                    eng.tensor_tensor(hf[k % 2][:, 0:INTER], ps_u[k % 2][:, 0:INTER], gs[k % 2][:, 0:INTER],
                                      ALU.mult).then_inc(r_hf, 1)
                if k + 1 < NTILE:
                    transposed(k + 1)
                if k:
                    b = k - 1
                    eng.wait_ge(r_hh, b + 1)
                    eng.tensor_tensor(hl[b % 2][:, :, 0:P], ps_d[1 + b % 2][:, 0:3 * P].rearrange("p (c t) -> p c t", c=3),
                                      hh[b % 2][:, :, 0:P], ALU.subtract).then_inc(r_hl, 1)
            done = 0
            for n in range(half_steps, len(steps)):
                shared(n)
                if n > half_steps:
                    combine(n - 1)
                ready = BT * HB if n == half_steps else BT * (steps[n - 1][0] + steps[n - 1][1])
                for _ in range(1 if n == half_steps else 4):
                    if done < ready:
                        gathered(done)
                        done += 1
            combine(len(steps) - 1)
            while done < NT:
                gathered(done)
                done += 1

        @block.tensor
        def _(eng):
            mm = eng.matmul
            eng.wait_ge(l_rh, 1)
            eng.wait_ge(l_rl, 1)
            transpose_rows(eng, moe, ps_d[3], hrow[:, NT - TT:NT, :]).then_inc(l_ht, 1)
            eng.wait_ge(l_th, 1)
            router(eng, moe, ps_d[1], last_T).then_inc(l_rt, 1)

            def counts():
                eng.wait_ge(f_c, 16)
                eng.wait_ge(l_sel, 1)
                for lhs, at in ((below, 0), (ones, NT * NE)):
                    last = mm(ps_d[2][:, at:at + NT * NE], lhs, sel[:, :, :], start=True, stop=True)
                last.then_inc(f_cnt, 1)

            def up(n):
                blk, e = steps[n]
                if e == 0:
                    eng.wait_ge(f_ht[blk % 2], 16 * (blk // 2 + 1))
                if n < 2:
                    eng.wait_ge(f_w[2 * n], 16)
                for c, m in enumerate(IC):
                    k = NC * n + c
                    for w0, o, s_out in ((0, ps_g[k % 2], f_gd), (UP0, ps_u[k % 2], f_ud)):
                        if n == half_steps and c < 2:
                            eng.wait_ge(r_hf, NTILE)
                        elif k >= 2:
                            eng.wait_ge(f_si if w0 == 0 else f_hf, k - 1)
                        for dc in range(DC):
                            at = w0 + dc * INTER + P * c
                            for wl, xl in TERMS:
                                last = mm(o[0:m, :], sw[:, e, wl, at:at + m], hT[blk % 2][:, :, xl, dc, :],
                                          start=dc == 0 and (wl, xl) == (0, 0), stop=dc == DC - 1 and xl == 1)
                        last.then_inc(s_out, 1)

            def down(n):
                blk, e = steps[n]
                eng.wait_ge(f_hl, NC * n + NC)
                if n == 0:
                    eng.wait_ge(l_sub, 1)
                if n < 2:
                    eng.wait_ge(f_w[2 * n + 1], 16)
                if n == 1:
                    eng.wait_ge(f_read, 1)
                if n >= 2:
                    eng.wait_ge(f_acc, 2 * (n - 1))
                if n == half_steps:
                    eng.wait_ge(r_ys, NTILE)
                    eng.wait_ge(r_hl, NTILE)
                for j in range(BT):
                    o = ps_d[2 * (n % 2) + j // 2][:, (j % 2) * D:(j % 2 + 1) * D]
                    for c, m in enumerate(IC):
                        at = DOWN0 + c * D
                        for wl, xl in TERMS:
                            last = mm(o, (hh, hl)[xl][n % 2][0:m, c, j * P:(j + 1) * P], sw[0:m, e, wl, at:at + D],
                                      start=c == 0 and (wl, xl) == (0, 0), stop=c == NC - 1 and xl == 1)
                    if j % 2:
                        last.then_inc(f_dn, 1)

            for n in range(half_steps):
                up(n)
                if n == 0:
                    counts()
                if n:
                    down(n - 1)
            down(half_steps - 1)

            expert = [None]

            def rows_T(k):
                eng.wait_ge(r_x[k % 3], 16 * (k // 3 + 1))
                if k:
                    eng.wait_ge(r_tx, k)
                else:
                    eng.wait_ge(f_acc, 2 * half_steps)
                for part in range(2):
                    for dc in range(DC):
                        at = part * DC + dc
                        last = eng.transpose(half_of(ps_d[0])[:, at * P:(at + 1) * P],
                                             xg[k % 3][:, at * P:(at + 1) * P], identh[:, :])
                last.then_inc(r_t, 1)

            eng.wait_ge(f_emap, 1)
            experts = {}
            rows_T(0)
            for k in range(NTILE + 2):
                if k < NTILE:
                    experts[k] = e = eng.value_load(emap[0:1, k:k + 1], min_val=0, max_val=NE - 1)
                    eng.wait_ge(r_tx, k + 1)
                    for w0, o, s_out in ((0, ps_g[k % 2], r_g), (UP0, ps_u[k % 2], r_u)):
                        if k >= 2:
                            eng.wait_ge(r_si if w0 == 0 else r_hf, k - 1)
                        else:
                            eng.wait_ge(f_hf, NC * half_steps)
                        for dc in range(DC):
                            for wl, xl in TERMS:
                                last = mm(o[:, 0:INTER], xgT[k % 2][:, xl, dc, :],
                                          (fwh, fwl)[wl][:, bass.ds(e, 1), w0 + dc * INTER:w0 + (dc + 1) * INTER],
                                          start=dc == 0 and (wl, xl) == (0, 0), stop=dc == DC - 1 and xl == 1)
                        last.then_inc(s_out, 1)
                if 0 <= k - 1 < NTILE:
                    b = k - 1
                    eng.wait_ge(r_hf, b + 1)
                    if b >= 2:
                        eng.wait_ge(r_hl, b - 1)
                    for c in range(3):
                        last = eng.transpose(ps_d[1 + b % 2][:, c * P:(c + 1) * P], hf[b % 2][:, c * P:(c + 1) * P],
                                             ident[:, :])
                    last.then_inc(r_ht, 1)
                if k + 1 < NTILE:
                    rows_T(k + 1)
                if 0 <= k - 2 < NTILE:
                    b = k - 2
                    eng.wait_ge(r_hl, b + 1)
                    if b:
                        eng.wait_ge(r_ys, b)
                    e = experts.pop(b)
                    for c in range(3):
                        at = DOWN0 + c * D
                        for wl, xl in TERMS:
                            last = mm(ps_d[3][:, 0:D], (hh, hl)[xl][b % 2][:, c, 0:P],
                                      (fwh, fwl)[wl][:, bass.ds(e, 1), at:at + D],
                                      start=c == 0 and (wl, xl) == (0, 0), stop=c == 2 and xl == 1)
                    last.then_inc(r_y, 1)
            for n in range(half_steps, len(steps)):
                up(n)
                if n > half_steps:
                    down(n - 1)
            down(len(steps) - 1)


def kernel(x, ctx_1024, mask_1x1xSxS2_ik0, L0_xattn_Wq_w, L0_xattn_Wq_b, L0_xattn_Wk_w, L0_xattn_Wk_b,
           L0_xattn_Wv_w, L0_xattn_Wv_b, L0_xattn_Wo_w, L0_xattn_Wo_b, L0_ffn_gate_w, L0_ffn_experts_gate_up,
           L0_ffn_experts_down, L0_ffn_shared_gate_w, L0_ffn_shared_up_w, L0_ffn_shared_down_w,
           L0_ffn_shared_expert_gate_w):
    import numpy as np
    import concourse.bacc as bacc
    from concourse.bass_utils import run_bass_kernel_spmd

    a = np.asarray
    halves = np.concatenate([np.arange(h * DK, (h + 1) * DK) for hh in range(2) for h in range(hh, H, 2)])

    def rows(w):
        return a(w).reshape(DC, P, -1).transpose(1, 0, 2).reshape(P, -1)

    w_in = np.concatenate([rows(a(L0_xattn_Wq_w)[:, halves]), rows(a(L0_xattn_Wk_w)[:, halves]), rows(L0_xattn_Wv_w)], 1)
    bias = np.concatenate([a(L0_xattn_Wq_b)[halves], a(L0_xattn_Wk_b)[halves], a(L0_xattn_Wv_b), a(L0_xattn_Wo_b)])[None]
    w_o = np.zeros((HG, 4, 32, D), np.float32)
    w_o[:, :, 0:DK] = a(L0_xattn_Wo_w).reshape(HG, 4, DK, D)
    w_o = w_o.reshape(HG, P, D).transpose(1, 0, 2).reshape(P, HG * D)
    gate = np.concatenate([a(L0_ffn_experts_gate_up)[:, :INTER], a(L0_ffn_shared_gate_w).reshape(2, INTER, D)])
    up = np.concatenate([a(L0_ffn_experts_gate_up)[:, INTER:], a(L0_ffn_shared_up_w).reshape(2, INTER, D)])
    down = np.concatenate([a(L0_ffn_experts_down), a(L0_ffn_shared_down_w).reshape(D, 2, INTER).transpose(1, 0, 2)])
    ffn_w = np.zeros((NX, P, FW), np.float32)
    for e in range(NX):
        ffn_w[e, :, 0:UP0] = rows(gate[e].T)
        ffn_w[e, :, UP0:DOWN0] = rows(up[e].T)
        padded = np.zeros((len(IC) * P, D), np.float32)
        padded[0:INTER] = down[e].T
        ffn_w[e, :, DOWN0:] = padded.reshape(len(IC), P, D).transpose(1, 0, 2).reshape(P, -1)
    router = np.concatenate([a(L0_ffn_gate_w), a(L0_ffn_shared_expert_gate_w)]).T
    consts = np.concatenate([np.triu(np.ones((P, P)), 1), np.ones((P, P)),
                             np.broadcast_to(np.arange(NT) * P, (P, NT)), np.broadcast_to(np.arange(NTILE), (P, NTILE))],
                            1).astype(np.float32)
    arrays = {
        "x_dram": a(x).reshape(TOK, D), "ctx_dram": a(ctx_1024).reshape(TOK, D),
        "mask_dram": a(mask_1x1xSxS2_ik0).reshape(SEQ, SEQ), "w_in_dram": w_in, "bias_dram": bias, "w_o_dram": w_o,
        "ffn_dram": ffn_w, "router_dram": router, "ident_dram": np.eye(P, dtype=np.float32), "consts_dram": consts,
    }
    arrays = {k: np.ascontiguousarray(v) for k, v in arrays.items()}
    nc = bacc.Bacc("TRN2", target_bir_lowering=False, num_devices=1)
    d = {k: nc.dram_tensor(k, v.shape, mybir.dt.from_np(v.dtype), kind="ExternalInput").ap() for k, v in arrays.items()}
    out = nc.dram_tensor("out_dram", (TOK, D), FP32, kind="ExternalOutput").ap()
    qk_scratch = nc.dram_tensor("qk_scratch", (NB, 2, 2, 2, P, SEQ), FP16, kind="Internal").ap()
    m_scratch = nc.dram_tensor("m_scratch", (NB, H, SEQ), FP16, kind="Internal").ap()
    hrow_dram = nc.dram_tensor("hrow_dram", (TOK, 2 * D), FP16, kind="Internal").ap()
    sw_dram = nc.dram_tensor("sw_dram", (2, 2, P, FW), FP16, kind="Internal").ap()
    hT_dram = nc.dram_tensor("hT_dram", (NB, P, 2 * DC * SEQ), FP16, kind="Internal").ap()
    den_scratch = nc.dram_tensor("den_scratch", (NB, 2, H * SEQ), FP32, kind="Internal").ap()
    sorted_rows = nc.dram_tensor("sorted_rows", (NTILE * P, 2 * D), FP16, kind="Internal").ap()
    sorted_out = nc.dram_tensor("sorted_out", (NTILE * P, D), FP32, kind="Internal").ap()
    block_kernel(nc, d["x_dram"], d["ctx_dram"], d["mask_dram"], d["w_in_dram"], d["bias_dram"], d["w_o_dram"],
                 d["ffn_dram"], d["router_dram"], d["ident_dram"], d["consts_dram"], out, qk_scratch, m_scratch,
                 den_scratch, hrow_dram, hT_dram, sw_dram, sorted_rows, sorted_out)
    r = run_bass_kernel_spmd(nc, [arrays], core_ids=[0])
    return r.results[0]["out_dram"].reshape(NB, SEQ, D)
```
